# Optimizing a Trainium2 kernel written in Bass

```python
import numpy as np
import jax
import jax.numpy as jnp

def _softmax(x, axis=-1):
    return jax.nn.softmax(x, axis=axis)

def _gelu(x):
    return jax.nn.gelu(x, approximate=True)

def _silu(x):
    return jax.nn.silu(x)

def _sigmoid(x):
    return jax.nn.sigmoid(x)

def _layernorm(x, axis=-1, eps=1e-05):
    m = jnp.mean(x, axis=axis, keepdims=True)
    v = jnp.var(x, axis=axis, keepdims=True)
    return (x - m) / jnp.sqrt(v + eps)

def _scatter_add(tgt, idx, src, axis=0):
    return tgt.at[idx].add(src)

def _segment_sum(src, seg, n):
    return jax.ops.segment_sum(src, seg, n)
kernel_name = 'mk_xattn_ffn_d2_seqx_r4_22cdb8'

def setup_inputs(seed: int=0):
    np.random.seed(seed)
    _w = jnp.asarray

    def _rec_inputs():
        import jax
        import jax.numpy as jnp
        _rk = jax.random.key(seed)
        x = -0.0003929 + 0.9999 * jax.random.normal(jax.random.fold_in(_rk, 1), (16, 128, 512), jnp.float32)
        _lenS = 128 - jax.random.randint(jax.random.fold_in(_rk, 7), (16,), 0, max(1, 128 // 4) + 1, jnp.int32)
        _lenS2 = 128 - jax.random.randint(jax.random.fold_in(_rk, 8), (16,), 0, max(1, 128 // 4) + 1, jnp.int32)
        _ctx_2048P = jax.random.normal(jax.random.fold_in(_rk, 11), (16, 16, 512), jnp.float32)
        _ctx_2048c = jax.random.dirichlet(jax.random.fold_in(_rk, 511), 0.3 * jnp.ones((16,), jnp.float32), (16, 128))
        _ctx_2048t = jnp.einsum('bsk,bkd->bsd', _ctx_2048c, _ctx_2048P)
        _ctx_2048t = _ctx_2048t * jax.lax.rsqrt(jnp.mean(jnp.square(_ctx_2048t)) + 1e-12) * 0.953939
        ctx_2048 = -1.39393e-06 + 0.999914 * (_ctx_2048t + 0.3 * jax.random.normal(jax.random.fold_in(_rk, 611), (16, 128, 512), jnp.float32))
        itok_BxS_0_1023 = jax.random.randint(jax.random.fold_in(_rk, 12), (16, 128), 0, 256, jnp.int32)
        _validS = jnp.arange(128)[None, :] < _lenS[:, None]
        _validS2 = jnp.arange(128)[None, :] < _lenS2[:, None]
        _causal = jnp.tril(jnp.ones((128, 128), dtype=bool))
        mask_BxS2_bk0 = jnp.logical_not(jnp.broadcast_to(_validS2[:, :], (16, 128)))
        return (x, ctx_2048, itok_BxS_0_1023, mask_BxS2_bk0)
    x, ctx_2048, itok_BxS_0_1023, mask_BxS2_bk0 = _rec_inputs()

    def _L0_xattn_setup():
        import jax, jax.numpy as jnp
        import numpy as np
        B, Lq, Lk = (2, 1024, 256)
        Q_DIM, KV_DIM = (512, 512)
        H, HD = (16, 128)
        KVC, QC, R = (128, 192, 64)
        LOOKBACK = 8
        NEG = -1e+30

        def _rope(x, L):
            half = x.shape[-1] // 2
            inv_freq = 1.0 / 10000.0 ** (jnp.arange(half, dtype=jnp.float32) / half)
            ang = jnp.arange(L, dtype=jnp.float32)[:, None] * inv_freq
            cos, sin = (jnp.cos(ang), jnp.sin(ang))
            x1, x2 = (x[..., :half], x[..., half:])
            return jnp.concatenate([x1 * cos - x2 * sin, x1 * sin + x2 * cos], axis=-1)
        key = jax.random.key(seed)
        ks = jax.random.split(key, 11)

        def w(k, shape, fan_in):
            return jax.random.normal(k, shape, jnp.float32) / np.sqrt(fan_in).astype(np.float32)
        return {'q': jax.random.normal(ks[0], (B, Lq, Q_DIM), jnp.float32), 'kv': jax.random.normal(ks[1], (B, Lk, KV_DIM), jnp.float32), 'seg_id': jnp.sort(jax.random.randint(ks[2], (B, Lq), 0, Lk), axis=-1), 'W_kvc': w(ks[3], (KV_DIM, KVC), KV_DIM), 'W_dq': w(ks[4], (Q_DIM, QC), Q_DIM), 'W_uq': w(ks[5], (QC, H * HD), QC), 'W_qr': w(ks[6], (QC, H * R), QC), 'W_uk': w(ks[7], (KVC, H * HD), KVC), 'W_kr': w(ks[8], (KVC, R), KVC), 'W_uv': w(ks[9], (KVC, H * HD), KVC), 'W_o': w(ks[10], (H * HD, Q_DIM), H * HD)}
    _L0_xattn_all = _L0_xattn_setup()
    _L0_xattn_in = {k: v for k, v in _L0_xattn_all.items() if k in ('W_kvc', 'W_dq', 'W_uq', 'W_qr', 'W_uk', 'W_kr', 'W_uv', 'W_o')}
    del _L0_xattn_all

    def _L0_ffn_setup():
        import jax, jax.numpy as jnp
        import numpy as np
        B, S, D = (2, 512, 512)
        MOE_D = 352
        E = 16
        K = 6
        ALPHA = 0.001

        def _moe_forward(x, gate_w, w_gate, w_up, w_down):
            b, s, d = x.shape
            T = b * s
            h = x.reshape(T, d)
            logits = h @ gate_w.T
            scores = jax.nn.softmax(logits.astype(jnp.float32), axis=-1)
            topk_w, topk_idx = jax.lax.top_k(scores, K)
            cw = jnp.zeros((T, E), jnp.float32)
            cw = cw.at[jnp.arange(T)[:, None], topk_idx].add(topk_w)
            y = jnp.zeros((T, d), x.dtype)
            for e in range(E):
                g = h @ w_gate[e].T
                u = h @ w_up[e].T
                out = jax.nn.silu(g) * u @ w_down[e].T
                y = y + cw[:, e:e + 1].astype(x.dtype) * out
            counts = jnp.sum(jax.nn.one_hot(topk_idx.reshape(b, s * K), E, dtype=jnp.float32), axis=1)
            ce = counts * (E / (s * K))
            scores_bse = scores.reshape(b, s, E)
            aux = jnp.mean(jnp.sum(ce * scores_bse.mean(axis=1), axis=1)) * ALPHA
            return (y.reshape(b, s, d), aux)
        key = jax.random.key(seed)
        ks = jax.random.split(key, 5)
        sd = 1.0 / np.sqrt(D)
        sm = 1.0 / np.sqrt(MOE_D)
        return {'x': jax.random.normal(ks[0], (B, S, D), jnp.float32), 'gate_w': jax.random.normal(ks[1], (E, D), jnp.float32) * sd, 'w_gate': jax.random.normal(ks[2], (E, MOE_D, D), jnp.float32) * sd, 'w_up': jax.random.normal(ks[3], (E, MOE_D, D), jnp.float32) * sd, 'w_down': jax.random.normal(ks[4], (E, D, MOE_D), jnp.float32) * sm}
    _L0_ffn_all = _L0_ffn_setup()
    _L0_ffn_in = {k: v for k, v in _L0_ffn_all.items() if k in ('gate_w', 'w_gate', 'w_up', 'w_down')}
    del _L0_ffn_all

    def _L1_xattn_setup():
        import jax, jax.numpy as jnp
        import numpy as np
        key = jax.random.key(seed)
        k1, k2, k3 = jax.random.split(key, 3)
        B, S, D, M = (8, 512, 512, 128)
        hidden_states = jax.random.normal(k1, (B, S, D), dtype=jnp.float32)
        memory_tokens = jax.random.normal(k2, (B, M, D), dtype=jnp.float32)
        memory_mask = jax.random.randint(k3, (B, M), 0, 2).astype(jnp.bool_)
        return {'hidden_states': hidden_states, 'memory_tokens': memory_tokens, 'memory_mask': memory_mask}
    _L1_xattn_all = _L1_xattn_setup()
    _L1_xattn_in = {k: v for k, v in _L1_xattn_all.items() if k in ()}
    del _L1_xattn_all

    def _L1_ffn_setup():
        import jax, jax.numpy as jnp
        import numpy as np
        HIDDEN = 512
        INTER = 2048
        RETRIEVAL = 128
        NUM_EXPERTS = 1024
        NUM_KEYS = 64
        TOP_K = 8
        B, S = (4, 512)
        key = jax.random.key(seed)
        ks = jax.random.split(key, 8)
        sc = 0.02
        return {'hidden_states': jax.random.normal(ks[0], (B, S, HIDDEN), jnp.float32), 'W_q': jax.random.normal(ks[1], (HIDDEN, RETRIEVAL), jnp.float32) * sc, 'keys': jax.random.normal(ks[2], (2, RETRIEVAL // 2, NUM_KEYS), jnp.float32) * sc, 'down_embed': jax.random.normal(ks[3], (NUM_EXPERTS, HIDDEN), jnp.float32) * sc, 'up_embed': jax.random.normal(ks[4], (NUM_EXPERTS, HIDDEN), jnp.float32) * sc, 'gate_w': jax.random.normal(ks[5], (HIDDEN, INTER), jnp.float32) * sc, 'up_w': jax.random.normal(ks[6], (HIDDEN, INTER), jnp.float32) * sc, 'down_w': jax.random.normal(ks[7], (INTER, HIDDEN), jnp.float32) * sc}
    _L1_ffn_all = _L1_ffn_setup()
    _L1_ffn_in = {k: v for k, v in _L1_ffn_all.items() if k in ('W_q', 'keys', 'down_embed', 'up_embed', 'gate_w', 'up_w', 'down_w')}
    del _L1_ffn_all
    return {'x': x, 'ctx_2048': ctx_2048, 'itok_BxS_0_1023': itok_BxS_0_1023, 'mask_BxS2_bk0': mask_BxS2_bk0, 'L0_xattn_W_kvc': _L0_xattn_in['W_kvc'], 'L0_xattn_W_dq': _L0_xattn_in['W_dq'], 'L0_xattn_W_uq': _L0_xattn_in['W_uq'], 'L0_xattn_W_qr': _L0_xattn_in['W_qr'], 'L0_xattn_W_uk': _L0_xattn_in['W_uk'], 'L0_xattn_W_kr': _L0_xattn_in['W_kr'], 'L0_xattn_W_uv': _L0_xattn_in['W_uv'], 'L0_xattn_W_o': _L0_xattn_in['W_o'], 'L0_ffn_gate_w': _L0_ffn_in['gate_w'], 'L0_ffn_w_gate': _L0_ffn_in['w_gate'], 'L0_ffn_w_up': _L0_ffn_in['w_up'], 'L0_ffn_w_down': _L0_ffn_in['w_down'], 'L1_ffn_W_q': _L1_ffn_in['W_q'], 'L1_ffn_keys': _L1_ffn_in['keys'], 'L1_ffn_down_embed': _L1_ffn_in['down_embed'], 'L1_ffn_up_embed': _L1_ffn_in['up_embed'], 'L1_ffn_gate_w': _L1_ffn_in['gate_w'], 'L1_ffn_up_w': _L1_ffn_in['up_w'], 'L1_ffn_down_w': _L1_ffn_in['down_w']}

def reference(x, ctx_2048, itok_BxS_0_1023, mask_BxS2_bk0, L0_xattn_W_kvc, L0_xattn_W_dq, L0_xattn_W_uq, L0_xattn_W_qr, L0_xattn_W_uk, L0_xattn_W_kr, L0_xattn_W_uv, L0_xattn_W_o, L0_ffn_gate_w, L0_ffn_w_gate, L0_ffn_w_up, L0_ffn_w_down, L1_ffn_W_q, L1_ffn_keys, L1_ffn_down_embed, L1_ffn_up_embed, L1_ffn_gate_w, L1_ffn_up_w, L1_ffn_down_w):
    import jax
    import jax.numpy as jnp

    def _L0_xattn_ref(q, kv, seg_id, W_kvc, W_dq, W_uq, W_qr, W_uk, W_kr, W_uv, W_o):
        import jax, jax.numpy as jnp
        import numpy as np
        B, Lq, Lk = (2, 1024, 256)
        Q_DIM, KV_DIM = (512, 512)
        H, HD = (16, 128)
        KVC, QC, R = (128, 192, 64)
        LOOKBACK = 8
        NEG = -1e+30

        def _rope(x, L):
            half = x.shape[-1] // 2
            inv_freq = 1.0 / 10000.0 ** (jnp.arange(half, dtype=jnp.float32) / half)
            ang = jnp.arange(L, dtype=jnp.float32)[:, None] * inv_freq
            cos, sin = (jnp.cos(ang), jnp.sin(ang))
            x1, x2 = (x[..., :half], x[..., half:])
            return jnp.concatenate([x1 * cos - x2 * sin, x1 * sin + x2 * cos], axis=-1)
        b, lq, _ = q.shape
        lk = kv.shape[1]
        kv_c = kv @ W_kvc
        q_c = q @ W_dq
        q_nope = (q_c @ W_uq).reshape(b, lq, H, HD).transpose(0, 2, 1, 3)
        q_rope = (q_c @ W_qr).reshape(b, lq, H, R).transpose(0, 2, 1, 3)
        k_nope = (kv_c @ W_uk).reshape(b, lk, H, HD)
        v = (kv_c @ W_uv).reshape(b, lk, H, HD)
        k_rope = kv_c @ W_kr
        q_rope = _rope(q_rope, lq)
        k_rope = _rope(k_rope, lk)
        scale = 1.0 / np.sqrt(HD + R).astype(np.float32)
        scores = (jnp.einsum('bhqd,bkhd->bhqk', q_nope, k_nope) + jnp.einsum('bhqr,bkr->bhqk', q_rope, k_rope)) * scale
        k_ids = jnp.arange(lk)[None, None, :]
        qs = seg_id[:, :, None]
        good = (k_ids <= qs) & (k_ids >= qs - LOOKBACK)
        scores = jnp.where(good[:, None, :, :], scores, NEG)
        attn = jax.nn.softmax(scores, axis=-1)
        out = jnp.einsum('bhqk,bkhd->bqhd', attn, v).reshape(b, lq, H * HD)
        return out @ W_o

    def _L0_ffn_ref(x, gate_w, w_gate, w_up, w_down):
        import jax, jax.numpy as jnp
        import numpy as np
        B, S, D = (2, 512, 512)
        MOE_D = 352
        E = 16
        K = 6
        ALPHA = 0.001

        def _moe_forward(x, gate_w, w_gate, w_up, w_down):
            b, s, d = x.shape
            T = b * s
            h = x.reshape(T, d)
            logits = h @ gate_w.T
            scores = jax.nn.softmax(logits.astype(jnp.float32), axis=-1)
            topk_w, topk_idx = jax.lax.top_k(scores, K)
            cw = jnp.zeros((T, E), jnp.float32)
            cw = cw.at[jnp.arange(T)[:, None], topk_idx].add(topk_w)
            y = jnp.zeros((T, d), x.dtype)
            for e in range(E):
                g = h @ w_gate[e].T
                u = h @ w_up[e].T
                out = jax.nn.silu(g) * u @ w_down[e].T
                y = y + cw[:, e:e + 1].astype(x.dtype) * out
            counts = jnp.sum(jax.nn.one_hot(topk_idx.reshape(b, s * K), E, dtype=jnp.float32), axis=1)
            ce = counts * (E / (s * K))
            scores_bse = scores.reshape(b, s, E)
            aux = jnp.mean(jnp.sum(ce * scores_bse.mean(axis=1), axis=1)) * ALPHA
            return (y.reshape(b, s, d), aux)
        y, _aux = _moe_forward(x, gate_w, w_gate, w_up, w_down)
        return y

    def _L1_xattn_ref(hidden_states, memory_tokens, memory_mask):
        import jax, jax.numpy as jnp
        import numpy as np
        B, S, D = hidden_states.shape
        scale = 1.0 / jnp.sqrt(jnp.asarray(D, hidden_states.dtype))
        scores = jnp.einsum('bsd,bmd->bsm', hidden_states, memory_tokens) * scale
        neg_inf = jnp.asarray(-1e+30, scores.dtype)
        scores = jnp.where(memory_mask[:, None, :], scores, neg_inf)
        attn = jax.nn.softmax(scores, axis=-1)
        readout = jnp.einsum('bsm,bmd->bsd', attn, memory_tokens)
        valid_b = jnp.any(memory_mask, axis=-1)
        out = jnp.where(valid_b[:, None, None], readout, jnp.zeros_like(readout))
        return out

    def _L1_ffn_ref(hidden_states, W_q, keys, down_embed, up_embed, gate_w, up_w, down_w):
        import jax, jax.numpy as jnp
        import numpy as np
        HIDDEN = 512
        INTER = 2048
        RETRIEVAL = 128
        NUM_EXPERTS = 1024
        NUM_KEYS = 64
        TOP_K = 8
        B, S = (4, 512)
        b, s, h = hidden_states.shape
        n = b * s
        queries = (hidden_states @ W_q).reshape(2, n, RETRIEVAL // 2)
        routing = jnp.einsum('tnd,tdk->tnk', queries, keys)
        scores2, idx2 = jax.lax.top_k(routing, TOP_K)
        sx, sy = (scores2[0], scores2[1])
        ix, iy = (idx2[0], idx2[1])
        all_scores = (sx[:, :, None] + sy[:, None, :]).reshape(n, TOP_K * TOP_K)
        all_idx = (ix[:, :, None] * NUM_KEYS + iy[:, None, :]).reshape(n, TOP_K * TOP_K)
        scores, pk = jax.lax.top_k(all_scores, TOP_K)
        indices = jnp.take_along_axis(all_idx, pk, axis=-1)
        de = down_embed[indices]
        ue = up_embed[indices]
        x = hidden_states.reshape(n, h)
        ew = jnp.einsum('nh,nkh->nk', x, de)
        ew = jax.nn.silu(ew) * jax.nn.softmax(scores, axis=-1)
        experts_states = jnp.einsum('nk,nkh->nh', ew, ue).reshape(b, s, h)
        mlp = jax.nn.silu(x @ gate_w) * (x @ up_w) @ down_w
        return mlp.reshape(b, s, h) + experts_states
    x = x + _L0_xattn_ref(_layernorm(x, axis=-1), ctx_2048, itok_BxS_0_1023, L0_xattn_W_kvc, L0_xattn_W_dq, L0_xattn_W_uq, L0_xattn_W_qr, L0_xattn_W_uk, L0_xattn_W_kr, L0_xattn_W_uv, L0_xattn_W_o)
    x = x + _L0_ffn_ref(_layernorm(x, axis=-1), L0_ffn_gate_w, L0_ffn_w_gate, L0_ffn_w_up, L0_ffn_w_down)
    x = x + _L1_xattn_ref(_layernorm(x, axis=-1), ctx_2048, mask_BxS2_bk0)
    x = x + _L1_ffn_ref(_layernorm(x, axis=-1), L1_ffn_W_q, L1_ffn_keys, L1_ffn_down_embed, L1_ffn_up_embed, L1_ffn_gate_w, L1_ffn_up_w, L1_ffn_down_w)
    return x

_drawn_inputs = setup_inputs


def setup_inputs(seed=0):
    import zlib

    import numpy as np

    out = dict(_drawn_inputs(seed))
    spreads = {}
    factors = {'L1_ffn_W_q': 8.0, 'L1_ffn_keys': 8.0, 'L1_ffn_down_embed': 8.0, 'L1_ffn_up_embed': 8.0}
    for name, (base, spread) in spreads.items():
        noise = np.random.default_rng([zlib.crc32(name.encode()), seed]).standard_normal(out[name].shape)
        drawn = base * np.exp(spread * noise) if base else spread * noise
        out[name] = jnp.asarray(drawn.astype(out[name].dtype))
    for name, factor in factors.items():
        out[name] = (out[name] * factor).astype(out[name].dtype)
    return out
```

```python
from contextlib import ExitStack

import numpy as np

import concourse.bass as bass
import concourse.mybir as mybir

F32, F16, BF16 = mybir.dt.float32, mybir.dt.float16, mybir.dt.bfloat16
I32, U32, U8 = mybir.dt.int32, mybir.dt.uint32, mybir.dt.uint8
ALU = mybir.AluOpType
ACT = mybir.ActivationFunctionType
AX = mybir.AxisListType
ds = bass.ds

P = 128
B, S, D = 16, 128, 512
T = B * S
NT = T // P
DC = D // P
BLK = 512
NB = T // BLK
TPB = BLK // P
H, HD, KVC, QC, R = 16, 128, 128, 192, 64
LOOKBACK = 8
NEG = -1e30
E, TOPE, MOE_D = 16, 6, 352
INTER, NEXP, NK, TOPK = 2048, 1024, 64, 8
KX = NEXP // NK
EPS = 1e-5
WS = 64.0
OS = 8.0
GS = 16.0
PS = 64.0
A_SCALE = 1.0 / float(np.sqrt(np.float32(HD + R)))
M_SCALE = 1.0 / float(np.sqrt(np.float32(D)))
GC = 2
GW = GC * P


def size_of(dt):
    return {F32: 4, I32: 4, U32: 4, F16: 2, BF16: 2, U8: 1}[dt]


def build(nc, ins, out):
    with ExitStack() as ctx:
        def sb(name, shape, dt=F32):
            return ctx.enter_context(nc.sbuf_tensor(name, shape, dt))

        def sem(name):
            return ctx.enter_context(nc.semaphore(name))

        def carve(arena, at, dims, dt=F32):
            n = int(np.prod(dims)) * size_of(dt) // 4
            v = arena[:, at:at + n]
            if dt != F32:
                v = v.bitcast(dt)
            if len(dims) == 2:
                v = v.rearrange("p (a b) -> p a b", a=dims[0])
            elif len(dims) == 3:
                v = v.rearrange("p (a b c) -> p a b c", a=dims[0], b=dims[1])
            return v, at + n

        class Room:
            def __init__(self, arena, words):
                self.arena, self.words, self.at = arena, words, 0

            def take(self, *dims, dt=F32):
                v, self.at = carve(self.arena, self.at, dims, dt)
                assert self.at <= self.words, (self.at, self.words)
                return v

        x = sb("x", [P, NT, D])
        XT_W, WORK_W = 8192, 36400
        xt_arena = sb("xt_arena", [P, XT_W])
        work_arena = sb("work_arena", [P, WORK_W])
        id32 = sb("id32", [P, P])
        id16 = sb("id16", [P, P], F16)
        idbf = sb("idbf", [P, P], BF16)
        bank = [ctx.enter_context(nc.psum_tensor(f"bank{i}", [P, 512], F32)) for i in range(8)]

        xt_room = Room(xt_arena, XT_W)
        xt_hi = xt_room.take(DC, T, dt=F16)
        xt_lo = xt_room.take(DC, T, dt=F16)
        q_room = Room(xt_arena, XT_W)
        qp_hi = q_room.take(H, BLK, dt=F16)
        qp_lo = q_room.take(H, BLK, dt=F16)

        phase_done = sem("phase_done")
        phase = {}

        def end_phase(eng, name):
            n = phase.get(name, 0) + 1
            phase[name] = n
            eng.drain().then_inc(phase_done, 1)
            eng.wait_ge(phase_done, 5 * n)

        LS = 4
        ln_st = sb("ln_st", [P, LS, 6])
        ln_mv = sb("ln_mv", [P, LS, 2])
        ln_ve = sb("ln_ve", [P, LS, 1])
        ln_rs = sb("ln_rs", [P, LS, 1])
        neg_half = sb("neg_half", [P, LS, 1])
        ln_var, ln_rstd, half_set = sem("ln_var"), sem("ln_rstd"), sem("half_set")

        ln_stat, ln_norm, ln_turned, ln_hi, ln_lo = (
            [sem(f"ln_{what}{s}") for s in range(LS)] for what in ("stat", "norm", "turned", "hi", "lo"))
        LN_IT = NT // LS

        def tile_cols(t, j, s):
            return t[:, :, ds((j * LS + s) * P, P)]

        def ln_vector(dve, n, xn):
            for j in range(LN_IT):
                done = j + n * LN_IT
                for s in range(LS):
                    dve.bn_stats(ln_st[:, s, :], x[:, ds(j * LS + s, 1), :]).then_inc(ln_stat[s], 1)
                for s in range(LS):
                    dve.wait_ge(ln_stat[s], done * 2 + 1)
                    dve.bn_aggr(ln_mv[:, s, :], ln_st[:, s, :]).then_inc(ln_stat[s], 1)
                for s in range(LS):
                    dve.wait_ge(ln_stat[s], done * 2 + 2)
                dve.tensor_scalar(ln_ve[:, :, :], ln_mv[:, :, 1:2], EPS, None, ALU.add).then_inc(ln_var, 1)
                dve.wait_ge(ln_rstd, done + 1)
                for s in range(LS):
                    dve.wait_ge(ln_turned[s], done)
                    dve.tensor_scalar(xn[:, s, :], x[:, ds(j * LS + s, 1), :].rearrange("p a b -> p (a b)"),
                                      ln_mv[:, s, 0:1], ln_rs[:, s, :], ALU.subtract,
                                      ALU.mult).then_inc(ln_norm[s], 1)
                for s in range(LS):
                    dve.wait_ge(ln_hi[s], done + 1)
                    dve.tensor_tensor(tile_cols(xt_lo, j, s),
                                      bank[s][:, :].rearrange("p (a b) -> p a b", a=DC),
                                      tile_cols(xt_hi, j, s), ALU.subtract).then_inc(ln_lo[s], 1)

        def ln_gpsimd(pool, n):
            with pool.Fori(0, LN_IT) as j:
                done = j + n * LN_IT
                pool.wait_ge(ln_var, done + 1)
                pool.tensor_tensor(ln_rs[:, :, :], ln_ve[:, :, :], neg_half[:, :, :], ALU.pow).then_inc(ln_rstd, 1)

        def ln_tensor(pe, n, xn):
            with pe.Fori(0, LN_IT) as j:
                done = j + n * LN_IT
                for s in range(LS):
                    pe.wait_ge(ln_norm[s], done + 1)
                    pe.wait_ge(ln_lo[s], ONE + done)
                    for c in range(DC):
                        m = pe.transpose(bank[s][:, c * P:(c + 1) * P], xn[:, s, c * P:(c + 1) * P], id32[:, :])
                    m.then_inc(ln_turned[s], 1)

        def ln_scalar(act, n):
            for j in range(LN_IT):
                done = j + n * LN_IT
                for s in range(LS):
                    act.wait_ge(ln_turned[s], done + 1)
                    act.activation(tile_cols(xt_hi, j, s),
                                   bank[s][:, :].rearrange("p (a b) -> p a b", a=DC),
                                   ACT.Copy).then_inc(ln_hi[s], 1)

        def mm3(pe, o, a_hi, a_lo, b_hi, b_lo, start, stop):
            pe.matmul(o, a_hi, b_hi, start=start, stop=False)
            pe.matmul(o, a_hi, b_lo, start=False, stop=False)
            return pe.matmul(o, a_lo, b_hi, start=False, stop=stop)

        wr = Room(work_arena, WORK_W)
        att_a_hi = wr.take(H, 2 * P, dt=F16)
        att_a_lo = wr.take(H, 2 * P, dt=F16)
        att_vo_hi = wr.take(H, D, dt=F16)
        att_vo_lo = wr.take(H, D, dt=F16)
        SW = DC * 256 + DC * 128 + 256 + 2048
        sw_hi = wr.take(SW, dt=F16)
        sw_lo = wr.take(SW, dt=F16)
        qc0_hi = wr.take(T, dt=F16)
        qc0_lo = wr.take(T, dt=F16)
        qc1 = wr.take(T, dt=F16)
        kv_hi = wr.take(T, dt=F16)
        kv_lo = wr.take(T, dt=F16)
        kvt_hi = wr.take(B, KVC, dt=F16)
        kvt_lo = wr.take(B, KVC, dt=F16)
        kr_hi = wr.take(T, dt=F16)
        kr_lo = wr.take(T, dt=F16)
        seg_bias = wr.take(B, S, dt=BF16)
        seg_scale = wr.take(B)
        cos_q = wr.take(R)
        sin_q = wr.take(R)
        cos_k = wr.take(S)
        sin_k = wr.take(S)
        att_end = wr.at

        def swv(t, at, *dims):
            n = int(np.prod(dims))
            v = t[:, at:at + n]
            return v.rearrange("p (a b) -> p a b", a=dims[0]) if len(dims) == 2 else v
        o_kvc, o_kr, o_qr = DC * 256, DC * 384, DC * 384 + 256
        wdq = [swv(t, 0, DC, 256) for t in (sw_hi, sw_lo)]
        wkvc = [swv(t, o_kvc, DC, 128) for t in (sw_hi, sw_lo)]
        wkr = [swv(t, o_kr, 2, 128) for t in (sw_hi, sw_lo)]
        wqr = [swv(t, o_qr, 2, 1024) for t in (sw_hi, sw_lo)]

        HW = 256 + 128 + 128 + 512
        pr = Room(work_arena, WORK_W)
        pr.at = att_end
        hw32 = pr.take(2, HW)
        hw_hi = pr.take(2, HW, dt=F16)
        hw_lo = pr.take(2, HW, dt=F16)
        ln_xn_prep = pr.take(LS, D)
        sw32 = xt_arena[:, 0:SW]
        prep_load = [sem(f"prep_load{s}") for s in range(2)]
        prep_hi = [sem(f"prep_hi{s}") for s in range(2)]
        prep_lo = [sem(f"prep_lo{s}") for s in range(2)]
        prep_mm = [sem(f"prep_mm{s}") for s in range(2)]
        prep_ahi = [sem(f"prep_ahi{s}") for s in range(2)]
        prep_alo = [sem(f"prep_alo{s}") for s in range(2)]
        consts_in, small_in, small_hi = (sem(n) for n in ("consts_in", "small_in", "small_hi"))
        x_in = sem("x_in")

        jr = Room(work_arena, WORK_W)
        jr.at = att_end
        ctx32 = jr.take(DC, BLK)
        ctx_hi = jr.take(DC, BLK, dt=F16)
        ctx_lo = jr.take(DC, BLK, dt=F16)
        kt1 = jr.take(BLK)
        kt2 = jr.take(BLK)
        krot = jr.take(BLK)
        segi = jr.take(B, dt=I32)
        segf = jr.take(B)
        iota = jr.take(S)
        dist = kt1
        gt1 = jr.take(S)
        gt2 = jr.take(S)
        v1 = jr.take(B)
        v2 = jr.take(B)
        ctx_load, ctx_h, ctx_l = sem("ctx_load"), sem("ctx_h"), sem("ctx_l")
        qkv_mm, qkv_h, qkv_l = sem("qkv_mm"), sem("qkv_h"), sem("qkv_l")
        kr_mm, kr_mul, kr_sum, kr_h = (sem(n) for n in ("kr_mm", "kr_mul", "kr_sum", "kr_h"))
        kvt_mm, kvt_cp = sem("kvt_mm"), sem("kvt_cp")
        seg_in, seg_step = sem("seg_in"), sem("seg_step")

        ar = Room(work_arena, WORK_W)
        ar.at = att_end
        rt1 = ar.take(H, R)
        rt2 = ar.take(H, R)
        rot = rt1
        rhl = ar.take(H, 2, R, dt=F16)
        qrt = ar.take(2, H, P, dt=F16)
        prob = ar.take(2, 4, P)
        pt_hi = ar.take(2, 4 * P, dt=F16)
        pt_lo = ar.take(2, 4 * P, dt=F16)
        ot_hi = ar.take(2, 4 * P, dt=F16)
        ot_lo = ar.take(2, 4 * P, dt=F16)
        nmax = ar.take(2, 4)
        ebias = ar.take(2, 4)
        escale = ar.take(2, 1)
        esum = ar.take(2, 4)
        rinv = ar.take(2, 4)
        q_mm = [sem(f"q_mm{s}") for s in range(2)]
        q_h = [sem(f"q_h{s}") for s in range(2)]
        q_free = [sem(f"q_free{s}") for s in range(2)]
        rope_sum, rope_h, rope_l, rope_tr, rope_cp = (
            sem(n) for n in ("rope_sum", "rope_h", "rope_l", "rope_tr", "rope_cp"))
        score_mm, smax, pth, ptl, oth, otl, yadd = (
            sem(n) for n in ("score_mm", "smax", "pth", "ptl", "oth", "otl", "yadd"))
        exped = [sem(f"exped{s}") for s in range(2)]
        recip = [sem(f"recip{s}") for s in range(2)]
        normed = [sem(f"normed{s}") for s in range(2)]
        pt_mm = [sem(f"pt_mm{s}") for s in range(2)]
        o_mm = [sem(f"o_mm{s}") for s in range(2)]
        y_mm = [sem(f"y_mm{s}") for s in range(2)]
        NG = 4 * 4

        mr = Room(work_arena, WORK_W)
        cwt = mr.take(T, dt=F16)
        ffn_at = mr.at

        ffn_sems = [[sem(f"ffn_{what}{s}") for s in range(2)] for what in (
            "landed", "whi", "wlo", "selc", "up", "silu", "m1d", "m2d", "hhi", "hlo", "ymm", "yadd")]

        class FFN:
            (landed, whi, wlo, selc, up, silu, m1d, m2d, hhi, hlo, ymm, yadd) = ffn_sems


        def make_ffn(groups, pieces, gated, at, before):
            f = FFN()
            f.groups, f.pieces, f.land = groups, pieces, 32 if gated else 16
            f.step0 = before.step0 + before.groups * NB if before else 0
            f.piece0 = before.piece0 + before.groups // 2 * before.pieces if before else 0
            f.land0 = before.land0 + before.groups // 2 * before.land if before else 0
            r = Room(work_arena, WORK_W)
            r.at = at
            f.w32 = r.take(2, pieces * 1024)
            f.w_hi = r.take(2, pieces * 1024, dt=F16)
            f.w_lo = r.take(2, pieces * 1024, dt=F16)
            f.sel32 = r.take(2, GW, dt=F16)
            f.sel = r.take(2, GW, dt=F16)
            f.sg = r.take(2, BLK)
            f.m1 = r.take(2, BLK)
            f.m2 = r.take(2, BLK)
            f.h_hi = r.take(2, GC, BLK, dt=F16)
            f.h_lo = r.take(2, GC, BLK, dt=F16)
            f.end = r.at
            return f

        moe = make_ffn(E * MOE_D // GW, 3, True, ffn_at, None)
        gr = Room(work_arena, WORK_W)
        gr.at = moe.end
        gw32 = gr.take(DC, E)
        gw_hi = gr.take(DC, E, dt=F16)
        gw_lo = gr.take(DC, E, dt=F16)
        gmx = gr.take(NT)
        gsub = gr.take(NT, E)
        gexp = gr.take(NT, E)
        gsum = gr.take(NT)
        grc = gr.take(NT)
        gsc = gr.take(NT, E + 2)
        gtop = gr.take(NT, 8)
        grep_ = gr.take(NT, E + 2)
        gcw = gr.take(NT, E)
        ln_xn_moe = gr.take(LS, D)
        gate_done = sem("gate_done")
        gate_in, gate_s, gate_mm, gate_v, gate_t, gate_c = (
            sem(n) for n in ("gate_in", "gate_s", "gate_mm", "gate_v", "gate_t", "gate_c"))

        cr = Room(work_arena, WORK_W)
        memT_hi = cr.take(DC, T, dt=F16)
        memT_lo = cr.take(DC, T, dt=F16)
        mem_hi = cr.take(B, D, dt=F16)
        mem_lo = cr.take(B, D, dt=F16)
        mem32 = cr.take(2, DC * P)
        mm8 = cr.take(T, dt=U8)
        mm_f = cr.take(B, S)
        mm_bias = cr.take(B, S, dt=BF16)
        mvalid = cr.take(B)
        mscale = cr.take(B)
        mprob = cr.take(2, P)
        mpt_hi = cr.take(2, P, dt=F16)
        mpt_lo = cr.take(2, P, dt=F16)
        mst = cr.take(2, 4)
        mfac = cr.take(2, 1)
        ln_xn_mem = cr.take(LS, D)
        mem_load = [sem(f"mem_load{s}") for s in range(2)]
        mem_h = [sem(f"mem_h{s}") for s in range(2)]
        mem_l = [sem(f"mem_l{s}") for s in range(2)]
        mem_fac = [sem(f"mem_fac{s}") for s in range(2)]
        mask_in, mask_s = sem("mask_in"), sem("mask_s")
        ms_mm = [sem(f"ms_mm{s}") for s in range(2)]
        ms_v = [sem(f"ms_v{s}") for s in range(2)]
        ms_e = [sem(f"ms_e{s}") for s in range(2)]
        mp_t = [sem(f"mp_t{s}") for s in range(2)]
        mp_h = [sem(f"mp_h{s}") for s in range(2)]
        mp_l = [sem(f"mp_l{s}") for s in range(2)]
        mo_mm = [sem(f"mo_mm{s}") for s in range(2)]
        mo_a = [sem(f"mo_a{s}") for s in range(2)]

        kr_ = Room(work_arena, WORK_W)
        gT = kr_.take(NEXP // P, T)
        pk_at = kr_.at
        mlp = make_ffn(INTER // GW, 3, False, pk_at, moe)
        pkm = make_ffn(NEXP // GW, 2, False, pk_at, mlp)
        rr = Room(work_arena, WORK_W)
        rr.at = pk_at
        ln_xn_pk = rr.take(LS, D)
        kw32 = rr.take(DC * P + 2 * P)
        kw_hi = rr.take(DC * P + 2 * P, dt=F16)
        kw_lo = rr.take(DC * P + 2 * P, dt=F16)
        qT_hi = rr.take(T, dt=F16)
        qT_lo = rr.take(T, dt=F16)
        rx = rr.take(16, NK)
        ry = rr.take(16, NK)
        sx = rr.take(16, 8)
        sy = rr.take(16, 8)
        ixu = rr.take(16, 8, dt=U32)
        iyu = rr.take(16, 8, dt=U32)
        ixf = rr.take(16, 8)
        iyf = rr.take(16, 8)
        al = rr.take(16, 64)
        al_rep = rr.take(16, 64)
        top = rr.take(16, 8)
        wsum = rr.take(16, 8)
        cnt = rr.take(16, 8)
        den = rr.take(16)
        ex_ = rr.take(16, KX)
        wtmp = rr.take(16, 8)
        far = rr.take(16)
        iota64 = rr.take(NK)
        rank8 = rr.take(8)
        G = rr.take(KX, NK)
        cc = rr.take(2, KX)
        s64 = rr.take(2, NK)
        eq = rr.take(8, NK)
        eqx = rr.take(KX, 8)
        pk_in, pk_s, pk_qmm, pk_qh, pk_ql, pk_rmm, pk_r, pk_act = (
            sem(n) for n in ("pk_in", "pk_s", "pk_qmm", "pk_qh", "pk_ql", "pk_rmm", "pk_r", "pk_act"))
        pk_v, pk_g, pk_t, pk_c0, pk_c1 = (sem(n) for n in ("pk_v", "pk_g", "pk_t", "pk_c0", "pk_c1"))
        pk_g0, pk_u = sem("pk_chain"), sem("pk_unit")
        stored = sem("stored")

        ONE = 1
        from_one = [prep_lo, prep_alo, FFN.wlo, FFN.selc, FFN.yadd, ln_lo, q_free, exped, pt_mm, o_mm, y_mm,
                    mem_l, ms_e, mp_l, mo_a,
                    [ctx_l, qkv_l, kr_mul, kvt_cp, ptl, otl, yadd, rope_cp, score_mm, rope_tr, rope_h, rope_l,
                     pk_c0, pk_c1, pk_u, pk_t]]

        block = ctx.enter_context(nc.Block())

        @block.sync
        def _(sp):
            sp.dma_start(id32[:, :], ins["ident"]).then_inc(consts_in, 16)
            for dst, src in ((cos_q, "cos_q"), (sin_q, "sin_q"), (cos_k, "cos_k"), (sin_k, "sin_k")):
                sp.dma_start(dst, ins[src]).then_inc(consts_in, 16)
            sp.dma_start(sw32, ins["small_w"]).then_inc(small_in, 16)
            for s in range(LS):
                sp.dma_start(x[:, s * 4:(s + 1) * 4, :], ins["x"][:, s * 4:(s + 1) * 4, :]).then_inc(x_in, 16)
            for several in from_one:
                for semaphore in several:
                    sp.sem_inc(semaphore, ONE)
            for j in range(H // 2):
                for s in range(2):
                    sp.wait_ge(prep_lo[s], ONE + j)
                    sp.dma_start(hw32[:, s, :], ins["head_w"][ds(j * 2 + s, 1), :, :].rearrange(
                        "a p n -> p (a n)")).then_inc(prep_load[s], 16)
            end_phase(sp, "sp")
            sp.dma_start(segi, ins["seg"]).then_inc(seg_in, 16)
            sp.dma_start(iota, ins["iota"]).then_inc(seg_in, 16)
            for j in range(NB):
                sp.wait_ge(ctx_l, ONE + j)
                sp.dma_start(ctx32, ins["ctxT"][:, :, ds(j * BLK, BLK)]).then_inc(ctx_load, 16)
            end_phase(sp, "sp")
            end_phase(sp, "sp")

            def ffn_loads(f, w, sel):
                for j in range(f.groups // 2):
                    for s in range(2):
                        sp.wait_ge(f.wlo[s], ONE + f.piece0 + j * f.pieces)
                        if sel is not None:
                            sp.wait_ge(f.selc[s], ONE + j)
                        sp.dma_start(f.w32[:, s, :], w[ds(j * 2 + s, 1), :, :].rearrange(
                            "a p n -> p (a n)")).then_inc(f.landed[s], 16)
                        if sel is not None:
                            sp.dma_start(f.sel32[:, s, :], sel[ds(j * 2 + s, 1), :, :].rearrange(
                                "a p n -> p (a n)")).then_inc(f.landed[s], 16)

            sp.dma_start(gw32, ins["moe_gate"]).then_inc(gate_in, 16)
            ffn_loads(moe, ins["moe_w"], ins["moe_sel"])
            end_phase(sp, "sp")
            sp.dma_start(mm8, ins["mem_mask"].partition_broadcast(P)).then_inc(mask_in, 16)
            for j in range(B):
                for s in range(2):
                    sp.wait_ge(mem_l[s], ONE + j)
                    src = (ins["ctxT"][:, :, ds(j * P, P)], ins["ctx"][:, ds(j, 1), :])[s]
                    dst = mem32[:, s, :].rearrange("p (a b) -> p a b", a=(DC, 1)[s])
                    sp.dma_start(dst, src).then_inc(mem_load[s], 16)
            end_phase(sp, "sp")
            sp.dma_start(kw32, ins["pk_w"]).then_inc(pk_in, 16)
            sp.dma_start(iota64, ins["iota"][:, 0:NK]).then_inc(pk_in, 16)
            sp.dma_start(rank8, ins["rank8"]).then_inc(pk_in, 16)
            end_phase(sp, "sp")
            ffn_loads(mlp, ins["mlp_w"], None)
            end_phase(sp, "sp")
            ffn_loads(pkm, ins["pk_e"], None)
            end_phase(sp, "sp")
            for s in range(NB):
                sp.dma_start(out[:, s * 4:(s + 1) * 4, :], x[:, s * 4:(s + 1) * 4, :]).then_inc(stored, 16)
            sp.wait_ge(stored, 16 * NB)

        @block.tensor
        def _(pe):
            pe.wait_ge(small_hi, 3)
            with pe.Fori(0, H // 2) as j:
                for s in range(2):
                    hh, hl = hw_hi[:, s, :], hw_lo[:, s, :]
                    pe.wait_ge(prep_lo[s], ONE + j + 1)
                    pe.wait_ge(prep_alo[s], ONE + j)
                    for c in range(2):
                        cs = slice(c * P, (c + 1) * P)
                        mm3(pe, bank[4 + 2 * s][:, cs], hh[:, cs], hl[:, cs], hh[:, 256:384],
                            hl[:, 256:384], start=True, stop=True)
                    mm3(pe, bank[5 + 2 * s][:, :], hh[:, 384:512], hl[:, 384:512], hh[:, 512:1024],
                        hl[:, 512:1024], start=True, stop=True).then_inc(prep_mm[s], 1)
            ln_tensor(pe, 0, ln_xn_prep)
            end_phase(pe, "pe")
            with pe.Fori(0, NB) as j:
                blk = ds(j * BLK, BLK)
                pe.wait_ge(ctx_l, ONE + j + 1)
                pe.wait_ge(qkv_l, ONE + j * 3)
                for c in range(DC):
                    for i in range(2):
                        cs = slice(i * P, (i + 1) * P)
                        mm3(pe, bank[i][:, :], wdq[0][:, c, cs], wdq[1][:, c, cs], xt_hi[:, c, blk],
                            xt_lo[:, c, blk], start=(c == 0), stop=(c == DC - 1))
                    m = mm3(pe, bank[2][:, :], wkvc[0][:, c, :], wkvc[1][:, c, :], ctx_hi[:, c, :],
                            ctx_lo[:, c, :], start=(c == 0), stop=(c == DC - 1))
                m.then_inc(qkv_mm, 1)
                pe.wait_ge(qkv_l, ONE + j * 3 + 1)
                pe.wait_ge(kr_mul, ONE + j * 2)
                for i in range(2):
                    m = mm3(pe, bank[3 + i][:, :], wkr[0][:, i, :], wkr[1][:, i, :], kv_hi[:, blk],
                            kv_lo[:, blk], start=True, stop=True)
                m.then_inc(kr_mm, 1)
                pe.wait_ge(kvt_cp, ONE + j * 2)
                o = bank[5][:, :].bitcast(F16)
                for i, t in enumerate((kv_hi, kv_lo)):
                    for u in range(TPB):
                        m = pe.transpose(o[:, (i * TPB + u) * P:(i * TPB + u + 1) * P],
                                         t[:, ds(j * BLK + u * P, P)], id16[:, :])
                m.then_inc(kvt_mm, 1)
            end_phase(pe, "pe")
            TR = bank[7][:, :].bitcast(F16)

            def rope_pe(j, u):
                tok = ds(j * BLK + u * P, P)
                for a in range(2):
                    pe.wait_ge(q_free[a], ONE + j * 12 + 8 + u)
                    cs = slice(a * 512, (a + 1) * 512)
                    o = bank[5 + a][:, :]
                    pe.matmul(o, qc0_hi[:, tok], wqr[0][:, 0, cs], start=True, stop=False)
                    pe.matmul(o, qc0_hi[:, tok], wqr[1][:, 0, cs], start=False, stop=False)
                    pe.matmul(o, qc0_lo[:, tok], wqr[0][:, 0, cs], start=False, stop=False)
                    pe.matmul(o, qc1[:, tok], wqr[0][:, 1, cs], start=False, stop=False)
                    pe.matmul(o, qc1[:, tok], wqr[1][:, 1, cs], start=False, stop=True).then_inc(q_mm[a], 1)

            def rope_turn(j, u):
                pe.wait_ge(rope_l, ONE + j * 4 + u + 1)
                for a in range(2):
                    pe.wait_ge(rope_cp, ONE + j * 8 + u * 2 + a)
                    for h in range(8):
                        m = pe.transpose(TR[:, h * P:(h + 1) * P],
                                         rhl[:, a * 8 + h, :, :].rearrange("p a b -> p (a b)"), id16[:, :])
                    m.then_inc(rope_tr, 1)

            with pe.Fori(0, NB) as j:
                blk = ds(j * BLK, BLK)
                for h in range(H):
                    o = bank[5 + h % 2][:, :]
                    pe.wait_ge(q_free[h % 2], ONE + j * 12 + h // 2)
                    pe.matmul(o, att_a_hi[:, h, 0:P], qc0_hi[:, blk], start=True, stop=False)
                    pe.matmul(o, att_a_hi[:, h, 0:P], qc0_lo[:, blk], start=False, stop=False)
                    pe.matmul(o, att_a_lo[:, h, 0:P], qc0_hi[:, blk], start=False, stop=False)
                    pe.matmul(o, att_a_hi[:, h, P:2 * P], qc1[:, blk], start=False, stop=False)
                    pe.matmul(o, att_a_lo[:, h, P:2 * P], qc1[:, blk], start=False,
                              stop=True).then_inc(q_mm[h % 2], 1)
                rope_pe(j, 0)
                for n in range(NG + 3):
                    if n < NG:
                        u, g, k = n // 4, n % 4, n % 2
                        if g == 0:
                            rope_turn(j, u)
                            if u < 3:
                                rope_pe(j, u + 1)
                            pe.wait_ge(rope_cp, ONE + j * 8 + u * 2 + 2)
                        pe.wait_ge(q_free[0], ONE + j * 12 + 2 * g + 2)
                        pe.wait_ge(q_free[1], ONE + j * 12 + 2 * g + 2)
                        pe.wait_ge(exped[k], ONE + j * 8 + n // 2)
                        sc = bank[k]
                        keys = ds(j * BLK + u * P, P)
                        pe.matmul(sc[:, :].rearrange("p (a b) -> p a b", a=4), idbf[:, :],
                                  seg_bias[:, ds(j * 4 + u, 1), :].to_broadcast([P, 4, S]),
                                  start=True, stop=False)
                        for i in range(4):
                            h = 4 * g + i
                            o = sc[:, i * P:(i + 1) * P]
                            qs = slice(u * P, (u + 1) * P)
                            pe.matmul(o, qp_hi[:, h, qs], kv_hi[:, keys], start=False, stop=False)
                            pe.matmul(o, qp_hi[:, h, qs], kv_lo[:, keys], start=False, stop=False)
                            pe.matmul(o, qp_lo[:, h, qs], kv_hi[:, keys], start=False, stop=False)
                            pe.matmul(o, qrt[:, u % 2, h, :], kr_hi[:, keys], start=False, stop=False)
                            m = pe.matmul(o, qrt[:, u % 2, h, :], kr_lo[:, keys], start=False,
                                          stop=(i == 3))
                        m.then_inc(score_mm, 1)
                    if 1 <= n <= NG:
                        q, k = n - 1, (n - 1) % 2
                        pe.wait_ge(normed[k], j * 8 + q // 2 + 1)
                        pe.wait_ge(ptl, ONE + j * NG + q)
                        for i in range(4):
                            m = pe.transpose(bank[2][:, i * P:(i + 1) * P], prob[:, k, i, :], id32[:, :])
                        m.then_inc(pt_mm[k], 1)
                    if 2 <= n <= NG + 1:
                        q, k = n - 2, (n - 2) % 2
                        u = q // 4
                        pe.wait_ge(ptl, ONE + j * NG + q + 1)
                        pe.wait_ge(otl, ONE + j * NG + q)
                        kh, kl = (t[:, ds(j * 4 + u, 1), :].rearrange("p a b -> p (a b)")
                                  for t in (kvt_hi, kvt_lo))
                        mm3(pe, bank[3][:, :], kh, kl, pt_hi[:, k, :], pt_lo[:, k, :],
                            start=True, stop=True).then_inc(o_mm[k], 1)
                    if n >= 3:
                        q, k = n - 3, (n - 3) % 2
                        u, g = q // 4, q % 4
                        pe.wait_ge(otl, ONE + j * NG + q + 1)
                        if g == 0:
                            pe.wait_ge(yadd, ONE + j * 4 + u)
                        for i in range(4):
                            h = 4 * g + i
                            m = mm3(pe, bank[4][:, :], ot_hi[:, k, i * P:(i + 1) * P],
                                    ot_lo[:, k, i * P:(i + 1) * P], att_vo_hi[:, h, :], att_vo_lo[:, h, :],
                                    start=(h == 0), stop=(h == H - 1))
                        m.then_inc(y_mm[k], 1)
            end_phase(pe, "pe")
            ln_tensor(pe, 1, ln_xn_moe)
            pe.wait_ge(gate_s, 2)
            for s in range(LS):
                pe.wait_ge(ln_lo[s], ONE + 2 * LN_IT)
            for t in range(NT):
                for c in range(DC):
                    ts_ = slice(t * P, (t + 1) * P)
                    m = mm3(pe, bank[4][:, t * E:(t + 1) * E], xt_hi[:, c, ts_], xt_lo[:, c, ts_],
                            gw_hi[:, c, :], gw_lo[:, c, :], start=(c == 0), stop=(c == DC - 1))
            m.then_inc(gate_mm, 1)
            pe.wait_ge(gate_done, 1)
            for t in range(NB):
                pe.wait_ge(gate_c, 2 * t)
                for i in range(TPB):
                    m = pe.transpose(bank[5][0:E, i * P:(i + 1) * P], gcw[:, t * TPB + i, :], id32[:, :])
                m.then_inc(gate_t, 1)
            pe.wait_ge(gate_c, 2 * NB)

            def ffn_tensor(f, gated):
                def A(j, s):
                    gs, t = (s // NB) % 2, s % NB
                    if t == 0:
                        it = j + 1 if s == 2 * NB else j
                        pe.wait_ge(f.wlo[gs], ONE + f.piece0 + it * f.pieces + f.pieces - 1)
                        if gated:
                            pe.wait_ge(f.selc[gs], ONE + it + 1)
                    k = f.step0 + j * (2 * NB) + s
                    wh, wl = f.w_hi[:, gs, :], f.w_lo[:, gs, :]
                    toks = slice(t * BLK, (t + 1) * BLK)
                    for c in range(GC):
                        pe.wait_ge(f.m2d[c], k)
                        for i in range(f.pieces - 1):
                            for d in range(DC):
                                ws = slice(i * 1024 + d * GW + c * P, i * 1024 + d * GW + (c + 1) * P)
                                m = mm3(pe, bank[2 * i + c][:, :], wh[:, ws], wl[:, ws], xt_hi[:, d, toks],
                                        xt_lo[:, d, toks], start=(d == 0), stop=(d == DC - 1))
                        if gated:
                            m = pe.matmul(bank[4 + c][:, :], f.sel[:, gs, c * P:(c + 1) * P], cwt[:, toks],
                                          start=True, stop=True)
                        m.then_inc(f.up[c], 1)

                def Dn(j, s):
                    gs, t, hp = s // NB, s % NB, s % 2
                    k = f.step0 + j * (2 * NB) + s
                    if t == 0:
                        pe.wait_ge(f.wlo[gs], ONE + f.piece0 + j * f.pieces + f.pieces)
                    for c in range(GC):
                        pe.wait_ge(f.hlo[c], k + 1)
                    wh, wl = f.w_hi[:, gs, :], f.w_lo[:, gs, :]
                    o0 = (f.pieces - 1) * 1024
                    for q in range(TPB):
                        yb = q % 2
                        pe.wait_ge(f.yadd[yb], ONE + k * 2 + q // 2)
                        for c in range(GC):
                            ws = slice(o0 + c * D, o0 + (c + 1) * D)
                            qs = slice(q * P, (q + 1) * P)
                            m = mm3(pe, bank[6 + yb][:, :], f.h_hi[:, hp, c, qs], f.h_lo[:, hp, c, qs],
                                    wh[:, ws], wl[:, ws], start=(c == 0), stop=(c == GC - 1))
                        m.then_inc(f.ymm[yb], 1)

                def body(j, last):
                    for s in range(2 * NB):
                        if not (last and s == 2 * NB - 1):
                            A(j, s + 1)
                        Dn(j, s)

                A(0, 0)
                n = f.groups // 2
                if n > 1:
                    with pe.Fori(0, n - 1) as j:
                        body(j, False)
                body(n - 1, True)

            ffn_tensor(moe, True)
            end_phase(pe, "pe")
            ln_tensor(pe, 2, ln_xn_mem)
            for s in range(LS):
                pe.wait_ge(ln_lo[s], ONE + 3 * LN_IT)
            pe.wait_ge(mask_s, 4)
            for s in range(2):
                pe.wait_ge(mem_l[s], ONE + B)

            def mem_scores(b, i, s):
                pe.wait_ge(ms_e[s], ONE + i)
                toks = ds(b * P, P)
                pe.matmul(bank[s][:, 0:P], idbf[:, :], mm_bias[:, ds(b, 1), :].rearrange("p a b -> p (a b)"),
                          start=True, stop=False)
                for c in range(DC):
                    m = mm3(pe, bank[s][:, 0:P], xt_hi[:, c, toks], xt_lo[:, c, toks], memT_hi[:, c, toks],
                            memT_lo[:, c, toks], start=False, stop=(c == DC - 1))
                m.then_inc(ms_mm[s], 1)

            with pe.Fori(0, B // 2) as j:
                for s in range(2):
                    mem_scores(j * 2 + s, j, s)
                for s in range(2):
                    pe.wait_ge(ms_e[s], ONE + j + 1)
                    pe.wait_ge(mp_l[s], ONE + j)
                    pe.transpose(bank[2 + s][:, 0:P], mprob[:, s, :], id32[:, :]).then_inc(mp_t[s], 1)
                for s in range(2):
                    pe.wait_ge(mp_l[s], ONE + j + 1)
                    pe.wait_ge(mo_a[s], ONE + j)
                    mh, ml = (t[:, ds(j * 2 + s, 1), :].rearrange("p a b -> p (a b)") for t in (mem_hi, mem_lo))
                    mm3(pe, bank[4 + s][:, :], mpt_hi[:, s, :], mpt_lo[:, s, :], mh, ml,
                        start=True, stop=True).then_inc(mo_mm[s], 1)
            end_phase(pe, "pe")
            ln_tensor(pe, 3, ln_xn_pk)
            pe.wait_ge(pk_s, 2)
            for s in range(LS):
                pe.wait_ge(ln_lo[s], ONE + 4 * LN_IT)
            for t in range(NB):
                toks = slice(t * BLK, (t + 1) * BLK)
                for c in range(DC):
                    ws = slice(c * P, (c + 1) * P)
                    m = mm3(pe, bank[4 + t][:, :], kw_hi[:, ws], kw_lo[:, ws], xt_hi[:, c, toks],
                            xt_lo[:, c, toks], start=(c == 0), stop=(c == DC - 1))
                m.then_inc(pk_qmm, 1)
            pe.wait_ge(pk_ql, NB)
            for t in range(NT):
                ts_, half = slice(t * P, (t + 1) * P), t // 8
                ks = slice(DC * P + half * P, DC * P + (half + 1) * P)
                m = mm3(pe, bank[t // 4][:, (t % 4) * P:(t % 4 + 1) * P], qT_hi[:, ts_], qT_lo[:, ts_],
                        kw_hi[:, ks], kw_lo[:, ks], start=True, stop=True)
            m.then_inc(pk_rmm, 1)
            with pe.Fori(0, NT) as u:
                pe.wait_ge(pk_g, u + 1)
                for a, done in enumerate((pk_c0, pk_c1)):
                    pe.wait_ge(done, ONE + u)
                    for i in range(4):
                        e = a * 4 + i
                        m = pe.transpose(bank[4 + a][:, i * P:(i + 1) * P],
                                         G[:, 2 * e:2 * e + 2, :].rearrange("p a b -> p (a b)"), id32[:, :])
                    m.then_inc(pk_t, 1)
            end_phase(pe, "pe")
            ffn_tensor(mlp, False)
            end_phase(pe, "pe")
            ffn_tensor(pkm, False)
            end_phase(pe, "pe")

        @block.scalar
        def _(act):
            act.wait_ge(consts_in, 80)
            act.activation(id16[:, :], id32[:, :], ACT.Copy).then_inc(small_hi, 1)
            act.activation(idbf[:, :], id32[:, :], ACT.Copy).then_inc(small_hi, 1)
            act.wait_ge(small_in, 16)
            act.activation(sw_hi, sw32, ACT.Copy, scale=WS).then_inc(small_hi, 1)
            for j in range(H // 2):
                for s in range(2):
                    act.wait_ge(prep_load[s], j * 16 + 16)
                    act.wait_ge(prep_mm[s], j)
                    act.activation(hw_hi[:, s, :], hw32[:, s, :], ACT.Copy, scale=WS).then_inc(prep_hi[s], 1)
                for s in range(2):
                    hsl = ds(j * 2 + s, 1)
                    act.wait_ge(prep_mm[s], j + 1)
                    act.activation(att_a_hi[:, hsl, :].rearrange("p a b -> p (a b)"),
                                   bank[4 + 2 * s][:, 0:256], ACT.Copy, scale=1 / WS)
                    act.activation(att_vo_hi[:, hsl, :].rearrange("p a b -> p (a b)"),
                                   bank[5 + 2 * s][:, :], ACT.Copy, scale=1 / WS).then_inc(prep_ahi[s], 1)
            ln_scalar(act, 0)
            end_phase(act, "act")
            for j in range(NB):
                blk = ds(j * BLK, BLK)
                act.wait_ge(ctx_load, j * 16 + 16)
                act.wait_ge(qkv_mm, j)
                act.activation(ctx_hi, ctx32, ACT.Copy).then_inc(ctx_h, 1)
                act.wait_ge(qkv_mm, j + 1)
                act.activation(kv_hi[:, blk], bank[2][:, :], ACT.Copy, scale=1 / WS).then_inc(qkv_h, 1)
                act.activation(qc0_hi[:, blk], bank[0][:, :], ACT.Copy, scale=1 / WS).then_inc(qkv_h, 1)
                act.activation(qc1[:, blk], bank[1][:, :], ACT.Copy, scale=1 / WS).then_inc(qkv_h, 1)
                act.wait_ge(kr_sum, j + 1)
                act.activation(kr_hi[:, blk], krot, ACT.Copy).then_inc(kr_h, 1)
                act.wait_ge(kvt_mm, j + 1)
                o = bank[5][:, :].bitcast(F16)
                for i, t in enumerate((kvt_hi, kvt_lo)):
                    act.activation(t[:, ds(j * TPB, TPB), :],
                                   o[:, i * BLK:(i + 1) * BLK].rearrange("p (a b) -> p a b", a=TPB),
                                   ACT.Copy).then_inc(kvt_cp, 1)
            end_phase(act, "act")
            TR = bank[7][:, :].bitcast(F16)

            def rope_act(j, u):
                act.wait_ge(rope_sum, j * 4 + u + 1)
                act.wait_ge(rope_tr, ONE + j * 8 + u * 2)
                act.activation(rhl[:, :, 0, :], rot, ACT.Copy).then_inc(rope_h, 1)

            def rope_copy(j, u):
                for a in range(2):
                    act.wait_ge(rope_tr, ONE + j * 8 + u * 2 + a + 1)
                    act.activation(qrt[:, u % 2, a * 8:(a + 1) * 8, :].rearrange("p a b -> p (a b)"),
                                   TR[:, :], ACT.Copy).then_inc(rope_cp, 1)

            with act.Fori(0, NB) as j:
                act.wait_ge(score_mm, ONE + j * NG)
                for h in range(H):
                    act.wait_ge(q_mm[h % 2], j * 12 + h // 2 + 1)
                    act.activation(qp_hi[:, h, :], bank[5 + h % 2][:, :], ACT.Copy,
                                   scale=1 / WS).then_inc(q_h[h % 2], 1)
                rope_act(j, 0)
                for n in range(NG + 2):
                    if n < NG:
                        u, g, k = n // 4, n % 4, n % 2
                        if g == 0:
                            rope_copy(j, u)
                        act.wait_ge(pt_mm[k], ONE + j * 8 + n // 2)
                        act.wait_ge(smax, (j * NG + n) * 2 + 2)
                        for i in range(4):
                            m = act.activation(prob[:, k, i, :], bank[k][:, i * P:(i + 1) * P], ACT.Exp,
                                               bias=ebias[:, k, i:i + 1],
                                               scale=escale[:, u % 2, :],
                                               accum_out=esum[:, k, i:i + 1])
                        m.then_inc(exped[k], 1)
                        if g == 1 and u < 3:
                            rope_act(j, u + 1)
                    if 1 <= n <= NG:
                        q, k = n - 1, (n - 1) % 2
                        act.wait_ge(pt_mm[k], ONE + j * 8 + q // 2 + 1)
                        act.wait_ge(o_mm[k], ONE + j * 8 + q // 2)
                        act.activation(pt_hi[:, k, :], bank[2][:, :], ACT.Copy, scale=PS).then_inc(pth, 1)
                    if n >= 2:
                        q, k = n - 2, (n - 2) % 2
                        act.wait_ge(o_mm[k], ONE + j * 8 + q // 2 + 1)
                        act.wait_ge(y_mm[k], ONE + j * 8 + q // 2)
                        act.activation(ot_hi[:, k, :], bank[3][:, :], ACT.Copy, scale=OS / PS).then_inc(oth, 1)
            end_phase(act, "act")
            ln_scalar(act, 1)
            act.wait_ge(gate_in, 16)
            act.activation(gw_hi, gw32, ACT.Copy, scale=WS).then_inc(gate_s, 1)
            act.wait_ge(gate_v, 2)
            act.activation(gexp, gsub, ACT.Exp, scale=1 / WS).then_inc(gate_v, 1)
            for t in range(NB):
                act.wait_ge(gate_t, t + 1)
                act.activation(cwt[0:E, t * BLK:(t + 1) * BLK], bank[5][0:E, :], ACT.Copy,
                               scale=GS).then_inc(gate_c, 1)

            def ffn_scalar(f, gated):
                def units(k, s):
                    for c in range(GC):
                        act.wait_ge(f.up[c], k + 1)
                        act.activation(f.sg[:, c, :], bank[c][:, :], ACT.Silu,
                                       scale=1 / WS).then_inc(f.silu[c], 1)
                    for c in range(GC):
                        act.wait_ge(f.m2d[c], k + 1)
                        act.activation(f.h_hi[:, s % 2, c, :], f.m2[:, c, :], ACT.Copy).then_inc(f.hhi[c], 1)

                def split(gs, it, piece):
                    if piece == 0:
                        act.wait_ge(f.landed[gs], f.land0 + it * f.land + f.land)
                        if gated:
                            act.activation(f.sel[:, gs, :], f.sel32[:, gs, :], ACT.Copy).then_inc(f.selc[gs], 1)
                    cs = slice(piece * 1024, (piece + 1) * 1024)
                    act.activation(f.w_hi[:, gs, cs], f.w32[:, gs, cs], ACT.Copy,
                                   scale=WS).then_inc(f.whi[gs], 1)

                def body(j, last):
                    for s in range(2 * NB):
                        units(f.step0 + j * (2 * NB) + s, s)
                        gs, t = s // NB, s % NB
                        if 1 <= t <= f.pieces and not (last and gs == 1):
                            split(1 - gs, j + gs, t - 1)

                for piece in range(f.pieces):
                    split(0, 0, piece)
                n = f.groups // 2
                if n > 1:
                    with act.Fori(0, n - 1) as j:
                        body(j, False)
                body(n - 1, True)

            ffn_scalar(moe, True)
            end_phase(act, "act")
            ln_scalar(act, 2)
            for j in range(B):
                for s in range(2):
                    act.wait_ge(mem_load[s], j * 16 + 16)
                    dst = (memT_hi[:, :, ds(j * P, P)], mem_hi[:, ds(j, 1), :])[s]
                    act.activation(dst, mem32[:, s, :].rearrange("p (a b) -> p a b", a=(DC, 1)[s]),
                                   ACT.Copy).then_inc(mem_h[s], 1)
            for j in range(B // 2):
                for s in range(2):
                    act.wait_ge(mp_t[s], j)
                    act.wait_ge(ms_v[s], j * 3 + 2)
                    act.activation(mprob[:, s, :], bank[s][:, 0:P], ACT.Exp, bias=mst[:, s, 1:2],
                                   scale=mscale[:, ds(j * 2 + s, 1)],
                                   accum_out=mst[:, s, 2:3]).then_inc(ms_e[s], 1)
                for s in range(2):
                    act.wait_ge(mp_t[s], j + 1)
                    act.wait_ge(mo_mm[s], j)
                    act.activation(mpt_hi[:, s, :], bank[2 + s][:, 0:P], ACT.Copy).then_inc(mp_h[s], 1)
            end_phase(act, "act")
            ln_scalar(act, 3)
            act.wait_ge(pk_in, 48)
            act.activation(kw_hi, kw32, ACT.Copy, scale=WS).then_inc(pk_s, 1)
            for t in range(NB):
                act.wait_ge(pk_qmm, t + 1)
                act.activation(qT_hi[:, t * BLK:(t + 1) * BLK], bank[4 + t][:, :], ACT.Copy,
                               scale=1 / WS).then_inc(pk_qh, 1)
            act.wait_ge(pk_rmm, 1)
            for a in range(2):
                for i, t in enumerate((rx, ry)):
                    act.activation(t[:, a * 8:(a + 1) * 8, :].rearrange("p a b -> p (a b)"),
                                   bank[2 * i + a][:, :], ACT.Copy, scale=1 / WS).then_inc(pk_r, 1)
            act.wait_ge(pk_v, 3)
            act.activation(al, al, ACT.Exp).then_inc(pk_act, 1)
            act.activation(rx, rx, ACT.Exp).then_inc(pk_act, 1)
            act.activation(ry, ry, ACT.Exp).then_inc(pk_act, 1)
            for q in range(NT // 2):
                for h in range(2):
                    act.wait_ge(pk_t, ONE + q * 4 + h * 2 + 1)
                    act.activation(gT[:, 0:4, ds(q * 256 + h, P, 2)],
                                   bank[4][:, :].rearrange("p (a b) -> p a b", a=4), ACT.Copy,
                                   scale=WS).then_inc(pk_c0, 1)
            end_phase(act, "act")
            ffn_scalar(mlp, False)
            end_phase(act, "act")
            ffn_scalar(pkm, False)
            end_phase(act, "act")

        @block.vector
        def _(dve):
            def lo_of(o, src, scale, hi):
                return dve.scalar_tensor_tensor(out=o, in0=src, scalar=scale, in1=hi, op0=ALU.mult,
                                                op1=ALU.subtract)

            dve.wait_ge(small_hi, 3)
            lo_of(sw_lo, sw32, WS, sw_hi)
            with dve.Fori(0, H // 2) as j:
                for s in range(2):
                    dve.wait_ge(prep_hi[s], j + 1)
                    lo_of(hw_lo[:, s, :], hw32[:, s, :], WS, hw_hi[:, s, :]).then_inc(prep_lo[s], 1)
                for s in range(2):
                    hsl = ds(j * 2 + s, 1)
                    dve.wait_ge(prep_ahi[s], j + 1)
                    lo_of(att_a_lo[:, hsl, :].rearrange("p a b -> p (a b)"), bank[4 + 2 * s][:, 0:256],
                          1 / WS, att_a_hi[:, hsl, :].rearrange("p a b -> p (a b)"))
                    lo_of(att_vo_lo[:, hsl, :].rearrange("p a b -> p (a b)"), bank[5 + 2 * s][:, :],
                          1 / WS, att_vo_hi[:, hsl, :].rearrange("p a b -> p (a b)")).then_inc(prep_alo[s], 1)
            dve.wait_ge(x_in, 16 * LS)
            ln_vector(dve, 0, ln_xn_prep)
            end_phase(dve, "dve")
            dve.wait_ge(seg_in, 32)
            dve.tensor_copy(segf, segi).then_inc(seg_step, 1)
            dve.wait_ge(seg_step, 1)
            dve.tensor_scalar(v1, segf, 0.0, A_SCALE, ALU.is_ge, ALU.mult).then_inc(seg_step, 1)
            dve.tensor_scalar(v2, segf, float(S - 1 + LOOKBACK), None, ALU.is_le).then_inc(seg_step, 1)
            dve.wait_ge(seg_step, 3)
            dve.tensor_tensor(seg_scale, v1, v2, ALU.mult).then_inc(seg_step, 1)
            with dve.Fori(0, B) as b:
                dve.wait_ge(seg_step, b * 4 + 4)
                dve.tensor_scalar(dist[:, 0:S], iota, segf[:, ds(b, 1)], None, ALU.subtract).then_inc(seg_step, 1)
                dve.wait_ge(seg_step, b * 4 + 5)
                dve.tensor_scalar(gt1, dist[:, 0:S], 0.0, NEG, ALU.is_gt, ALU.mult).then_inc(seg_step, 1)
                dve.tensor_scalar(gt2, dist[:, 0:S], float(-LOOKBACK), NEG, ALU.is_lt,
                                  ALU.mult).then_inc(seg_step, 1)
                dve.wait_ge(seg_step, b * 4 + 7)
                dve.tensor_tensor(seg_bias[:, ds(b, 1), :].rearrange("p a b -> p (a b)"), gt1, gt2,
                                  ALU.add).then_inc(seg_step, 1)
            dve.wait_ge(seg_step, 4 * B + 4)
            with dve.Fori(0, NB) as j:
                blk = ds(j * BLK, BLK)
                dve.wait_ge(ctx_h, j + 1)
                dve.tensor_tensor(ctx_lo, ctx32, ctx_hi, ALU.subtract).then_inc(ctx_l, 1)
                dve.wait_ge(qkv_h, j * 3 + 1)
                lo_of(kv_lo[:, blk], bank[2][:, :], 1 / WS, kv_hi[:, blk]).then_inc(qkv_l, 1)
                dve.wait_ge(qkv_h, j * 3 + 2)
                lo_of(qc0_lo[:, blk], bank[0][:, :], 1 / WS, qc0_hi[:, blk]).then_inc(qkv_l, 1)
                dve.wait_ge(qkv_h, j * 3 + 3)
                lo_of(qc1[64:128, blk], bank[1][64:128, :], 1 / WS, qc1[64:128, blk]).then_inc(qkv_l, 1)
                dve.wait_ge(kr_mm, j + 1)
                for i, (t, tab) in enumerate(((kt1, cos_k), (kt2, sin_k))):
                    dve.tensor_tensor(t.rearrange("p (a b) -> p a b", a=TPB),
                                      bank[3 + i][:, :].rearrange("p (a b) -> p a b", a=TPB),
                                      tab.unsqueeze(1).to_broadcast([P, TPB, S]),
                                      ALU.mult).then_inc(kr_mul, 1)
                dve.wait_ge(kr_mul, ONE + j * 2 + 2)
                dve.tensor_tensor(krot, kt1, kt2, ALU.add).then_inc(kr_sum, 1)
                dve.wait_ge(kr_h, j + 1)
                dve.tensor_tensor(kr_lo[:, blk], krot, kr_hi[:, blk], ALU.subtract)
            end_phase(dve, "dve")

            def rope_dve(j, u):
                dve.wait_ge(rope_h, ONE + j * 4 + u)
                dve.wait_ge(rope_l, ONE + j * 4 + u)
                for a in range(2):
                    dve.wait_ge(q_mm[a], j * 12 + 8 + u + 1)
                    src = bank[5 + a][:, :].rearrange("p (h r) -> p h r", r=R)
                    hs = slice(8 * a, 8 * a + 8)
                    dve.tensor_tensor(rt1[:, hs, :], src, cos_q.unsqueeze(1).to_broadcast([P, 8, R]), ALU.mult)
                    for c in range(2):
                        oc = slice(32 * c, 32 * c + 32)
                        ic = slice(32 - 32 * c, 64 - 32 * c)
                        m = dve.tensor_tensor(rt2[:, hs, oc], src[:, :, ic],
                                              sin_q[:, oc].unsqueeze(1).to_broadcast([P, 8, 32]), ALU.mult)
                    m.then_inc(q_free[a], 1)

            with dve.Fori(0, NB) as j:
                for h in range(H):
                    k = h % 2
                    dve.wait_ge(q_h[k], j * 8 + h // 2 + 1)
                    lo_of(qp_lo[:, h, :], bank[5 + k][:, :], 1 / WS, qp_hi[:, h, :]).then_inc(q_free[k], 1)
                rope_dve(j, 0)
                for n in range(NG + 3):
                    if n < NG:
                        u, g, k = n // 4, n % 4, n % 2
                        dve.wait_ge(score_mm, ONE + j * NG + n + 1)
                        if g == 0:
                            dve.tensor_copy(escale[:, u % 2, :], seg_scale[:, ds(j * 4 + u, 1)])
                        dve.tensor_reduce(nmax[:, k, :], bank[k][:, :].rearrange("p (a b) -> p a b", a=4),
                                          AX.X, ALU.max, negate=True).then_inc(smax, 1)
                        dve.wait_ge(smax, (j * NG + n) * 2 + 1)
                        dve.tensor_scalar(ebias[:, k, :], nmax[:, k, :], seg_scale[:, ds(j * 4 + u, 1)],
                                          None, ALU.mult).then_inc(smax, 1)
                        if g == 0 and u < 3:
                            rope_dve(j, u + 1)
                        dve.wait_ge(exped[k], ONE + j * 8 + n // 2 + 1)
                        dve.reciprocal(rinv[:, k, :], esum[:, k, :]).then_inc(recip[k], 1)
                    if 1 <= n <= NG:
                        q, k = n - 1, (n - 1) % 2
                        dve.wait_ge(pth, j * NG + q + 1)
                        lo_of(pt_lo[:, k, :], bank[2][:, :], PS, pt_hi[:, k, :]).then_inc(ptl, 1)
                    if 2 <= n <= NG + 1:
                        q, k = n - 2, (n - 2) % 2
                        dve.wait_ge(oth, j * NG + q + 1)
                        lo_of(ot_lo[:, k, :], bank[3][:, :], OS / PS, ot_hi[:, k, :]).then_inc(otl, 1)
                    if n >= 3 and (n - 3) % 4 == 3:
                        q = n - 3
                        u = q // 4
                        xv = x[:, ds(j * 4 + u, 1), :].rearrange("p a b -> p (a b)")
                        dve.wait_ge(y_mm[1], ONE + j * 8 + q // 2 + 1)
                        dve.scalar_tensor_tensor(out=xv, in0=bank[4][:, :], scalar=1 / (OS * WS), in1=xv,
                                                 op0=ALU.mult, op1=ALU.add).then_inc(yadd, 1)
            end_phase(dve, "dve")
            ln_vector(dve, 1, ln_xn_moe)
            dve.wait_ge(gate_s, 1)
            lo_of(gw_lo, gw32, WS, gw_hi).then_inc(gate_s, 1)
            dve.memset(gsc, 2.0)
            dve.memset(cwt, 0.0)
            lg = bank[4][:, 0:NT * E].rearrange("p (a b) -> p a b", b=E)
            dve.wait_ge(gate_mm, 1)
            dve.tensor_reduce(gmx, lg, AX.X, ALU.max).then_inc(gate_v, 1)
            dve.wait_ge(gate_v, 1)
            dve.tensor_tensor(gsub, lg, gmx.unsqueeze(2).to_broadcast([P, NT, E]), ALU.subtract).then_inc(gate_v, 1)
            dve.wait_ge(gate_v, 3)
            dve.tensor_reduce(gsum, gexp, AX.X, ALU.add).then_inc(gate_v, 1)
            dve.wait_ge(gate_v, 4)
            dve.reciprocal(grc, gsum).then_inc(gate_v, 1)
            dve.wait_ge(gate_v, 5)
            dve.tensor_tensor(gsc[:, :, 0:E], gexp, grc.unsqueeze(2).to_broadcast([P, NT, E]),
                              ALU.mult).then_inc(gate_v, 1)
            dve.wait_ge(gate_v, 6)
            for t in range(NT):
                m = dve.max(gtop[:, t, :], gsc[:, t, :])
            m.then_inc(gate_v, 1)
            dve.wait_ge(gate_v, 7)
            for t in range(NT):
                m = dve.match_replace(grep_[:, t, :], gtop[:, t, :], gsc[:, t, :], 0.0)
            m.then_inc(gate_v, 1)
            dve.wait_ge(gate_v, 8)
            dve.tensor_tensor(gcw, gsc[:, :, 0:E], grep_[:, :, 0:E], ALU.subtract).then_inc(gate_done, 1)
            for t in range(NB):
                dve.wait_ge(gate_c, 2 * t + 1)
                lo_of(cwt[32:32 + E, t * BLK:(t + 1) * BLK], bank[5][0:E, :], GS,
                      cwt[0:E, t * BLK:(t + 1) * BLK]).then_inc(gate_c, 1)

            def ffn_vector(f, kind):
                def split(gs, it, piece):
                    dve.wait_ge(f.whi[gs], f.piece0 + it * f.pieces + piece + 1)
                    cs = slice(piece * 1024, (piece + 1) * 1024)
                    lo_of(f.w_lo[:, gs, cs], f.w32[:, gs, cs], WS, f.w_hi[:, gs, cs]).then_inc(f.wlo[gs], 1)

                def units(j, s):
                    k = f.step0 + j * (2 * NB) + s
                    for c in range(GC):
                        dve.wait_ge(f.silu[c], k + 1)
                        dve.wait_ge(f.hlo[c], k)
                        if kind == "moe":
                            dve.scalar_tensor_tensor(out=f.m1[:, c, :], in0=f.sg[:, c, :], scalar=1 / GS,
                                                     in1=bank[2 + c][:, :], op0=ALU.mult,
                                                     op1=ALU.mult).then_inc(f.m1d[c], 1)
                            dve.wait_ge(f.m1d[c], k + 1)
                            dve.tensor_tensor(f.m2[:, c, :], f.m1[:, c, :], bank[4 + c][:, :],
                                              ALU.mult).then_inc(f.m2d[c], 1)
                        elif kind == "mlp":
                            dve.tensor_tensor(f.m2[:, c, :], f.sg[:, c, :], bank[2 + c][:, :],
                                              ALU.mult).then_inc(f.m2d[c], 1)
                        else:
                            g = gT[:, ds((j * 2 + s // NB) * GC + c, 1), (s % NB) * BLK:(s % NB + 1) * BLK]
                            dve.tensor_tensor(f.m2[:, c, :], f.sg[:, c, :], g.rearrange("p a b -> p (a b)"),
                                              ALU.mult).then_inc(f.m2d[c], 1)

                def adds(j, s):
                    k = f.step0 + j * (2 * NB) + s
                    for q in range(TPB):
                        yb = q % 2
                        xv = x[:, (s % NB) * TPB + q, :]
                        dve.wait_ge(f.ymm[yb], k * 2 + q // 2 + 1)
                        dve.scalar_tensor_tensor(out=xv, in0=bank[6 + yb][:, :], scalar=1 / (WS * WS), in1=xv,
                                                 op0=ALU.mult, op1=ALU.add).then_inc(f.yadd[yb], 1)

                def body(j, last):
                    for s in range(2 * NB):
                        if not (last and s == 2 * NB - 1):
                            units(j, s + 1)
                        adds(j, s)
                        gs, t = (s + 1) // NB % 2, (s + 1) % NB
                        it = j + 1 if s + 1 == 2 * NB else j
                        if 1 <= t <= f.pieces and not (last and gs == 1):
                            split(1 - gs, it + gs, t - 1)

                for piece in range(f.pieces):
                    split(0, 0, piece)
                units(0, 0)
                n = f.groups // 2
                if n > 1:
                    with dve.Fori(0, n - 1) as j:
                        body(j, False)
                body(n - 1, True)

            ffn_vector(moe, "moe")
            end_phase(dve, "dve")
            dve.wait_ge(mask_in, 16)
            dve.tensor_copy(mm_f.rearrange("p a b -> p (a b)"), mm8).then_inc(mask_s, 1)
            dve.wait_ge(mask_s, 1)
            dve.tensor_scalar(mm_bias, mm_f, -NEG, NEG, ALU.mult, ALU.add).then_inc(mask_s, 1)
            dve.tensor_reduce(mvalid, mm_f, AX.X, ALU.max).then_inc(mask_s, 1)
            dve.wait_ge(mask_s, 3)
            dve.tensor_scalar(mscale, mvalid, M_SCALE, None, ALU.mult).then_inc(mask_s, 1)
            ln_vector(dve, 2, ln_xn_mem)
            with dve.Fori(0, B) as j:
                for s in range(2):
                    dve.wait_ge(mem_h[s], j + 1)
                    dst = (memT_lo[:, :, ds(j * P, P)], mem_lo[:, ds(j, 1), :])[s]
                    hi = (memT_hi[:, :, ds(j * P, P)], mem_hi[:, ds(j, 1), :])[s]
                    dve.tensor_tensor(dst, mem32[:, s, :].rearrange("p (a b) -> p a b", a=(DC, 1)[s]), hi,
                                      ALU.subtract).then_inc(mem_l[s], 1)
            with dve.Fori(0, B // 2) as j:
                for s in range(2):
                    b1 = ds(j * 2 + s, 1)
                    dve.wait_ge(ms_mm[s], j + 1)
                    dve.tensor_reduce(mst[:, s, 0:1], bank[s][:, 0:P], AX.X, ALU.max,
                                      negate=True).then_inc(ms_v[s], 1)
                    dve.wait_ge(ms_v[s], j * 3 + 1)
                    dve.tensor_scalar(mst[:, s, 1:2], mst[:, s, 0:1], mscale[:, b1], None,
                                      ALU.mult).then_inc(ms_v[s], 1)
                for s in range(2):
                    b1 = ds(j * 2 + s, 1)
                    dve.wait_ge(ms_e[s], ONE + j + 1)
                    dve.reciprocal(mst[:, s, 3:4], mst[:, s, 2:3]).then_inc(ms_v[s], 1)
                for s in range(2):
                    dve.wait_ge(mp_h[s], j + 1)
                    dve.tensor_tensor(mpt_lo[:, s, :], bank[2 + s][:, 0:P], mpt_hi[:, s, :],
                                      ALU.subtract).then_inc(mp_l[s], 1)
                for s in range(2):
                    b1 = ds(j * 2 + s, 1)
                    xv = x[:, b1, :].rearrange("p a b -> p (a b)")
                    dve.wait_ge(ms_v[s], j * 3 + 3)
                    dve.tensor_tensor(mfac[:, s, :], mst[:, s, 3:4], mvalid[:, b1], ALU.mult).then_inc(mem_fac[s], 1)
                    dve.wait_ge(mem_fac[s], j + 1)
                    dve.wait_ge(mo_mm[s], j + 1)
                    dve.scalar_tensor_tensor(out=xv, in0=bank[4 + s][:, :], scalar=mfac[:, s, :], in1=xv,
                                             op0=ALU.mult, op1=ALU.add).then_inc(mo_a[s], 1)
            end_phase(dve, "dve")
            ln_vector(dve, 3, ln_xn_pk)
            dve.wait_ge(pk_s, 1)
            lo_of(kw_lo, kw32, WS, kw_hi).then_inc(pk_s, 1)
            for t in range(NB):
                dve.wait_ge(pk_qh, t + 1)
                ts_ = slice(t * BLK, (t + 1) * BLK)
                lo_of(qT_lo[:, ts_], bank[4 + t][:, :], 1 / WS, qT_hi[:, ts_]).then_inc(pk_ql, 1)
            dve.wait_ge(pk_r, 4)
            for u in range(NT):
                dve.max(sx[:, u, :], rx[:, u, :])
                m = dve.max(sy[:, u, :], ry[:, u, :])
            m.then_inc(pk_v, 1)
            dve.wait_ge(pk_v, 1)
            for u in range(NT):
                dve.max_index(ixu[:, u, :], sx[:, u, :], rx[:, u, :])
                dve.max_index(iyu[:, u, :], sy[:, u, :], ry[:, u, :])
                m = dve.tensor_tensor(al[:, u, :].rearrange("p (a b) -> p a b", a=8),
                                      sx[:, u, :].unsqueeze(2).to_broadcast([P, 8, 8]),
                                      sy[:, u, :].unsqueeze(1).to_broadcast([P, 8, 8]), ALU.add)
            m.then_inc(pk_v, 1)
            step = [0]

            def after(m):
                step[0] += 1
                m.then_inc(pk_g0, 1)
                dve.wait_ge(pk_g0, step[0])

            dve.wait_ge(pk_v, 2)
            dve.tensor_copy(ixf, ixu)
            for u in range(NT):
                m = dve.max(top[:, u, :], al[:, u, :])
            after(dve.tensor_copy(iyf, iyu))
            for u in range(NT):
                m = dve.match_replace(al_rep[:, u, :], top[:, u, :], al[:, u, :], -3e38)
            after(m)
            after(dve.tensor_tensor(al_rep, al_rep, al, ALU.not_equal))
            dve.tensor_tensor(al, al, top[:, :, 0:1].to_broadcast([P, NT, 64]), ALU.subtract)
            dve.tensor_tensor(rx, rx, sx[:, :, 0:1].to_broadcast([P, NT, NK]), ALU.subtract)
            dve.tensor_tensor(ry, ry, sy[:, :, 0:1].to_broadcast([P, NT, NK]), ALU.subtract).then_inc(pk_v, 1)
            dve.wait_ge(pk_act, 3)
            after(dve.tensor_tensor(al, al, al_rep, ALU.mult))
            dve.tensor_reduce(den, al, AX.X, ALU.add)
            dve.tensor_reduce(wsum.rearrange("p a b -> p (a b)"), al.rearrange("p u (a b) -> p (u a) b", b=8),
                              AX.X, ALU.add)
            after(dve.tensor_reduce(cnt.rearrange("p a b -> p (a b)"),
                                    al_rep.rearrange("p u (a b) -> p (u a) b", b=8), AX.X, ALU.add))
            dve.tensor_scalar(wtmp, ixf, float(KX), None, ALU.is_ge)
            after(dve.reciprocal(far, den))
            dve.tensor_tensor(ex_, rx[:, :, 0:KX], far.unsqueeze(2).to_broadcast([P, NT, KX]), ALU.mult)
            after(dve.tensor_tensor(wtmp, wtmp, wsum, ALU.mult))
            after(dve.tensor_reduce(den, wtmp, AX.X, ALU.add))
            after(dve.tensor_tensor(den, den, far, ALU.mult))
            with dve.Fori(0, NT // 2) as q:
                for h in range(2):
                    u = q * 2 + h
                    u1 = ds(u, 1)
                    dve.wait_ge(pk_u, ONE + u * 6)
                    dve.tensor_tensor(eq, iota64.unsqueeze(1).to_broadcast([P, 8, NK]),
                                      iyf[:, u1, :].rearrange("p a b -> p b a").to_broadcast([P, 8, NK]),
                                      ALU.is_equal)
                    dve.tensor_tensor(eqx, iota64[:, 0:KX].unsqueeze(2).to_broadcast([P, KX, 8]),
                                      ixf[:, u1, :].to_broadcast([P, KX, 8]), ALU.is_equal).then_inc(pk_u, 1)
                    dve.wait_ge(pk_u, ONE + u * 6 + 1)
                    dve.tensor_tensor(eq, eq, rank8.unsqueeze(2).to_broadcast([P, 8, NK]), ALU.mult)
                    dve.tensor_tensor(eqx, eqx, cnt[:, u1, :].to_broadcast([P, KX, 8]), ALU.mult).then_inc(pk_u, 1)
                    dve.wait_ge(pk_u, ONE + u * 6 + 2)
                    dve.tensor_reduce(s64[:, 0, :], eq.rearrange("p a b -> p b a"), AX.X, ALU.add)
                    dve.tensor_reduce(cc[:, 0, :], eqx, AX.X, ALU.add).then_inc(pk_u, 1)
                    dve.wait_ge(pk_u, ONE + u * 6 + 3)
                    dve.wait_ge(pk_t, ONE + u * 2)
                    dve.tensor_tensor(G, s64[:, 0:1, :].to_broadcast([P, KX, NK]),
                                      cc[:, 0, :].unsqueeze(2).to_broadcast([P, KX, NK]), ALU.add).then_inc(pk_u, 1)
                    dve.wait_ge(pk_u, ONE + u * 6 + 4)
                    dve.scalar_tensor_tensor(out=G, in0=G, scalar=8.0,
                                             in1=ry[:, u1, :].to_broadcast([P, KX, NK]),
                                             op0=ALU.is_gt, op1=ALU.mult).then_inc(pk_u, 1)
                    dve.wait_ge(pk_u, ONE + u * 6 + 5)
                    dve.tensor_tensor(G, G, ex_[:, u1, :].rearrange("p a b -> p b a").to_broadcast([P, KX, NK]),
                                      ALU.mult).then_inc(pk_u, 1)
                    dve.wait_ge(pk_u, ONE + u * 6 + 6)
                    dve.tensor_tensor(G[:, KX - 1, NK - 1:NK], G[:, KX - 1, NK - 1:NK], den[:, u1],
                                      ALU.add).then_inc(pk_g, 1)
                    dve.wait_ge(pk_t, ONE + u * 2 + 2)
                    dve.tensor_scalar(gT[:, 4:8, ds(q * 256 + h, P, 2)],
                                      bank[5][:, :].rearrange("p (a b) -> p a b", a=4), WS, None,
                                      ALU.mult).then_inc(pk_c1, 1)
            end_phase(dve, "dve")
            ffn_vector(mlp, "mlp")
            end_phase(dve, "dve")
            ffn_vector(pkm, "pkm")
            end_phase(dve, "dve")

        @block.gpsimd
        def _(pool):
            pool.memset(neg_half[:, :, :], -0.5).then_inc(half_set, 1)
            pool.wait_ge(half_set, 1)
            ln_gpsimd(pool, 0)
            end_phase(pool, "pool")
            end_phase(pool, "pool")

            def rope_pool(j, u):
                for a in range(2):
                    pool.wait_ge(q_free[a], ONE + j * 12 + 9 + u)
                pool.tensor_tensor(rot, rt1, rt2, ALU.add).then_inc(rope_sum, 1)
                pool.wait_ge(rope_sum, j * 4 + u + 1)
                pool.wait_ge(rope_h, ONE + j * 4 + u + 1)
                pool.tensor_tensor(rhl[:, :, 1, :], rot, rhl[:, :, 0, :], ALU.subtract).then_inc(rope_l, 1)

            with pool.Fori(0, NB) as j:
                rope_pool(j, 0)
                for n in range(NG):
                    u, g, k = n // 4, n % 4, n % 2
                    pool.wait_ge(recip[k], j * 8 + n // 2 + 1)
                    pool.tensor_tensor(prob[:, k, :, :], prob[:, k, :, :],
                                       rinv[:, k, :].unsqueeze(2).to_broadcast([P, 4, P]),
                                       ALU.mult).then_inc(normed[k], 1)
                    if g == 1 and u < 3:
                        rope_pool(j, u + 1)
            end_phase(pool, "pool")
            ln_gpsimd(pool, 1)

            def ffn_gpsimd(f):
                def body(j, last):
                    for s in range(2 * NB):
                        k = f.step0 + j * (2 * NB) + s
                        for c in range(GC):
                            pool.wait_ge(f.hhi[c], k + 1)
                            pool.tensor_tensor(f.h_lo[:, s % 2, c, :], f.m2[:, c, :], f.h_hi[:, s % 2, c, :],
                                               ALU.subtract).then_inc(f.hlo[c], 1)

                n = f.groups // 2
                if n > 1:
                    with pool.Fori(0, n - 1) as j:
                        body(j, False)
                body(n - 1, True)

            ffn_gpsimd(moe)
            end_phase(pool, "pool")
            ln_gpsimd(pool, 2)
            end_phase(pool, "pool")
            ln_gpsimd(pool, 3)
            end_phase(pool, "pool")
            ffn_gpsimd(mlp)
            end_phase(pool, "pool")
            ffn_gpsimd(pkm)
            end_phase(pool, "pool")


def shape_constants():
    half = R // 2
    inv = (1.0 / 10000.0 ** (np.arange(half, dtype=np.float32) / np.float32(half))).astype(np.float32)
    ang = np.arange(S, dtype=np.float32)[:, None] * inv
    cos, sin = np.cos(ang).astype(np.float32), np.sin(ang).astype(np.float32)
    cos2, sin2 = np.concatenate([cos, cos], 1) / WS, np.concatenate([-sin, sin], 1) / WS
    sel = np.zeros((P, E * MOE_D), np.float16)
    for e in range(E):
        sel[e, e * MOE_D:(e + 1) * MOE_D] = 1.0
        sel[32 + e, e * MOE_D:(e + 1) * MOE_D] = 1.0
    return {
        "ident": np.eye(P, dtype=np.float32),
        "iota": np.tile(np.arange(S, dtype=np.float32), (P, 1)),
        "rank8": np.tile(8.0 - np.arange(8, dtype=np.float32), (P, 1)),
        "cos_q": cos2.astype(np.float32), "sin_q": sin2.astype(np.float32),
        "cos_k": np.tile(cos2.T, (2, 1)).astype(np.float32), "sin_k": np.tile(sin2.T, (2, 1)).astype(np.float32),
        "moe_sel": np.ascontiguousarray(sel.reshape(P, -1, GW).transpose(1, 0, 2)),
    }


def by_group(gate_t, up_t, down):
    def wide(w):
        return w.reshape(DC, P, -1, GW).transpose(2, 1, 0, 3).reshape(-1, P, DC * GW)
    parts = [wide(gate_t)] + ([wide(up_t)] if up_t is not None else [])
    parts.append(down.reshape(-1, GC, P, D).transpose(0, 2, 1, 3).reshape(-1, P, GC * D))
    return np.concatenate(parts, axis=2)


def lay_out(i):
    i = {k: np.asarray(v) for k, v in i.items()}
    a = dict(shape_constants())
    a["x"] = i["x"].transpose(1, 0, 2)
    a["ctx"] = i["ctx_2048"].transpose(1, 0, 2)
    a["ctxT"] = i["ctx_2048"].reshape(T, DC, P).transpose(2, 1, 0)
    a["seg"] = i["itok_BxS_0_1023"].T
    a["mem_mask"] = i["mask_BxS2_bk0"].reshape(T)
    dq = i["L0_xattn_W_dq"].reshape(DC, P, QC).transpose(1, 0, 2)
    dq = np.concatenate([dq, dq[:, :, P:]], axis=2).reshape(P, -1)
    kvc = i["L0_xattn_W_kvc"].reshape(DC, P, KVC).transpose(1, 0, 2).reshape(P, -1)
    kr = i["L0_xattn_W_kr"]
    sw = np.concatenate([kr[:, R // 2:], kr[:, :R // 2]], axis=1)
    qr = i["L0_xattn_W_qr"]
    a["small_w"] = np.concatenate([dq, kvc, kr, kr, sw, sw, qr[:P], np.concatenate([qr[P:], qr[P:]], axis=0)],
                                  axis=1)
    uq = i["L0_xattn_W_uq"].reshape(QC, H, HD).transpose(1, 2, 0)
    uk = i["L0_xattn_W_uk"].reshape(KVC, H, HD).transpose(1, 2, 0)
    uv = i["L0_xattn_W_uv"].reshape(KVC, H, HD).transpose(1, 2, 0)
    wo = i["L0_xattn_W_o"].reshape(H, HD, D)
    a["head_w"] = np.concatenate([uq, uq[:, :, P:], uk, uv, wo], axis=2)
    a["moe_gate"] = i["L0_ffn_gate_w"].reshape(E, DC, P).transpose(2, 1, 0).reshape(P, DC * E)
    a["moe_w"] = by_group(i["L0_ffn_w_gate"].reshape(-1, D).T, i["L0_ffn_w_up"].reshape(-1, D).T,
                          i["L0_ffn_w_down"].transpose(0, 2, 1).reshape(-1, D))
    a["mlp_w"] = by_group(i["L1_ffn_gate_w"], i["L1_ffn_up_w"], i["L1_ffn_down_w"])
    a["pk_e"] = by_group(i["L1_ffn_down_embed"].T, None, i["L1_ffn_up_embed"])
    wq = i["L1_ffn_W_q"].reshape(DC, P, P).transpose(1, 0, 2).reshape(P, -1)
    keys = np.zeros((P, 2, 2, NK), np.float32)
    for t in range(2):
        for h in range(2):
            keys[h * NK:(h + 1) * NK, t, h] = i["L1_ffn_keys"][t]
    a["pk_w"] = np.concatenate([wq, keys.reshape(P, -1)], axis=1)
    return {k: np.ascontiguousarray(v) for k, v in a.items()}


def kernel(**inputs):
    import concourse.bacc as bacc
    from concourse.bass_utils import run_bass_kernel_spmd

    nc = bacc.Bacc("TRN2", target_bir_lowering=False, num_devices=1)
    arrays, aps = {}, {}
    for name, a in lay_out(inputs).items():
        arrays[f"in_{name}"] = a
        aps[name] = nc.dram_tensor(f"in_{name}", a.shape, mybir.dt.from_np(a.dtype), kind="ExternalInput").ap()
    out = nc.dram_tensor("out", (P, NT, D), F32, kind="ExternalOutput").ap()
    build(nc, aps, out)
    r = run_bass_kernel_spmd(nc, [arrays], core_ids=[0])
    return r.results[0]["out"].transpose(1, 0, 2).reshape(B, S, D)
```

```python
from contextlib import ExitStack

import numpy as np

import concourse.bass as bass
import concourse.mybir as mybir

F32, F16, BF16 = mybir.dt.float32, mybir.dt.float16, mybir.dt.bfloat16
I32, U32, U8 = mybir.dt.int32, mybir.dt.uint32, mybir.dt.uint8
ALU = mybir.AluOpType
ACT = mybir.ActivationFunctionType
AX = mybir.AxisListType
ds = bass.ds

P = 128
B, S, D = 16, 128, 512
T = B * S
NT = T // P
DC = D // P
BLK = 512
NB = T // BLK
TPB = BLK // P
H, HD, KVC, QC, R = 16, 128, 128, 192, 64
LOOKBACK = 8
NEG = -1e30
E, TOPE, MOE_D = 16, 6, 352
INTER, NEXP, NK, TOPK = 2048, 1024, 64, 8
KX = NEXP // NK
EPS = 1e-5
WS = 64.0
OS = 8.0
GS = 16.0
PS = 64.0
A_SCALE = 1.0 / float(np.sqrt(np.float32(HD + R)))
M_SCALE = 1.0 / float(np.sqrt(np.float32(D)))
GC = 2
GW = GC * P


def size_of(dt):
    return {F32: 4, I32: 4, U32: 4, F16: 2, BF16: 2, U8: 1}[dt]


def build(nc, ins, out):
    with ExitStack() as ctx:
        def sb(name, shape, dt=F32):
            return ctx.enter_context(nc.sbuf_tensor(name, shape, dt))

        def sem(name):
            return ctx.enter_context(nc.semaphore(name))

        def carve(arena, at, dims, dt=F32):
            n = int(np.prod(dims)) * size_of(dt) // 4
            v = arena[:, at:at + n]
            if dt != F32:
                v = v.bitcast(dt)
            if len(dims) == 2:
                v = v.rearrange("p (a b) -> p a b", a=dims[0])
            elif len(dims) == 3:
                v = v.rearrange("p (a b c) -> p a b c", a=dims[0], b=dims[1])
            return v, at + n

        class Room:
            def __init__(self, arena, words):
                self.arena, self.words, self.at = arena, words, 0

            def take(self, *dims, dt=F32):
                v, self.at = carve(self.arena, self.at, dims, dt)
                assert self.at <= self.words, (self.at, self.words)
                return v

        x = sb("x", [P, NT, D])
        XT_W, WORK_W = 8192, 36400
        xt_arena = sb("xt_arena", [P, XT_W])
        work_arena = sb("work_arena", [P, WORK_W])
        id32 = sb("id32", [P, P])
        id16 = sb("id16", [P, P], F16)
        idbf = sb("idbf", [P, P], BF16)
        bank = [ctx.enter_context(nc.psum_tensor(f"bank{i}", [P, 512], F32)) for i in range(8)]

        xt_room = Room(xt_arena, XT_W)
        xt_hi = xt_room.take(DC, T, dt=F16)
        xt_lo = xt_room.take(DC, T, dt=F16)
        q_room = Room(xt_arena, XT_W)
        qp_hi = q_room.take(H, BLK, dt=F16)
        qp_lo = q_room.take(H, BLK, dt=F16)

        phase_done = sem("phase_done")
        phase = {}

        def end_phase(eng, name):
            n = phase.get(name, 0) + 1
            phase[name] = n
            eng.drain().then_inc(phase_done, 1)
            eng.wait_ge(phase_done, 5 * n)

        LS = 4
        ln_st = sb("ln_st", [P, LS, 6])
        ln_mv = sb("ln_mv", [P, LS, 2])
        ln_ve = sb("ln_ve", [P, LS, 1])
        ln_rs = sb("ln_rs", [P, LS, 1])
        neg_half = sb("neg_half", [P, LS, 1])
        ln_var, ln_rstd, half_set = sem("ln_var"), sem("ln_rstd"), sem("half_set")

        ln_stat, ln_norm, ln_turned, ln_hi, ln_lo = (
            [sem(f"ln_{what}{s}") for s in range(LS)] for what in ("stat", "norm", "turned", "hi", "lo"))
        LN_IT = NT // LS

        def tile_cols(t, j, s):
            return t[:, :, ds((j * LS + s) * P, P)]

        def ln_vector(dve, n, xn):
            def stats(j):
                done = j + n * LN_IT
                for s in range(LS):
                    dve.bn_stats(ln_st[:, s, :], x[:, j * LS + s, :]).then_inc(ln_stat[s], 1)
                for s in range(LS):
                    dve.wait_ge(ln_stat[s], done * 2 + 1)
                    dve.bn_aggr(ln_mv[:, s, :], ln_st[:, s, :]).then_inc(ln_stat[s], 1)
                for s in range(LS):
                    dve.wait_ge(ln_stat[s], done * 2 + 2)
                dve.tensor_scalar(ln_ve[:, :, :], ln_mv[:, :, 1:2], EPS, None, ALU.add).then_inc(ln_var, 1)

            stats(0)
            for j in range(LN_IT):
                done = j + n * LN_IT
                dve.wait_ge(ln_rstd, done + 1)
                for s in range(LS):
                    dve.wait_ge(ln_turned[s], done)
                    dve.tensor_scalar(xn[:, s, :], x[:, j * LS + s, :], ln_mv[:, s, 0:1], ln_rs[:, s, :],
                                      ALU.subtract, ALU.mult).then_inc(ln_norm[s], 1)
                if j + 1 < LN_IT:
                    stats(j + 1)
                for s in range(LS):
                    dve.wait_ge(ln_hi[s], done + 1)
                    dve.tensor_tensor(tile_cols(xt_lo, j, s),
                                      bank[s][:, :].rearrange("p (a b) -> p a b", a=DC),
                                      tile_cols(xt_hi, j, s), ALU.subtract).then_inc(ln_lo[s], 1)

        def ln_gpsimd(pool, n):
            with pool.Fori(0, LN_IT) as j:
                done = j + n * LN_IT
                pool.wait_ge(ln_var, done + 1)
                pool.tensor_tensor(ln_rs[:, :, :], ln_ve[:, :, :], neg_half[:, :, :], ALU.pow).then_inc(ln_rstd, 1)

        def ln_tensor(pe, n, xn):
            with pe.Fori(0, LN_IT) as j:
                done = j + n * LN_IT
                for s in range(LS):
                    pe.wait_ge(ln_norm[s], done + 1)
                    pe.wait_ge(ln_lo[s], ONE + done)
                    for c in range(DC):
                        m = pe.transpose(bank[s][:, c * P:(c + 1) * P], xn[:, s, c * P:(c + 1) * P], id32[:, :])
                    m.then_inc(ln_turned[s], 1)

        def ln_scalar(act, n):
            for j in range(LN_IT):
                done = j + n * LN_IT
                for s in range(LS):
                    act.wait_ge(ln_turned[s], done + 1)
                    act.activation(tile_cols(xt_hi, j, s),
                                   bank[s][:, :].rearrange("p (a b) -> p a b", a=DC),
                                   ACT.Copy).then_inc(ln_hi[s], 1)

        def mm3(pe, o, a_hi, a_lo, b_hi, b_lo, start, stop):
            pe.matmul(o, a_hi, b_hi, start=start, stop=False)
            pe.matmul(o, a_hi, b_lo, start=False, stop=False)
            return pe.matmul(o, a_lo, b_hi, start=False, stop=stop)

        wr = Room(work_arena, WORK_W)
        att_a_hi = wr.take(H, 2 * P, dt=F16)
        att_a_lo = wr.take(H, 2 * P, dt=F16)
        att_vo_hi = wr.take(H, D, dt=F16)
        att_vo_lo = wr.take(H, D, dt=F16)
        SW = DC * 256 + DC * 128 + 256 + 2048
        sw_hi = wr.take(SW, dt=F16)
        sw_lo = wr.take(SW, dt=F16)
        qc0_hi = wr.take(T, dt=F16)
        qc0_lo = wr.take(T, dt=F16)
        qc1 = wr.take(T, dt=F16)
        kv_hi = wr.take(T, dt=F16)
        kv_lo = wr.take(T, dt=F16)
        kvt_hi = wr.take(B, KVC, dt=F16)
        kvt_lo = wr.take(B, KVC, dt=F16)
        kr_hi = wr.take(T, dt=F16)
        kr_lo = wr.take(T, dt=F16)
        seg_bias = wr.take(B, S, dt=BF16)
        seg_scale = wr.take(B)
        cos_q = wr.take(R)
        sin_q = wr.take(R)
        cos_k = wr.take(S)
        sin_k = wr.take(S)
        att_end = wr.at

        def swv(t, at, *dims):
            n = int(np.prod(dims))
            v = t[:, at:at + n]
            return v.rearrange("p (a b) -> p a b", a=dims[0]) if len(dims) == 2 else v
        o_kvc, o_kr, o_qr = DC * 256, DC * 384, DC * 384 + 256
        wdq = [swv(t, 0, DC, 256) for t in (sw_hi, sw_lo)]
        wkvc = [swv(t, o_kvc, DC, 128) for t in (sw_hi, sw_lo)]
        wkr = [swv(t, o_kr, 2, 128) for t in (sw_hi, sw_lo)]
        wqr = [swv(t, o_qr, 2, 1024) for t in (sw_hi, sw_lo)]

        HW = 256 + 128 + 128 + 512
        pr = Room(work_arena, WORK_W)
        pr.at = att_end
        hw32 = pr.take(2, HW)
        hw_hi = pr.take(2, HW, dt=F16)
        hw_lo = pr.take(2, HW, dt=F16)
        ln_xn_prep = pr.take(LS, D)
        sw32 = xt_arena[:, 0:SW]
        prep_load = [sem(f"prep_load{s}") for s in range(2)]
        prep_hi = [sem(f"prep_hi{s}") for s in range(2)]
        prep_lo = [sem(f"prep_lo{s}") for s in range(2)]
        prep_mm = [sem(f"prep_mm{s}") for s in range(2)]
        prep_ahi = [sem(f"prep_ahi{s}") for s in range(2)]
        prep_alo = [sem(f"prep_alo{s}") for s in range(2)]
        consts_in, small_in, small_hi = (sem(n) for n in ("consts_in", "small_in", "small_hi"))
        x_in = sem("x_in")

        jr = Room(work_arena, WORK_W)
        jr.at = att_end
        ctx32 = jr.take(DC, BLK)
        ctx_hi = jr.take(DC, BLK, dt=F16)
        ctx_lo = jr.take(DC, BLK, dt=F16)
        kt1 = jr.take(BLK)
        kt2 = jr.take(BLK)
        krot = jr.take(BLK)
        segi = jr.take(B, dt=I32)
        segf = jr.take(B)
        iota = jr.take(S)
        dist = kt1
        gt1 = jr.take(S)
        gt2 = jr.take(S)
        v1 = jr.take(B)
        v2 = jr.take(B)
        ctx_load, ctx_h, ctx_l = sem("ctx_load"), sem("ctx_h"), sem("ctx_l")
        qkv_mm, qkv_h, qkv_l = sem("qkv_mm"), sem("qkv_h"), sem("qkv_l")
        kr_mm, kr_mul, kr_sum, kr_h = (sem(n) for n in ("kr_mm", "kr_mul", "kr_sum", "kr_h"))
        kvt_mm, kvt_cp = sem("kvt_mm"), sem("kvt_cp")
        seg_in, seg_step = sem("seg_in"), sem("seg_step")

        ar = Room(work_arena, WORK_W)
        ar.at = att_end
        rt1 = ar.take(H, R)
        rt2 = ar.take(H, R)
        rot = rt1
        rhl = ar.take(H, 2, R, dt=F16)
        qrt = ar.take(2, H, P, dt=F16)
        prob = ar.take(2, 4, P)
        pt_hi = ar.take(2, 4 * P, dt=F16)
        pt_lo = ar.take(2, 4 * P, dt=F16)
        ot_hi = ar.take(2, 4 * P, dt=F16)
        ot_lo = ar.take(2, 4 * P, dt=F16)
        nmax = ar.take(2, 4)
        ebias = ar.take(2, 4)
        escale = ar.take(2, 1)
        esum = ar.take(2, 4)
        rinv = ar.take(2, 4)
        q_mm = [sem(f"q_mm{s}") for s in range(2)]
        q_h = [sem(f"q_h{s}") for s in range(2)]
        q_free = [sem(f"q_free{s}") for s in range(2)]
        rope_sum, rope_h, rope_l, rope_tr, rope_cp = (
            sem(n) for n in ("rope_sum", "rope_h", "rope_l", "rope_tr", "rope_cp"))
        score_mm, smax, pth, ptl, oth, otl, yadd = (
            sem(n) for n in ("score_mm", "smax", "pth", "ptl", "oth", "otl", "yadd"))
        exped = [sem(f"exped{s}") for s in range(2)]
        recip = [sem(f"recip{s}") for s in range(2)]
        normed = [sem(f"normed{s}") for s in range(2)]
        pt_mm = [sem(f"pt_mm{s}") for s in range(2)]
        o_mm = [sem(f"o_mm{s}") for s in range(2)]
        y_mm = [sem(f"y_mm{s}") for s in range(2)]
        NG = 4 * 4

        CHANGE = (("rope", 0), ("step", NG), ("heads", 0), ("step", NG + 1), ("rope_split", 0), ("heads", 4),
                  ("step", NG + 2), ("heads", 8), ("turn", 0), ("heads", 12), ("turn", 1))

        def change_block(now, after, todo):
            for what, i in CHANGE:
                if what in todo:
                    block_ = now if what == "step" else after
                    if block_ is not None:
                        todo[what](block_, i)

        def rope_index(u):
            return 0 if u == 0 else 8 + u

        mr = Room(work_arena, WORK_W)
        cwt = mr.take(T, dt=F16)
        ffn_at = mr.at

        ffn_sems = [[sem(f"ffn_{what}{s}") for s in range(2)] for what in (
            "landed", "whi", "wlo", "selc", "up", "silu", "m1d", "m2d", "hhi", "hlo", "ymm", "yadd")]

        class FFN:
            (landed, whi, wlo, selc, up, silu, m1d, m2d, hhi, hlo, ymm, yadd) = ffn_sems


        def make_ffn(groups, pieces, kind, at, before):
            f = FFN()
            f.groups, f.pieces, f.kind, f.land = groups, pieces, kind, 32 if kind == "moe" else 16
            f.step0 = before.step0 + before.groups * NB if before else 0
            f.piece0 = before.piece0 + before.groups // 2 * before.pieces if before else 0
            f.land0 = before.land0 + before.groups // 2 * before.land if before else 0
            r = Room(work_arena, WORK_W)
            r.at = at
            f.w32 = r.take(2, pieces * 1024)
            f.w_hi = r.take(2, pieces * 1024, dt=F16)
            f.w_lo = r.take(2, pieces * 1024, dt=F16)
            f.sg = r.take(2, BLK)
            if kind == "moe":
                f.sel32 = r.take(2, GW, dt=F16)
                f.sel = r.take(2, GW, dt=F16)
                f.m1 = r.take(2, BLK)
            f.m2 = r.take(2, BLK)
            f.h_hi = r.take(2, GC, BLK, dt=F16)
            f.h_lo = r.take(2, GC, BLK, dt=F16)
            f.end = r.at
            return f

        moe = make_ffn(E * MOE_D // GW, 3, "moe", ffn_at, None)
        gr = Room(work_arena, WORK_W)
        gr.at = moe.end
        gw32 = gr.take(DC, E)
        gw_hi = gr.take(DC, E, dt=F16)
        gw_lo = gr.take(DC, E, dt=F16)
        gmx = gr.take(NT)
        gsub = gr.take(NT, E)
        gexp = gr.take(NT, E)
        gsum = gr.take(NT)
        grc = gr.take(NT)
        gsc = gr.take(NT, E + 2)
        gtop = gr.take(NT, 8)
        grep_ = gr.take(NT, E + 2)
        gcw = gr.take(NT, E)
        ln_xn_moe = gr.take(LS, D)
        gate_done = sem("gate_done")
        gate_in, gate_s, gate_mm, gate_v, gate_t, gate_c = (
            sem(n) for n in ("gate_in", "gate_s", "gate_mm", "gate_v", "gate_t", "gate_c"))

        cm = Room(work_arena, WORK_W)
        cm.at = moe.end
        memT_hi = cm.take(DC, T, dt=F16)
        memT_lo = cm.take(DC, T, dt=F16)
        mem_hi = cm.take(B, D, dt=F16)
        mem_lo = cm.take(B, D, dt=F16)
        mem32 = cm.take(2, DC * P)
        cr = Room(work_arena, moe.end)
        mm8 = cr.take(T, dt=U8)
        mm_f = cr.take(B, S)
        mm_bias = cr.take(B, S, dt=BF16)
        mvalid = cr.take(B)
        mscale = cr.take(B)
        mprob = cr.take(2, P)
        mpt_hi = cr.take(2, P, dt=F16)
        mpt_lo = cr.take(2, P, dt=F16)
        mst = cr.take(2, 4)
        mfac = cr.take(2, 1)
        ln_xn_mem = cr.take(LS, D)
        mem_load = [sem(f"mem_load{s}") for s in range(2)]
        mem_h = [sem(f"mem_h{s}") for s in range(2)]
        mem_l = [sem(f"mem_l{s}") for s in range(2)]
        mem_fac = [sem(f"mem_fac{s}") for s in range(2)]
        mask_in, mask_s = sem("mask_in"), sem("mask_s")
        ms_mm = [sem(f"ms_mm{s}") for s in range(2)]
        ms_v = [sem(f"ms_v{s}") for s in range(2)]
        ms_e = [sem(f"ms_e{s}") for s in range(2)]
        mp_t = [sem(f"mp_t{s}") for s in range(2)]
        mp_h = [sem(f"mp_h{s}") for s in range(2)]
        mp_l = [sem(f"mp_l{s}") for s in range(2)]
        mo_mm = [sem(f"mo_mm{s}") for s in range(2)]
        mo_a = [sem(f"mo_a{s}") for s in range(2)]

        kr_ = Room(work_arena, WORK_W)
        gT = kr_.take(NEXP // P, T)
        pk_at = kr_.at
        mlp = make_ffn(INTER // GW, 3, "mlp", pk_at, moe)
        pkm = make_ffn(NEXP // GW, 2, "pkm", pk_at, mlp)
        rr = Room(work_arena, pk_at)
        ln_xn_pk = rr.take(LS, D)
        kw32 = rr.take(DC * P + 2 * P)
        kw_hi = rr.take(DC * P + 2 * P, dt=F16)
        kw_lo = rr.take(DC * P + 2 * P, dt=F16)
        qT_hi = rr.take(T, dt=F16)
        qT_lo = rr.take(T, dt=F16)
        rx = rr.take(16, NK)
        sx = rr.take(16, 8)
        sy = rr.take(16, 8)
        ixu = rr.take(16, 8, dt=U32)
        iyu = rr.take(16, 8, dt=U32)
        al = rr.take(16, 64)
        al_rep = rr.take(16, 64)
        top = rr.take(16, 8)
        wsum = rr.take(16, 8)
        wtmp = rr.take(16, 8)
        far = rr.take(16)
        ur = Room(work_arena, WORK_W)
        ur.at = mlp.end
        ry = ur.take(16, NK)
        ixf = ur.take(16, 8)
        iyf = ur.take(16, 8)
        cnt = ur.take(16, 8)
        den = ur.take(16)
        ex_ = ur.take(16, KX)
        iota64 = ur.take(NK)
        rank8 = ur.take(8)
        G = ur.take(KX, NK)
        cc = ur.take(1, KX)
        s64 = ur.take(1, NK)
        eq = ur.take(8, NK)
        eqx = ur.take(KX, 8)
        pk_in, pk_s, pk_qmm, pk_qh, pk_ql, pk_rmm, pk_r, pk_act = (
            sem(n) for n in ("pk_in", "pk_s", "pk_qmm", "pk_qh", "pk_ql", "pk_rmm", "pk_r", "pk_act"))
        pk_v, pk_g, pk_t, pk_c = (sem(n) for n in ("pk_v", "pk_g", "pk_t", "pk_c"))
        pk_g0, pk_u = sem("pk_chain"), sem("pk_unit")
        stored = sem("stored")

        ONE = 1
        from_one = [prep_lo, prep_alo, FFN.wlo, FFN.selc, FFN.yadd, ln_lo, q_free, exped, pt_mm, o_mm, y_mm,
                    mem_l, ms_e, mp_l, mo_a,
                    [ctx_l, qkv_l, kr_mul, kvt_cp, ptl, otl, yadd, rope_cp, score_mm, rope_tr, rope_h, rope_l,
                     pk_c, pk_u, pk_t]]

        block = ctx.enter_context(nc.Block())

        @block.sync
        def _(sp):
            sp.dma_start(id32[:, :], ins["ident"]).then_inc(consts_in, 16)
            for dst, src in ((cos_q, "cos_q"), (sin_q, "sin_q"), (cos_k, "cos_k"), (sin_k, "sin_k")):
                sp.dma_start(dst, ins[src]).then_inc(consts_in, 16)
            sp.dma_start(sw32, ins["small_w"]).then_inc(small_in, 16)
            for s in range(LS):
                sp.dma_start(x[:, s * 4:(s + 1) * 4, :], ins["x"][:, s * 4:(s + 1) * 4, :]).then_inc(x_in, 16)
            for several in from_one:
                for semaphore in several:
                    sp.sem_inc(semaphore, ONE)
            for j in range(H // 2):
                for s in range(2):
                    sp.wait_ge(prep_lo[s], ONE + j)
                    sp.dma_start(hw32[:, s, :], ins["head_w"][ds(j * 2 + s, 1), :, :].rearrange(
                        "a p n -> p (a n)")).then_inc(prep_load[s], 16)
            end_phase(sp, "sp")
            sp.dma_start(segi, ins["seg"]).then_inc(seg_in, 16)
            sp.dma_start(iota, ins["iota"]).then_inc(seg_in, 16)
            for j in range(NB):
                sp.wait_ge(ctx_l, ONE + j)
                sp.dma_start(ctx32, ins["ctxT"][:, :, ds(j * BLK, BLK)]).then_inc(ctx_load, 16)
            end_phase(sp, "sp")
            end_phase(sp, "sp")

            def ffn_loads(f, w, sel, also=None):
                for g in range(f.groups):
                    s = g % 2
                    sp.wait_ge(f.wlo[s], ONE + f.piece0 + g // 2 * f.pieces)
                    if sel is not None:
                        sp.wait_ge(f.selc[s], ONE + g // 2)
                    sp.dma_start(f.w32[:, s, :], w[ds(g, 1), :, :].rearrange("a p n -> p (a n)")).then_inc(
                        f.landed[s], 16)
                    if sel is not None:
                        sp.dma_start(f.sel32[:, s, :], sel[ds(g, 1), :, :].rearrange(
                            "a p n -> p (a n)")).then_inc(f.landed[s], 16)
                    if also is not None and 2 <= g < 2 + B:
                        also(g - 2)

            def memory_load(b):
                if b == 0:
                    sp.wait_ge(gate_c, 2 * NB)
                for s in range(2):
                    sp.wait_ge(mem_l[s], ONE + b)
                    src = (ins["ctxT"][:, :, b * P:(b + 1) * P], ins["ctx"][:, b:b + 1, :])[s]
                    dst = mem32[:, s, :].rearrange("p (a b) -> p a b", a=(DC, 1)[s])
                    sp.dma_start(dst, src).then_inc(mem_load[s], 16)

            sp.dma_start(gw32, ins["moe_gate"]).then_inc(gate_in, 16)
            ffn_loads(moe, ins["moe_w"], ins["moe_sel"], memory_load)
            end_phase(sp, "sp")
            sp.dma_start(mm8, ins["mem_mask"].partition_broadcast(P)).then_inc(mask_in, 16)
            end_phase(sp, "sp")
            sp.dma_start(kw32, ins["pk_w"]).then_inc(pk_in, 16)
            sp.dma_start(iota64, ins["iota"][:, 0:NK]).then_inc(pk_in, 16)
            sp.dma_start(rank8, ins["rank8"]).then_inc(pk_in, 16)
            ffn_loads(mlp, ins["mlp_w"], None)
            end_phase(sp, "sp")
            ffn_loads(pkm, ins["pk_e"], None)
            end_phase(sp, "sp")
            for s in range(NB):
                sp.dma_start(out[:, s * 4:(s + 1) * 4, :], x[:, s * 4:(s + 1) * 4, :]).then_inc(stored, 16)
            sp.wait_ge(stored, 16 * NB)

        @block.tensor
        def _(pe):
            pe.wait_ge(small_hi, 3)
            with pe.Fori(0, H // 2) as j:
                for s in range(2):
                    hh, hl = hw_hi[:, s, :], hw_lo[:, s, :]
                    pe.wait_ge(prep_lo[s], ONE + j + 1)
                    pe.wait_ge(prep_alo[s], ONE + j)
                    for c in range(2):
                        cs = slice(c * P, (c + 1) * P)
                        mm3(pe, bank[4 + 2 * s][:, cs], hh[:, cs], hl[:, cs], hh[:, 256:384],
                            hl[:, 256:384], start=True, stop=True)
                    mm3(pe, bank[5 + 2 * s][:, :], hh[:, 384:512], hl[:, 384:512], hh[:, 512:1024],
                        hl[:, 512:1024], start=True, stop=True).then_inc(prep_mm[s], 1)
            ln_tensor(pe, 0, ln_xn_prep)
            end_phase(pe, "pe")
            with pe.Fori(0, NB) as j:
                blk = ds(j * BLK, BLK)
                pe.wait_ge(ctx_l, ONE + j + 1)
                pe.wait_ge(qkv_l, ONE + j * 3)
                for c in range(DC):
                    for i in range(2):
                        cs = slice(i * P, (i + 1) * P)
                        mm3(pe, bank[i][:, :], wdq[0][:, c, cs], wdq[1][:, c, cs], xt_hi[:, c, blk],
                            xt_lo[:, c, blk], start=(c == 0), stop=(c == DC - 1))
                    m = mm3(pe, bank[2][:, :], wkvc[0][:, c, :], wkvc[1][:, c, :], ctx_hi[:, c, :],
                            ctx_lo[:, c, :], start=(c == 0), stop=(c == DC - 1))
                m.then_inc(qkv_mm, 1)
                pe.wait_ge(qkv_l, ONE + j * 3 + 1)
                pe.wait_ge(kr_mul, ONE + j * 2)
                for i in range(2):
                    m = mm3(pe, bank[3 + i][:, :], wkr[0][:, i, :], wkr[1][:, i, :], kv_hi[:, blk],
                            kv_lo[:, blk], start=True, stop=True)
                m.then_inc(kr_mm, 1)
                pe.wait_ge(kvt_cp, ONE + j * 2)
                o = bank[5][:, :].bitcast(F16)
                for i, t in enumerate((kv_hi, kv_lo)):
                    for u in range(TPB):
                        m = pe.transpose(o[:, (i * TPB + u) * P:(i * TPB + u + 1) * P],
                                         t[:, ds(j * BLK + u * P, P)], id16[:, :])
                m.then_inc(kvt_mm, 1)
            end_phase(pe, "pe")
            TR = bank[7][:, :].bitcast(F16)

            def rope_pe(j, u):
                tok = ds(j * BLK + u * P, P)
                for a in range(2):
                    pe.wait_ge(q_free[a], ONE + j * 12 + rope_index(u))
                    cs = slice(a * 512, (a + 1) * 512)
                    o = bank[5 + a][:, :]
                    pe.matmul(o, qc0_hi[:, tok], wqr[0][:, 0, cs], start=True, stop=False)
                    pe.matmul(o, qc0_hi[:, tok], wqr[1][:, 0, cs], start=False, stop=False)
                    pe.matmul(o, qc0_lo[:, tok], wqr[0][:, 0, cs], start=False, stop=False)
                    pe.matmul(o, qc1[:, tok], wqr[0][:, 1, cs], start=False, stop=False)
                    pe.matmul(o, qc1[:, tok], wqr[1][:, 1, cs], start=False, stop=True).then_inc(q_mm[a], 1)

            def rope_turn(j, u, a):
                if a == 0:
                    pe.wait_ge(rope_l, ONE + j * 4 + u + 1)
                pe.wait_ge(rope_cp, ONE + j * 8 + u * 2 + a)
                for h in range(8):
                    m = pe.transpose(TR[:, h * P:(h + 1) * P],
                                     rhl[:, a * 8 + h, :, :].rearrange("p a b -> p (a b)"), id16[:, :])
                m.then_inc(rope_tr, 1)

            def queries_pe(j, h0):
                blk = ds(j * BLK, BLK)
                for h in range(h0, h0 + 4):
                    o = bank[5 + h % 2][:, :]
                    pe.wait_ge(q_free[h % 2], ONE + j * 12 + 1 + h // 2)
                    pe.matmul(o, att_a_hi[:, h, 0:P], qc0_hi[:, blk], start=True, stop=False)
                    pe.matmul(o, att_a_hi[:, h, 0:P], qc0_lo[:, blk], start=False, stop=False)
                    pe.matmul(o, att_a_lo[:, h, 0:P], qc0_hi[:, blk], start=False, stop=False)
                    pe.matmul(o, att_a_hi[:, h, P:2 * P], qc1[:, blk], start=False, stop=False)
                    pe.matmul(o, att_a_lo[:, h, P:2 * P], qc1[:, blk], start=False,
                              stop=True).then_inc(q_mm[h % 2], 1)

            def attend_pe(j, n):
                if n < NG:
                    u, g, k = n // 4, n % 4, n % 2
                    if g in (0, 2):
                        pe.wait_ge(rope_cp, ONE + j * 8 + u * 2 + 1 + g // 2)
                    pe.wait_ge(q_free[0], ONE + j * 12 + 2 * g + 3)
                    pe.wait_ge(q_free[1], ONE + j * 12 + 2 * g + 3)
                    pe.wait_ge(exped[k], ONE + j * 8 + n // 2)
                    sc = bank[k]
                    keys = ds(j * BLK + u * P, P)
                    pe.matmul(sc[:, :].rearrange("p (a b) -> p a b", a=4), idbf[:, :],
                              seg_bias[:, ds(j * 4 + u, 1), :].to_broadcast([P, 4, S]),
                              start=True, stop=False)
                    for i in range(4):
                        h = 4 * g + i
                        o = sc[:, i * P:(i + 1) * P]
                        qs = slice(u * P, (u + 1) * P)
                        pe.matmul(o, qp_hi[:, h, qs], kv_hi[:, keys], start=False, stop=False)
                        pe.matmul(o, qp_hi[:, h, qs], kv_lo[:, keys], start=False, stop=False)
                        pe.matmul(o, qp_lo[:, h, qs], kv_hi[:, keys], start=False, stop=False)
                        pe.matmul(o, qrt[:, u % 2, h, :], kr_hi[:, keys], start=False, stop=False)
                        m = pe.matmul(o, qrt[:, u % 2, h, :], kr_lo[:, keys], start=False,
                                      stop=(i == 3))
                    m.then_inc(score_mm, 1)
                    if g == 0 and u < 3:
                        rope_pe(j, u + 1)
                if 1 <= n <= NG:
                    q, k = n - 1, (n - 1) % 2
                    pe.wait_ge(normed[k], j * 8 + q // 2 + 1)
                    pe.wait_ge(ptl, ONE + j * NG + q)
                    for i in range(4):
                        m = pe.transpose(bank[2][:, i * P:(i + 1) * P], prob[:, k, i, :], id32[:, :])
                    m.then_inc(pt_mm[k], 1)
                if 2 <= n <= NG + 1:
                    q, k = n - 2, (n - 2) % 2
                    u = q // 4
                    pe.wait_ge(ptl, ONE + j * NG + q + 1)
                    pe.wait_ge(otl, ONE + j * NG + q)
                    kh, kl = (t[:, ds(j * 4 + u, 1), :].rearrange("p a b -> p (a b)")
                              for t in (kvt_hi, kvt_lo))
                    mm3(pe, bank[3][:, :], kh, kl, pt_hi[:, k, :], pt_lo[:, k, :],
                        start=True, stop=True).then_inc(o_mm[k], 1)
                if n >= 3:
                    q, k = n - 3, (n - 3) % 2
                    u, g = q // 4, q % 4
                    pe.wait_ge(otl, ONE + j * NG + q + 1)
                    if g == 0:
                        pe.wait_ge(yadd, ONE + j * 4 + u)
                    for i in range(4):
                        h = 4 * g + i
                        m = mm3(pe, bank[4][:, :], ot_hi[:, k, i * P:(i + 1) * P],
                                ot_lo[:, k, i * P:(i + 1) * P], att_vo_hi[:, h, :], att_vo_lo[:, h, :],
                                start=(h == 0), stop=(h == H - 1))
                    m.then_inc(y_mm[k], 1)
                if n < NG - 4 and n % 4 >= 2:
                    rope_turn(j, n // 4 + 1, n % 4 - 2)

            todo = {"rope": rope_pe, "heads": queries_pe, "step": attend_pe,
                    "turn": lambda j, a: rope_turn(j, 0, a)}
            change_block(None, 0, todo)
            with pe.Fori(0, NB - 1) as j:
                for n in range(NG):
                    attend_pe(j, n)
                change_block(j, j + 1, todo)
            for n in range(NG):
                attend_pe(NB - 1, n)
            change_block(NB - 1, None, todo)
            end_phase(pe, "pe")
            ln_tensor(pe, 1, ln_xn_moe)
            pe.wait_ge(gate_s, 2)
            for s in range(LS):
                pe.wait_ge(ln_lo[s], ONE + 2 * LN_IT)
            for t in range(NT):
                for c in range(DC):
                    ts_ = slice(t * P, (t + 1) * P)
                    m = mm3(pe, bank[4][:, t * E:(t + 1) * E], xt_hi[:, c, ts_], xt_lo[:, c, ts_],
                            gw_hi[:, c, :], gw_lo[:, c, :], start=(c == 0), stop=(c == DC - 1))
            m.then_inc(gate_mm, 1)
            pe.wait_ge(gate_done, 1)
            for t in range(NB):
                pe.wait_ge(gate_c, 2 * t)
                for i in range(TPB):
                    m = pe.transpose(bank[5][0:E, i * P:(i + 1) * P], gcw[:, t * TPB + i, :], id32[:, :])
                m.then_inc(gate_t, 1)
            pe.wait_ge(gate_c, 2 * NB)

            def turn_gates(u):
                pe.wait_ge(pk_g, u + 1)
                pe.wait_ge(pk_c, ONE + u)
                for i in range(NEXP // P):
                    m = pe.transpose(bank[4 + i // 4][:, i % 4 * P:(i % 4 + 1) * P],
                                     G[:, 2 * i:2 * i + 2, :].rearrange("p a b -> p (a b)"), id32[:, :])
                m.then_inc(pk_t, 1)

            def ffn_tensor(f):
                def A(j, s):
                    gs, t = (s // NB) % 2, s % NB
                    if t == 0:
                        it = j + 1 if s == 2 * NB else j
                        pe.wait_ge(f.wlo[gs], ONE + f.piece0 + it * f.pieces + f.pieces - 1)
                        if f.kind == "moe":
                            pe.wait_ge(f.selc[gs], ONE + it + 1)
                    k = f.step0 + j * (2 * NB) + s
                    wh, wl = f.w_hi[:, gs, :], f.w_lo[:, gs, :]
                    toks = slice(t * BLK, (t + 1) * BLK)
                    for c in range(GC):
                        pe.wait_ge(f.m2d[c], k)
                        for i in range(f.pieces - 1):
                            for d in range(DC):
                                ws = slice(i * 1024 + d * GW + c * P, i * 1024 + d * GW + (c + 1) * P)
                                m = mm3(pe, bank[2 * i + c][:, :], wh[:, ws], wl[:, ws], xt_hi[:, d, toks],
                                        xt_lo[:, d, toks], start=(d == 0), stop=(d == DC - 1))
                        if f.kind == "moe":
                            m = pe.matmul(bank[4 + c][:, :], f.sel[:, gs, c * P:(c + 1) * P], cwt[:, toks],
                                          start=True, stop=True)
                        m.then_inc(f.up[c], 1)

                def Dn(j, s):
                    gs, t, hp = s // NB, s % NB, s % 2
                    k = f.step0 + j * (2 * NB) + s
                    if t == 0:
                        pe.wait_ge(f.wlo[gs], ONE + f.piece0 + j * f.pieces + f.pieces)
                    for c in range(GC):
                        pe.wait_ge(f.hlo[c], k + 1)
                    wh, wl = f.w_hi[:, gs, :], f.w_lo[:, gs, :]
                    o0 = (f.pieces - 1) * 1024
                    for q in range(TPB):
                        yb = q % 2
                        pe.wait_ge(f.yadd[yb], ONE + k * 2 + q // 2)
                        for c in range(GC):
                            ws = slice(o0 + c * D, o0 + (c + 1) * D)
                            qs = slice(q * P, (q + 1) * P)
                            m = mm3(pe, bank[6 + yb][:, :], f.h_hi[:, hp, c, qs], f.h_lo[:, hp, c, qs],
                                    wh[:, ws], wl[:, ws], start=(c == 0), stop=(c == GC - 1))
                        m.then_inc(f.ymm[yb], 1)

                def body(j, last):
                    for s in range(2 * NB):
                        if not (last and s == 2 * NB - 1):
                            A(j, s + 1)
                        if f.kind == "mlp" and s % 2 == 1:
                            turn_gates(j * NB + s // 2)
                        Dn(j, s)

                A(0, 0)
                n = f.groups // 2
                if n > 1:
                    with pe.Fori(0, n - 1) as j:
                        body(j, False)
                body(n - 1, True)

            ffn_tensor(moe)
            end_phase(pe, "pe")
            ln_tensor(pe, 2, ln_xn_mem)
            for s in range(LS):
                pe.wait_ge(ln_lo[s], ONE + 3 * LN_IT)
            pe.wait_ge(mask_s, 4)

            def mem_scores(b, i, s):
                pe.wait_ge(ms_e[s], ONE + i)
                toks = ds(b * P, P)
                pe.matmul(bank[s][:, 0:P], idbf[:, :], mm_bias[:, ds(b, 1), :].rearrange("p a b -> p (a b)"),
                          start=True, stop=False)
                for c in range(DC):
                    m = mm3(pe, bank[s][:, 0:P], xt_hi[:, c, toks], xt_lo[:, c, toks], memT_hi[:, c, toks],
                            memT_lo[:, c, toks], start=False, stop=(c == DC - 1))
                m.then_inc(ms_mm[s], 1)

            with pe.Fori(0, B // 2) as j:
                for s in range(2):
                    mem_scores(j * 2 + s, j, s)
                for s in range(2):
                    pe.wait_ge(ms_e[s], ONE + j + 1)
                    pe.wait_ge(mp_l[s], ONE + j)
                    pe.transpose(bank[2 + s][:, 0:P], mprob[:, s, :], id32[:, :]).then_inc(mp_t[s], 1)
                for s in range(2):
                    pe.wait_ge(mp_l[s], ONE + j + 1)
                    pe.wait_ge(mo_a[s], ONE + j)
                    mh, ml = (t[:, ds(j * 2 + s, 1), :].rearrange("p a b -> p (a b)") for t in (mem_hi, mem_lo))
                    mm3(pe, bank[4 + s][:, :], mpt_hi[:, s, :], mpt_lo[:, s, :], mh, ml,
                        start=True, stop=True).then_inc(mo_mm[s], 1)
            end_phase(pe, "pe")
            ln_tensor(pe, 3, ln_xn_pk)
            pe.wait_ge(pk_s, 2)
            for s in range(LS):
                pe.wait_ge(ln_lo[s], ONE + 4 * LN_IT)
            for t in range(NB):
                toks = slice(t * BLK, (t + 1) * BLK)
                for c in range(DC):
                    ws = slice(c * P, (c + 1) * P)
                    m = mm3(pe, bank[4 + t][:, :], kw_hi[:, ws], kw_lo[:, ws], xt_hi[:, c, toks],
                            xt_lo[:, c, toks], start=(c == 0), stop=(c == DC - 1))
                m.then_inc(pk_qmm, 1)
            pe.wait_ge(pk_ql, NB)
            for t in range(NT):
                ts_, half = slice(t * P, (t + 1) * P), t // 8
                ks = slice(DC * P + half * P, DC * P + (half + 1) * P)
                m = mm3(pe, bank[t // 4][:, (t % 4) * P:(t % 4 + 1) * P], qT_hi[:, ts_], qT_lo[:, ts_],
                        kw_hi[:, ks], kw_lo[:, ks], start=True, stop=True)
            m.then_inc(pk_rmm, 1)
            pe.wait_ge(pk_r, 4)
            ffn_tensor(mlp)
            end_phase(pe, "pe")
            ffn_tensor(pkm)
            end_phase(pe, "pe")

        @block.scalar
        def _(act):
            act.wait_ge(consts_in, 80)
            act.activation(id16[:, :], id32[:, :], ACT.Copy).then_inc(small_hi, 1)
            act.activation(idbf[:, :], id32[:, :], ACT.Copy).then_inc(small_hi, 1)
            act.wait_ge(small_in, 16)
            act.activation(sw_hi, sw32, ACT.Copy, scale=WS).then_inc(small_hi, 1)
            for j in range(H // 2):
                for s in range(2):
                    act.wait_ge(prep_load[s], j * 16 + 16)
                    act.wait_ge(prep_mm[s], j)
                    act.activation(hw_hi[:, s, :], hw32[:, s, :], ACT.Copy, scale=WS).then_inc(prep_hi[s], 1)
                for s in range(2):
                    hsl = ds(j * 2 + s, 1)
                    act.wait_ge(prep_mm[s], j + 1)
                    act.activation(att_a_hi[:, hsl, :].rearrange("p a b -> p (a b)"),
                                   bank[4 + 2 * s][:, 0:256], ACT.Copy, scale=1 / WS)
                    act.activation(att_vo_hi[:, hsl, :].rearrange("p a b -> p (a b)"),
                                   bank[5 + 2 * s][:, :], ACT.Copy, scale=1 / WS).then_inc(prep_ahi[s], 1)
            ln_scalar(act, 0)
            end_phase(act, "act")
            for j in range(NB):
                blk = ds(j * BLK, BLK)
                act.wait_ge(ctx_load, j * 16 + 16)
                act.wait_ge(qkv_mm, j)
                act.activation(ctx_hi, ctx32, ACT.Copy).then_inc(ctx_h, 1)
                act.wait_ge(qkv_mm, j + 1)
                act.activation(kv_hi[:, blk], bank[2][:, :], ACT.Copy, scale=1 / WS).then_inc(qkv_h, 1)
                act.activation(qc0_hi[:, blk], bank[0][:, :], ACT.Copy, scale=1 / WS).then_inc(qkv_h, 1)
                act.activation(qc1[:, blk], bank[1][:, :], ACT.Copy, scale=1 / WS).then_inc(qkv_h, 1)
                act.wait_ge(kr_sum, j + 1)
                act.activation(kr_hi[:, blk], krot, ACT.Copy).then_inc(kr_h, 1)
                act.wait_ge(kvt_mm, j + 1)
                o = bank[5][:, :].bitcast(F16)
                for i, t in enumerate((kvt_hi, kvt_lo)):
                    act.activation(t[:, ds(j * TPB, TPB), :],
                                   o[:, i * BLK:(i + 1) * BLK].rearrange("p (a b) -> p a b", a=TPB),
                                   ACT.Copy).then_inc(kvt_cp, 1)
            end_phase(act, "act")
            TR = bank[7][:, :].bitcast(F16)

            def rope_act(j, u):
                act.wait_ge(rope_sum, j * 4 + u + 1)
                act.wait_ge(rope_tr, ONE + j * 8 + u * 2)
                act.activation(rhl[:, :, 0, :], rot, ACT.Copy).then_inc(rope_h, 1)

            def rope_copy(j, u, a):
                act.wait_ge(rope_tr, ONE + j * 8 + u * 2 + a + 1)
                act.activation(qrt[:, u % 2, a * 8:(a + 1) * 8, :].rearrange("p a b -> p (a b)"),
                               TR[:, :], ACT.Copy).then_inc(rope_cp, 1)

            def queries_act(j, h0):
                act.wait_ge(score_mm, ONE + j * NG)
                for h in range(h0, h0 + 4):
                    act.wait_ge(q_mm[h % 2], j * 12 + 1 + h // 2 + 1)
                    act.activation(qp_hi[:, h, :], bank[5 + h % 2][:, :], ACT.Copy,
                                   scale=1 / WS).then_inc(q_h[h % 2], 1)

            def attend_act(j, n):
                if n < NG:
                    u, g, k = n // 4, n % 4, n % 2
                    act.wait_ge(pt_mm[k], ONE + j * 8 + n // 2)
                    act.wait_ge(smax, (j * NG + n) * 2 + 2)
                    for i in range(4):
                        m = act.activation(prob[:, k, i, :], bank[k][:, i * P:(i + 1) * P], ACT.Exp,
                                           bias=ebias[:, k, i:i + 1],
                                           scale=escale[:, u % 2, :],
                                           accum_out=esum[:, k, i:i + 1])
                    m.then_inc(exped[k], 1)
                    if g == 0 and u > 0:
                        rope_copy(j, u, 1)
                    if g == 1 and u < 3:
                        rope_act(j, u + 1)
                    if g == 3 and u < 3:
                        rope_copy(j, u + 1, 0)
                if 1 <= n <= NG:
                    q, k = n - 1, (n - 1) % 2
                    act.wait_ge(pt_mm[k], ONE + j * 8 + q // 2 + 1)
                    act.wait_ge(o_mm[k], ONE + j * 8 + q // 2)
                    act.activation(pt_hi[:, k, :], bank[2][:, :], ACT.Copy, scale=PS).then_inc(pth, 1)
                if 2 <= n <= NG + 1:
                    q, k = n - 2, (n - 2) % 2
                    act.wait_ge(o_mm[k], ONE + j * 8 + q // 2 + 1)
                    act.wait_ge(y_mm[k], ONE + j * 8 + q // 2)
                    act.activation(ot_hi[:, k, :], bank[3][:, :], ACT.Copy, scale=OS / PS).then_inc(oth, 1)

            todo = {"rope_split": rope_act, "heads": queries_act, "step": attend_act,
                    "turn": lambda j, a: rope_copy(j, 0, a)}
            change_block(None, 0, todo)
            with act.Fori(0, NB - 1) as j:
                for n in range(NG):
                    attend_act(j, n)
                change_block(j, j + 1, todo)
            for n in range(NG):
                attend_act(NB - 1, n)
            change_block(NB - 1, None, todo)
            end_phase(act, "act")
            ln_scalar(act, 1)
            act.wait_ge(gate_in, 16)
            act.activation(gw_hi, gw32, ACT.Copy, scale=WS).then_inc(gate_s, 1)
            act.wait_ge(gate_v, 2)
            act.activation(gexp, gsub, ACT.Exp, scale=1 / WS).then_inc(gate_v, 1)
            for t in range(NB):
                act.wait_ge(gate_t, t + 1)
                act.activation(cwt[0:E, t * BLK:(t + 1) * BLK], bank[5][0:E, :], ACT.Copy,
                               scale=GS).then_inc(gate_c, 1)

            def ffn_scalar(f, split_first=True):
                def units(k, s):
                    for c in range(GC):
                        act.wait_ge(f.up[c], k + 1)
                        act.activation(f.sg[:, c, :], bank[c][:, :], ACT.Silu,
                                       scale=1 / WS).then_inc(f.silu[c], 1)
                    for c in range(GC):
                        act.wait_ge(f.m2d[c], k + 1)
                        act.activation(f.h_hi[:, s % 2, c, :], f.m2[:, c, :], ACT.Copy).then_inc(f.hhi[c], 1)

                def split(gs, it, piece):
                    if piece == 0:
                        act.wait_ge(f.landed[gs], f.land0 + it * f.land + f.land)
                        if f.kind == "moe":
                            act.activation(f.sel[:, gs, :], f.sel32[:, gs, :], ACT.Copy).then_inc(f.selc[gs], 1)
                    cs = slice(piece * 1024, (piece + 1) * 1024)
                    act.activation(f.w_hi[:, gs, cs], f.w32[:, gs, cs], ACT.Copy,
                                   scale=WS).then_inc(f.whi[gs], 1)

                if split_first is None:
                    for piece in range(f.pieces):
                        split(0, 0, piece)
                    return

                def body(j, last):
                    for s in range(2 * NB):
                        units(f.step0 + j * (2 * NB) + s, s)
                        gs, t = s // NB, s % NB
                        if 1 <= t <= f.pieces and not (last and gs == 1):
                            split(1 - gs, j + gs, t - 1)

                if split_first:
                    for piece in range(f.pieces):
                        split(0, 0, piece)
                n = f.groups // 2
                if n > 1:
                    with act.Fori(0, n - 1) as j:
                        body(j, False)
                body(n - 1, True)

            ffn_scalar(moe)
            end_phase(act, "act")
            ln_scalar(act, 2)
            for j in range(B // 2):
                for s in range(2):
                    act.wait_ge(mp_t[s], j)
                    act.wait_ge(ms_v[s], j * 3 + 2)
                    act.activation(mprob[:, s, :], bank[s][:, 0:P], ACT.Exp, bias=mst[:, s, 1:2],
                                   scale=mscale[:, ds(j * 2 + s, 1)],
                                   accum_out=mst[:, s, 2:3]).then_inc(ms_e[s], 1)
                for s in range(2):
                    act.wait_ge(mp_t[s], j + 1)
                    act.wait_ge(mo_mm[s], j)
                    act.activation(mpt_hi[:, s, :], bank[2 + s][:, 0:P], ACT.Copy).then_inc(mp_h[s], 1)
            end_phase(act, "act")
            ln_scalar(act, 3)
            act.wait_ge(pk_in, 48)
            act.activation(kw_hi, kw32, ACT.Copy, scale=WS).then_inc(pk_s, 1)
            for t in range(NB):
                act.wait_ge(pk_qmm, t + 1)
                act.activation(qT_hi[:, t * BLK:(t + 1) * BLK], bank[4 + t][:, :], ACT.Copy,
                               scale=1 / WS).then_inc(pk_qh, 1)
            act.wait_ge(pk_rmm, 1)
            for a in range(2):
                for i, t in enumerate((rx, ry)):
                    act.activation(t[:, a * 8:(a + 1) * 8, :].rearrange("p a b -> p (a b)"),
                                   bank[2 * i + a][:, :], ACT.Copy, scale=1 / WS).then_inc(pk_r, 1)
            ffn_scalar(mlp, split_first=None)
            act.wait_ge(pk_v, 3)
            act.activation(al, al, ACT.Exp).then_inc(pk_act, 1)
            act.activation(rx, rx, ACT.Exp).then_inc(pk_act, 1)
            act.activation(ry, ry, ACT.Exp).then_inc(pk_act, 1)
            ffn_scalar(mlp, split_first=False)
            end_phase(act, "act")
            ffn_scalar(pkm)
            end_phase(act, "act")

        @block.vector
        def _(dve):
            def lo_of(o, src, scale, hi):
                return dve.scalar_tensor_tensor(out=o, in0=src, scalar=scale, in1=hi, op0=ALU.mult,
                                                op1=ALU.subtract)

            dve.wait_ge(small_hi, 3)
            lo_of(sw_lo, sw32, WS, sw_hi)
            with dve.Fori(0, H // 2) as j:
                for s in range(2):
                    dve.wait_ge(prep_hi[s], j + 1)
                    lo_of(hw_lo[:, s, :], hw32[:, s, :], WS, hw_hi[:, s, :]).then_inc(prep_lo[s], 1)
                for s in range(2):
                    hsl = ds(j * 2 + s, 1)
                    dve.wait_ge(prep_ahi[s], j + 1)
                    lo_of(att_a_lo[:, hsl, :].rearrange("p a b -> p (a b)"), bank[4 + 2 * s][:, 0:256],
                          1 / WS, att_a_hi[:, hsl, :].rearrange("p a b -> p (a b)"))
                    lo_of(att_vo_lo[:, hsl, :].rearrange("p a b -> p (a b)"), bank[5 + 2 * s][:, :],
                          1 / WS, att_vo_hi[:, hsl, :].rearrange("p a b -> p (a b)")).then_inc(prep_alo[s], 1)
            dve.wait_ge(x_in, 16 * LS)
            ln_vector(dve, 0, ln_xn_prep)
            end_phase(dve, "dve")
            dve.wait_ge(seg_in, 32)
            dve.tensor_copy(segf, segi).then_inc(seg_step, 1)
            dve.wait_ge(seg_step, 1)
            dve.tensor_scalar(v1, segf, 0.0, A_SCALE, ALU.is_ge, ALU.mult).then_inc(seg_step, 1)
            dve.tensor_scalar(v2, segf, float(S - 1 + LOOKBACK), None, ALU.is_le).then_inc(seg_step, 1)
            dve.wait_ge(seg_step, 3)
            dve.tensor_tensor(seg_scale, v1, v2, ALU.mult).then_inc(seg_step, 1)
            with dve.Fori(0, B) as b:
                dve.wait_ge(seg_step, b * 4 + 4)
                dve.tensor_scalar(dist[:, 0:S], iota, segf[:, ds(b, 1)], None, ALU.subtract).then_inc(seg_step, 1)
                dve.wait_ge(seg_step, b * 4 + 5)
                dve.tensor_scalar(gt1, dist[:, 0:S], 0.0, NEG, ALU.is_gt, ALU.mult).then_inc(seg_step, 1)
                dve.tensor_scalar(gt2, dist[:, 0:S], float(-LOOKBACK), NEG, ALU.is_lt,
                                  ALU.mult).then_inc(seg_step, 1)
                dve.wait_ge(seg_step, b * 4 + 7)
                dve.tensor_tensor(seg_bias[:, ds(b, 1), :].rearrange("p a b -> p (a b)"), gt1, gt2,
                                  ALU.add).then_inc(seg_step, 1)
            dve.wait_ge(seg_step, 4 * B + 4)
            with dve.Fori(0, NB) as j:
                blk = ds(j * BLK, BLK)
                dve.wait_ge(ctx_h, j + 1)
                dve.tensor_tensor(ctx_lo, ctx32, ctx_hi, ALU.subtract).then_inc(ctx_l, 1)
                dve.wait_ge(qkv_h, j * 3 + 1)
                lo_of(kv_lo[:, blk], bank[2][:, :], 1 / WS, kv_hi[:, blk]).then_inc(qkv_l, 1)
                dve.wait_ge(qkv_h, j * 3 + 2)
                lo_of(qc0_lo[:, blk], bank[0][:, :], 1 / WS, qc0_hi[:, blk]).then_inc(qkv_l, 1)
                dve.wait_ge(qkv_h, j * 3 + 3)
                lo_of(qc1[64:128, blk], bank[1][64:128, :], 1 / WS, qc1[64:128, blk]).then_inc(qkv_l, 1)
                dve.wait_ge(kr_mm, j + 1)
                for i, (t, tab) in enumerate(((kt1, cos_k), (kt2, sin_k))):
                    dve.tensor_tensor(t.rearrange("p (a b) -> p a b", a=TPB),
                                      bank[3 + i][:, :].rearrange("p (a b) -> p a b", a=TPB),
                                      tab.unsqueeze(1).to_broadcast([P, TPB, S]),
                                      ALU.mult).then_inc(kr_mul, 1)
                dve.wait_ge(kr_mul, ONE + j * 2 + 2)
                dve.tensor_tensor(krot, kt1, kt2, ALU.add).then_inc(kr_sum, 1)
                dve.wait_ge(kr_h, j + 1)
                dve.tensor_tensor(kr_lo[:, blk], krot, kr_hi[:, blk], ALU.subtract)
            end_phase(dve, "dve")

            def rope_dve(j, u):
                dve.wait_ge(rope_h, ONE + j * 4 + u)
                dve.wait_ge(rope_l, ONE + j * 4 + u)
                for a in range(2):
                    dve.wait_ge(q_mm[a], j * 12 + rope_index(u) + 1)
                    src = bank[5 + a][:, :].rearrange("p (h r) -> p h r", r=R)
                    hs = slice(8 * a, 8 * a + 8)
                    dve.tensor_tensor(rt1[:, hs, :], src, cos_q.unsqueeze(1).to_broadcast([P, 8, R]), ALU.mult)
                    for c in range(2):
                        oc = slice(32 * c, 32 * c + 32)
                        ic = slice(32 - 32 * c, 64 - 32 * c)
                        m = dve.tensor_tensor(rt2[:, hs, oc], src[:, :, ic],
                                              sin_q[:, oc].unsqueeze(1).to_broadcast([P, 8, 32]), ALU.mult)
                    m.then_inc(q_free[a], 1)

            def queries_dve(j, h0):
                for h in range(h0, h0 + 4):
                    k = h % 2
                    dve.wait_ge(q_h[k], j * 8 + h // 2 + 1)
                    lo_of(qp_lo[:, h, :], bank[5 + k][:, :], 1 / WS, qp_hi[:, h, :]).then_inc(q_free[k], 1)

            def attend_dve(j, n):
                if n < NG:
                    u, g, k = n // 4, n % 4, n % 2
                    dve.wait_ge(score_mm, ONE + j * NG + n + 1)
                    if g == 0:
                        dve.tensor_copy(escale[:, u % 2, :], seg_scale[:, ds(j * 4 + u, 1)])
                    dve.tensor_reduce(nmax[:, k, :], bank[k][:, :].rearrange("p (a b) -> p a b", a=4),
                                      AX.X, ALU.max, negate=True).then_inc(smax, 1)
                    dve.wait_ge(smax, (j * NG + n) * 2 + 1)
                    dve.tensor_scalar(ebias[:, k, :], nmax[:, k, :], seg_scale[:, ds(j * 4 + u, 1)],
                                      None, ALU.mult).then_inc(smax, 1)
                    if g == 0 and u < 3:
                        rope_dve(j, u + 1)
                    dve.wait_ge(exped[k], ONE + j * 8 + n // 2 + 1)
                    dve.reciprocal(rinv[:, k, :], esum[:, k, :]).then_inc(recip[k], 1)
                if 1 <= n <= NG:
                    q, k = n - 1, (n - 1) % 2
                    dve.wait_ge(pth, j * NG + q + 1)
                    lo_of(pt_lo[:, k, :], bank[2][:, :], PS, pt_hi[:, k, :]).then_inc(ptl, 1)
                if 2 <= n <= NG + 1:
                    q, k = n - 2, (n - 2) % 2
                    dve.wait_ge(oth, j * NG + q + 1)
                    lo_of(ot_lo[:, k, :], bank[3][:, :], OS / PS, ot_hi[:, k, :]).then_inc(otl, 1)
                if n >= 3 and (n - 3) % 4 == 3:
                    q = n - 3
                    u = q // 4
                    xv = x[:, ds(j * 4 + u, 1), :].rearrange("p a b -> p (a b)")
                    dve.wait_ge(y_mm[1], ONE + j * 8 + q // 2 + 1)
                    dve.scalar_tensor_tensor(out=xv, in0=bank[4][:, :], scalar=1 / (OS * WS), in1=xv,
                                             op0=ALU.mult, op1=ALU.add).then_inc(yadd, 1)

            todo = {"rope": rope_dve, "heads": queries_dve, "step": attend_dve}
            change_block(None, 0, todo)
            with dve.Fori(0, NB - 1) as j:
                for n in range(NG):
                    attend_dve(j, n)
                change_block(j, j + 1, todo)
            for n in range(NG):
                attend_dve(NB - 1, n)
            change_block(NB - 1, None, todo)
            end_phase(dve, "dve")
            ln_vector(dve, 1, ln_xn_moe)
            dve.wait_ge(gate_s, 1)
            lo_of(gw_lo, gw32, WS, gw_hi).then_inc(gate_s, 1)
            dve.memset(gsc, 2.0)
            dve.memset(cwt, 0.0)
            lg = bank[4][:, 0:NT * E].rearrange("p (a b) -> p a b", b=E)
            dve.wait_ge(gate_mm, 1)
            dve.tensor_reduce(gmx, lg, AX.X, ALU.max).then_inc(gate_v, 1)
            dve.wait_ge(gate_v, 1)
            dve.tensor_tensor(gsub, lg, gmx.unsqueeze(2).to_broadcast([P, NT, E]), ALU.subtract).then_inc(gate_v, 1)
            dve.wait_ge(gate_v, 3)
            dve.tensor_reduce(gsum, gexp, AX.X, ALU.add).then_inc(gate_v, 1)
            dve.wait_ge(gate_v, 4)
            dve.reciprocal(grc, gsum).then_inc(gate_v, 1)
            dve.wait_ge(gate_v, 5)
            dve.tensor_tensor(gsc[:, :, 0:E], gexp, grc.unsqueeze(2).to_broadcast([P, NT, E]),
                              ALU.mult).then_inc(gate_v, 1)
            dve.wait_ge(gate_v, 6)
            for t in range(NT):
                m = dve.max(gtop[:, t, :], gsc[:, t, :])
            m.then_inc(gate_v, 1)
            dve.wait_ge(gate_v, 7)
            for t in range(NT):
                m = dve.match_replace(grep_[:, t, :], gtop[:, t, :], gsc[:, t, :], 0.0)
            m.then_inc(gate_v, 1)
            dve.wait_ge(gate_v, 8)
            dve.tensor_tensor(gcw, gsc[:, :, 0:E], grep_[:, :, 0:E], ALU.subtract).then_inc(gate_done, 1)
            for t in range(NB):
                dve.wait_ge(gate_c, 2 * t + 1)
                lo_of(cwt[32:32 + E, t * BLK:(t + 1) * BLK], bank[5][0:E, :], GS,
                      cwt[0:E, t * BLK:(t + 1) * BLK]).then_inc(gate_c, 1)

            def build_gates(u, part):
                u1 = ds(u, 1)
                if part == 0:
                    dve.wait_ge(pk_u, ONE + u * 6)
                    dve.tensor_tensor(eq, iota64.unsqueeze(1).to_broadcast([P, 8, NK]),
                                      iyf[:, u1, :].rearrange("p a b -> p b a").to_broadcast([P, 8, NK]),
                                      ALU.is_equal)
                    dve.tensor_tensor(eqx, iota64[:, 0:KX].unsqueeze(2).to_broadcast([P, KX, 8]),
                                      ixf[:, u1, :].to_broadcast([P, KX, 8]), ALU.is_equal).then_inc(pk_u, 1)
                    dve.wait_ge(pk_u, ONE + u * 6 + 1)
                    dve.tensor_tensor(eq, eq, rank8.unsqueeze(2).to_broadcast([P, 8, NK]), ALU.mult)
                    dve.tensor_tensor(eqx, eqx, cnt[:, u1, :].to_broadcast([P, KX, 8]), ALU.mult).then_inc(pk_u, 1)
                    dve.wait_ge(pk_u, ONE + u * 6 + 2)
                    dve.tensor_reduce(s64[:, 0, :], eq.rearrange("p a b -> p b a"), AX.X, ALU.add)
                    dve.tensor_reduce(cc[:, 0, :], eqx, AX.X, ALU.add).then_inc(pk_u, 1)
                    dve.wait_ge(pk_u, ONE + u * 6 + 3)
                    dve.wait_ge(pk_t, ONE + u)
                    dve.tensor_tensor(G, s64[:, 0:1, :].to_broadcast([P, KX, NK]),
                                      cc[:, 0, :].unsqueeze(2).to_broadcast([P, KX, NK]), ALU.add).then_inc(pk_u, 1)
                    return
                dve.wait_ge(pk_u, ONE + u * 6 + 4)
                dve.scalar_tensor_tensor(out=G, in0=G, scalar=8.0, in1=ry[:, u1, :].to_broadcast([P, KX, NK]),
                                         op0=ALU.is_gt, op1=ALU.mult).then_inc(pk_u, 1)
                dve.wait_ge(pk_u, ONE + u * 6 + 5)
                dve.tensor_tensor(G, G, ex_[:, u1, :].rearrange("p a b -> p b a").to_broadcast([P, KX, NK]),
                                  ALU.mult).then_inc(pk_u, 1)
                dve.wait_ge(pk_u, ONE + u * 6 + 6)
                dve.tensor_tensor(G[:, KX - 1, NK - 1:NK], G[:, KX - 1, NK - 1:NK], den[:, u1],
                                  ALU.add).then_inc(pk_g, 1)

            def keep_gates(u, token0):
                dve.wait_ge(pk_t, ONE + u + 1)
                for a in range(2):
                    m = dve.tensor_scalar(gT[:, a * 4:a * 4 + 4, ds(token0, P, 2)],
                                          bank[4 + a][:, :].rearrange("p (a b) -> p a b", a=4), WS, None, ALU.mult)
                m.then_inc(pk_c, 1)

            def split_memory(b):
                for s in range(2):
                    dst_hi = (memT_hi[:, :, ds(b * P, P)], mem_hi[:, ds(b, 1), :])[s]
                    dst_lo = (memT_lo[:, :, ds(b * P, P)], mem_lo[:, ds(b, 1), :])[s]
                    src = mem32[:, s, :].rearrange("p (a b) -> p a b", a=(DC, 1)[s])
                    dve.wait_ge(mem_load[s], b * 16 + 16)
                    dve.tensor_scalar(dst_hi, src, 1.0, None, ALU.mult).then_inc(mem_h[s], 1)
                    dve.wait_ge(mem_h[s], b + 1)
                    dve.tensor_tensor(dst_lo, src, dst_hi, ALU.subtract).then_inc(mem_l[s], 1)

            def ffn_vector(f, split_first=True):
                def split(gs, it, piece):
                    dve.wait_ge(f.whi[gs], f.piece0 + it * f.pieces + piece + 1)
                    cs = slice(piece * 1024, (piece + 1) * 1024)
                    lo_of(f.w_lo[:, gs, cs], f.w32[:, gs, cs], WS, f.w_hi[:, gs, cs]).then_inc(f.wlo[gs], 1)

                if split_first is None:
                    for piece in range(f.pieces):
                        split(0, 0, piece)
                    return

                def units(j, s):
                    k = f.step0 + j * (2 * NB) + s
                    for c in range(GC):
                        dve.wait_ge(f.silu[c], k + 1)
                        dve.wait_ge(f.hlo[c], k)
                        if f.kind == "moe":
                            dve.scalar_tensor_tensor(out=f.m1[:, c, :], in0=f.sg[:, c, :], scalar=1 / GS,
                                                     in1=bank[2 + c][:, :], op0=ALU.mult,
                                                     op1=ALU.mult).then_inc(f.m1d[c], 1)
                            dve.wait_ge(f.m1d[c], k + 1)
                            dve.tensor_tensor(f.m2[:, c, :], f.m1[:, c, :], bank[4 + c][:, :],
                                              ALU.mult).then_inc(f.m2d[c], 1)
                        elif f.kind == "mlp":
                            dve.tensor_tensor(f.m2[:, c, :], f.sg[:, c, :], bank[2 + c][:, :],
                                              ALU.mult).then_inc(f.m2d[c], 1)
                        else:
                            g = gT[:, ds((j * 2 + s // NB) * GC + c, 1), (s % NB) * BLK:(s % NB + 1) * BLK]
                            dve.tensor_tensor(f.m2[:, c, :], f.sg[:, c, :], g.rearrange("p a b -> p (a b)"),
                                              ALU.mult).then_inc(f.m2d[c], 1)

                def adds(j, s):
                    k = f.step0 + j * (2 * NB) + s
                    for q in range(TPB):
                        yb = q % 2
                        xv = x[:, (s % NB) * TPB + q, :]
                        dve.wait_ge(f.ymm[yb], k * 2 + q // 2 + 1)
                        dve.scalar_tensor_tensor(out=xv, in0=bank[6 + yb][:, :], scalar=1 / (WS * WS), in1=xv,
                                                 op0=ALU.mult, op1=ALU.add).then_inc(f.yadd[yb], 1)

                def body(j, last, with_memory=False):
                    for s in range(2 * NB):
                        if f.kind == "mlp":
                            build_gates(j * NB + s // 2, s % 2)
                        if not (last and s == 2 * NB - 1):
                            units(j, s + 1)
                        adds(j, s)
                        if f.kind == "mlp" and s % 2 == 1:
                            h = s // 2
                            keep_gates(j * NB + h, j * (2 * 256) + h // 2 * 256 + h % 2)
                        gs, t = (s + 1) // NB % 2, (s + 1) % NB
                        it = j + 1 if s + 1 == 2 * NB else j
                        if 1 <= t <= f.pieces and not (last and gs == 1):
                            split(1 - gs, it + gs, t - 1)
                        if with_memory and s % NB == NB - 1:
                            split_memory(j * 2 + s // NB)

                if split_first:
                    for piece in range(f.pieces):
                        split(0, 0, piece)
                units(0, 0)
                n = f.groups // 2
                if f.kind == "moe":
                    with dve.Fori(0, B // 2) as j:
                        body(j, False, with_memory=True)
                with dve.Fori(B // 2 if f.kind == "moe" else 0, n - 1) as j:
                    body(j, False)
                body(n - 1, True)

            ffn_vector(moe)
            end_phase(dve, "dve")
            dve.wait_ge(mask_in, 16)
            dve.tensor_copy(mm_f.rearrange("p a b -> p (a b)"), mm8).then_inc(mask_s, 1)
            dve.wait_ge(mask_s, 1)
            dve.tensor_scalar(mm_bias, mm_f, -NEG, NEG, ALU.mult, ALU.add).then_inc(mask_s, 1)
            dve.tensor_reduce(mvalid, mm_f, AX.X, ALU.max).then_inc(mask_s, 1)
            dve.wait_ge(mask_s, 3)
            dve.tensor_scalar(mscale, mvalid, M_SCALE, None, ALU.mult).then_inc(mask_s, 1)
            ln_vector(dve, 2, ln_xn_mem)
            with dve.Fori(0, B // 2) as j:
                for s in range(2):
                    b1 = ds(j * 2 + s, 1)
                    dve.wait_ge(ms_mm[s], j + 1)
                    dve.tensor_reduce(mst[:, s, 0:1], bank[s][:, 0:P], AX.X, ALU.max,
                                      negate=True).then_inc(ms_v[s], 1)
                    dve.wait_ge(ms_v[s], j * 3 + 1)
                    dve.tensor_scalar(mst[:, s, 1:2], mst[:, s, 0:1], mscale[:, b1], None,
                                      ALU.mult).then_inc(ms_v[s], 1)
                for s in range(2):
                    b1 = ds(j * 2 + s, 1)
                    dve.wait_ge(ms_e[s], ONE + j + 1)
                    dve.reciprocal(mst[:, s, 3:4], mst[:, s, 2:3]).then_inc(ms_v[s], 1)
                for s in range(2):
                    dve.wait_ge(mp_h[s], j + 1)
                    dve.tensor_tensor(mpt_lo[:, s, :], bank[2 + s][:, 0:P], mpt_hi[:, s, :],
                                      ALU.subtract).then_inc(mp_l[s], 1)
                for s in range(2):
                    b1 = ds(j * 2 + s, 1)
                    xv = x[:, b1, :].rearrange("p a b -> p (a b)")
                    dve.wait_ge(ms_v[s], j * 3 + 3)
                    dve.tensor_tensor(mfac[:, s, :], mst[:, s, 3:4], mvalid[:, b1], ALU.mult).then_inc(mem_fac[s], 1)
                    dve.wait_ge(mem_fac[s], j + 1)
                    dve.wait_ge(mo_mm[s], j + 1)
                    dve.scalar_tensor_tensor(out=xv, in0=bank[4 + s][:, :], scalar=mfac[:, s, :], in1=xv,
                                             op0=ALU.mult, op1=ALU.add).then_inc(mo_a[s], 1)
            end_phase(dve, "dve")
            ln_vector(dve, 3, ln_xn_pk)
            dve.wait_ge(pk_s, 1)
            lo_of(kw_lo, kw32, WS, kw_hi).then_inc(pk_s, 1)
            for t in range(NB):
                dve.wait_ge(pk_qh, t + 1)
                ts_ = slice(t * BLK, (t + 1) * BLK)
                lo_of(qT_lo[:, ts_], bank[4 + t][:, :], 1 / WS, qT_hi[:, ts_]).then_inc(pk_ql, 1)
            ffn_vector(mlp, split_first=None)
            dve.wait_ge(pk_r, 4)
            for u in range(NT):
                dve.max(sx[:, u, :], rx[:, u, :])
                m = dve.max(sy[:, u, :], ry[:, u, :])
            m.then_inc(pk_v, 1)
            dve.wait_ge(pk_v, 1)
            for u in range(NT):
                dve.max_index(ixu[:, u, :], sx[:, u, :], rx[:, u, :])
                dve.max_index(iyu[:, u, :], sy[:, u, :], ry[:, u, :])
                m = dve.tensor_tensor(al[:, u, :].rearrange("p (a b) -> p a b", a=8),
                                      sx[:, u, :].unsqueeze(2).to_broadcast([P, 8, 8]),
                                      sy[:, u, :].unsqueeze(1).to_broadcast([P, 8, 8]), ALU.add)
            m.then_inc(pk_v, 1)
            step = [0]

            def after(m):
                step[0] += 1
                m.then_inc(pk_g0, 1)
                dve.wait_ge(pk_g0, step[0])

            dve.wait_ge(pk_v, 2)
            dve.tensor_copy(ixf, ixu)
            for u in range(NT):
                m = dve.max(top[:, u, :], al[:, u, :])
            after(dve.tensor_copy(iyf, iyu))
            for u in range(NT):
                m = dve.match_replace(al_rep[:, u, :], top[:, u, :], al[:, u, :], -3e38)
            after(m)
            after(dve.tensor_tensor(al_rep, al_rep, al, ALU.not_equal))
            dve.tensor_tensor(al, al, top[:, :, 0:1].to_broadcast([P, NT, 64]), ALU.subtract)
            dve.tensor_tensor(rx, rx, sx[:, :, 0:1].to_broadcast([P, NT, NK]), ALU.subtract)
            dve.tensor_tensor(ry, ry, sy[:, :, 0:1].to_broadcast([P, NT, NK]), ALU.subtract).then_inc(pk_v, 1)
            dve.wait_ge(pk_act, 3)
            after(dve.tensor_tensor(al, al, al_rep, ALU.mult))
            dve.tensor_reduce(den, al, AX.X, ALU.add)
            dve.tensor_reduce(wsum.rearrange("p a b -> p (a b)"), al.rearrange("p u (a b) -> p (u a) b", b=8),
                              AX.X, ALU.add)
            after(dve.tensor_reduce(cnt.rearrange("p a b -> p (a b)"),
                                    al_rep.rearrange("p u (a b) -> p (u a) b", b=8), AX.X, ALU.add))
            dve.tensor_scalar(wtmp, ixf, float(KX), None, ALU.is_ge)
            after(dve.reciprocal(far, den))
            dve.tensor_tensor(ex_, rx[:, :, 0:KX], far.unsqueeze(2).to_broadcast([P, NT, KX]), ALU.mult)
            after(dve.tensor_tensor(wtmp, wtmp, wsum, ALU.mult))
            after(dve.tensor_reduce(den, wtmp, AX.X, ALU.add))
            after(dve.tensor_tensor(den, den, far, ALU.mult))
            ffn_vector(mlp, split_first=False)
            end_phase(dve, "dve")
            ffn_vector(pkm)
            end_phase(dve, "dve")

        @block.gpsimd
        def _(pool):
            pool.memset(neg_half[:, :, :], -0.5).then_inc(half_set, 1)
            pool.wait_ge(half_set, 1)
            ln_gpsimd(pool, 0)
            end_phase(pool, "pool")
            end_phase(pool, "pool")

            def rope_pool(j, u):
                for a in range(2):
                    pool.wait_ge(q_free[a], ONE + j * 12 + rope_index(u) + 1)
                pool.tensor_tensor(rot, rt1, rt2, ALU.add).then_inc(rope_sum, 1)
                pool.wait_ge(rope_sum, j * 4 + u + 1)
                pool.wait_ge(rope_h, ONE + j * 4 + u + 1)
                pool.tensor_tensor(rhl[:, :, 1, :], rot, rhl[:, :, 0, :], ALU.subtract).then_inc(rope_l, 1)

            def attend_pool(j):
                for n in range(NG):
                    u, g, k = n // 4, n % 4, n % 2
                    pool.wait_ge(recip[k], j * 8 + n // 2 + 1)
                    pool.tensor_tensor(prob[:, k, :, :], prob[:, k, :, :],
                                       rinv[:, k, :].unsqueeze(2).to_broadcast([P, 4, P]),
                                       ALU.mult).then_inc(normed[k], 1)
                    if g == 1 and u < 3:
                        rope_pool(j, u + 1)

            rope_pool(0, 0)
            with pool.Fori(0, NB - 1) as j:
                attend_pool(j)
                rope_pool(j + 1, 0)
            attend_pool(NB - 1)
            end_phase(pool, "pool")
            ln_gpsimd(pool, 1)

            def ffn_gpsimd(f):
                def body(j, last):
                    for s in range(2 * NB):
                        k = f.step0 + j * (2 * NB) + s
                        for c in range(GC):
                            pool.wait_ge(f.hhi[c], k + 1)
                            pool.tensor_tensor(f.h_lo[:, s % 2, c, :], f.m2[:, c, :], f.h_hi[:, s % 2, c, :],
                                               ALU.subtract).then_inc(f.hlo[c], 1)

                n = f.groups // 2
                if n > 1:
                    with pool.Fori(0, n - 1) as j:
                        body(j, False)
                body(n - 1, True)

            ffn_gpsimd(moe)
            end_phase(pool, "pool")
            ln_gpsimd(pool, 2)
            end_phase(pool, "pool")
            ln_gpsimd(pool, 3)
            ffn_gpsimd(mlp)
            end_phase(pool, "pool")
            ffn_gpsimd(pkm)
            end_phase(pool, "pool")


def shape_constants():
    half = R // 2
    inv = (1.0 / 10000.0 ** (np.arange(half, dtype=np.float32) / np.float32(half))).astype(np.float32)
    ang = np.arange(S, dtype=np.float32)[:, None] * inv
    cos, sin = np.cos(ang).astype(np.float32), np.sin(ang).astype(np.float32)
    cos2, sin2 = np.concatenate([cos, cos], 1) / WS, np.concatenate([-sin, sin], 1) / WS
    sel = np.zeros((P, E * MOE_D), np.float16)
    for e in range(E):
        sel[e, e * MOE_D:(e + 1) * MOE_D] = 1.0
        sel[32 + e, e * MOE_D:(e + 1) * MOE_D] = 1.0
    return {
        "ident": np.eye(P, dtype=np.float32),
        "iota": np.tile(np.arange(S, dtype=np.float32), (P, 1)),
        "rank8": np.tile(8.0 - np.arange(8, dtype=np.float32), (P, 1)),
        "cos_q": cos2.astype(np.float32), "sin_q": sin2.astype(np.float32),
        "cos_k": np.tile(cos2.T, (2, 1)).astype(np.float32), "sin_k": np.tile(sin2.T, (2, 1)).astype(np.float32),
        "moe_sel": np.ascontiguousarray(sel.reshape(P, -1, GW).transpose(1, 0, 2)),
    }


def by_group(gate_t, up_t, down):
    def wide(w):
        return w.reshape(DC, P, -1, GW).transpose(2, 1, 0, 3).reshape(-1, P, DC * GW)
    parts = [wide(gate_t)] + ([wide(up_t)] if up_t is not None else [])
    parts.append(down.reshape(-1, GC, P, D).transpose(0, 2, 1, 3).reshape(-1, P, GC * D))
    return np.concatenate(parts, axis=2)


def lay_out(i):
    i = {k: np.asarray(v) for k, v in i.items()}
    a = dict(shape_constants())
    a["x"] = i["x"].transpose(1, 0, 2)
    a["ctx"] = i["ctx_2048"].transpose(1, 0, 2)
    a["ctxT"] = i["ctx_2048"].reshape(T, DC, P).transpose(2, 1, 0)
    a["seg"] = i["itok_BxS_0_1023"].T
    a["mem_mask"] = i["mask_BxS2_bk0"].reshape(T)
    dq = i["L0_xattn_W_dq"].reshape(DC, P, QC).transpose(1, 0, 2)
    dq = np.concatenate([dq, dq[:, :, P:]], axis=2).reshape(P, -1)
    kvc = i["L0_xattn_W_kvc"].reshape(DC, P, KVC).transpose(1, 0, 2).reshape(P, -1)
    kr = i["L0_xattn_W_kr"]
    sw = np.concatenate([kr[:, R // 2:], kr[:, :R // 2]], axis=1)
    qr = i["L0_xattn_W_qr"]
    a["small_w"] = np.concatenate([dq, kvc, kr, kr, sw, sw, qr[:P], np.concatenate([qr[P:], qr[P:]], axis=0)],
                                  axis=1)
    uq = i["L0_xattn_W_uq"].reshape(QC, H, HD).transpose(1, 2, 0)
    uk = i["L0_xattn_W_uk"].reshape(KVC, H, HD).transpose(1, 2, 0)
    uv = i["L0_xattn_W_uv"].reshape(KVC, H, HD).transpose(1, 2, 0)
    wo = i["L0_xattn_W_o"].reshape(H, HD, D)
    a["head_w"] = np.concatenate([uq, uq[:, :, P:], uk, uv, wo], axis=2)
    a["moe_gate"] = i["L0_ffn_gate_w"].reshape(E, DC, P).transpose(2, 1, 0).reshape(P, DC * E)
    a["moe_w"] = by_group(i["L0_ffn_w_gate"].reshape(-1, D).T, i["L0_ffn_w_up"].reshape(-1, D).T,
                          i["L0_ffn_w_down"].transpose(0, 2, 1).reshape(-1, D))
    a["mlp_w"] = by_group(i["L1_ffn_gate_w"], i["L1_ffn_up_w"], i["L1_ffn_down_w"])
    a["pk_e"] = by_group(i["L1_ffn_down_embed"].T, None, i["L1_ffn_up_embed"])
    wq = i["L1_ffn_W_q"].reshape(DC, P, P).transpose(1, 0, 2).reshape(P, -1)
    keys = np.zeros((P, 2, 2, NK), np.float32)
    for t in range(2):
        for h in range(2):
            keys[h * NK:(h + 1) * NK, t, h] = i["L1_ffn_keys"][t]
    a["pk_w"] = np.concatenate([wq, keys.reshape(P, -1)], axis=1)
    return {k: np.ascontiguousarray(v) for k, v in a.items()}


def kernel(**inputs):
    import concourse.bacc as bacc
    from concourse.bass_utils import run_bass_kernel_spmd

    nc = bacc.Bacc("TRN2", target_bir_lowering=False, num_devices=1)
    arrays, aps = {}, {}
    for name, a in lay_out(inputs).items():
        arrays[f"in_{name}"] = a
        aps[name] = nc.dram_tensor(f"in_{name}", a.shape, mybir.dt.from_np(a.dtype), kind="ExternalInput").ap()
    out = nc.dram_tensor("out", (P, NT, D), F32, kind="ExternalOutput").ap()
    build(nc, aps, out)
    r = run_bass_kernel_spmd(nc, [arrays], core_ids=[0])
    return r.results[0]["out"].transpose(1, 0, 2).reshape(B, S, D)
```

```python
from contextlib import ExitStack

import numpy as np

import concourse.bass as bass
import concourse.mybir as mybir

F32, F16, BF16 = mybir.dt.float32, mybir.dt.float16, mybir.dt.bfloat16
I32, U32, U8 = mybir.dt.int32, mybir.dt.uint32, mybir.dt.uint8
ALU = mybir.AluOpType
ACT = mybir.ActivationFunctionType
AX = mybir.AxisListType
ds = bass.ds

P = 128
B, S, D = 16, 128, 512
T = B * S
NT = T // P
DC = D // P
BLK = 512
NB = T // BLK
TPB = BLK // P
H, HD, KVC, QC, R = 16, 128, 128, 192, 64
LOOKBACK = 8
NEG = -1e30
E, TOPE, MOE_D = 16, 6, 352
INTER, NEXP, NK, TOPK = 2048, 1024, 64, 8
KX = NEXP // NK
EPS = 1e-5
WS = 64.0
OS = 8.0
GS = 16.0
PS = 64.0
A_SCALE = 1.0 / float(np.sqrt(np.float32(HD + R)))
M_SCALE = 1.0 / float(np.sqrt(np.float32(D)))
GC = 2
GW = GC * P


def size_of(dt):
    return {F32: 4, I32: 4, U32: 4, F16: 2, BF16: 2, U8: 1}[dt]


def build(nc, ins, out):
    with ExitStack() as ctx:
        def sb(name, shape, dt=F32):
            return ctx.enter_context(nc.sbuf_tensor(name, shape, dt))

        def sem(name):
            return ctx.enter_context(nc.semaphore(name))

        def carve(arena, at, dims, dt=F32):
            n = int(np.prod(dims)) * size_of(dt) // 4
            v = arena[:, at:at + n]
            if dt != F32:
                v = v.bitcast(dt)
            if len(dims) == 2:
                v = v.rearrange("p (a b) -> p a b", a=dims[0])
            elif len(dims) == 3:
                v = v.rearrange("p (a b c) -> p a b c", a=dims[0], b=dims[1])
            return v, at + n

        class Room:
            def __init__(self, arena, words):
                self.arena, self.words, self.at = arena, words, 0

            def take(self, *dims, dt=F32):
                v, self.at = carve(self.arena, self.at, dims, dt)
                assert self.at <= self.words, (self.at, self.words)
                return v

        x = sb("x", [P, NT, D])
        XT_W, WORK_W = 8192, 36400
        xt_arena = sb("xt_arena", [P, XT_W])
        work_arena = sb("work_arena", [P, WORK_W])
        id32 = sb("id32", [P, P])
        id16 = sb("id16", [P, P], F16)
        idbf = sb("idbf", [P, P], BF16)
        bank = [ctx.enter_context(nc.psum_tensor(f"bank{i}", [P, 512], F32)) for i in range(8)]

        xt_room = Room(xt_arena, XT_W)
        xt_hi = xt_room.take(DC, T, dt=F16)
        xt_lo = xt_room.take(DC, T, dt=F16)
        q_room = Room(xt_arena, XT_W)
        qp_hi = q_room.take(H, BLK, dt=F16)
        qp_lo = q_room.take(H, BLK, dt=F16)

        phase_done = sem("phase_done")
        phase = {}

        def end_phase(eng, name):
            n = phase.get(name, 0) + 1
            phase[name] = n
            eng.drain().then_inc(phase_done, 1)
            eng.wait_ge(phase_done, 5 * n)

        LS = 4
        ln_st = sb("ln_st", [P, LS, 6])
        ln_mv = sb("ln_mv", [P, LS, 2])
        ln_ve = sb("ln_ve", [P, LS, 1])
        ln_rs = sb("ln_rs", [P, LS, 1])
        neg_half = sb("neg_half", [P, LS, 1])
        ln_var, ln_rstd, half_set = sem("ln_var"), sem("ln_rstd"), sem("half_set")

        ln_stat, ln_norm, ln_turned, ln_hi, ln_lo = (
            [sem(f"ln_{what}{s}") for s in range(LS)] for what in ("stat", "norm", "turned", "hi", "lo"))
        LN_IT = NT // LS

        def tile_cols(t, j, s):
            return t[:, :, ds((j * LS + s) * P, P)]

        def ln_stats(dve, k, j):
            for s in range(LS):
                dve.bn_stats(ln_st[:, s, :], x[:, j * LS + s, :]).then_inc(ln_stat[s], 1)
            for s in range(LS):
                dve.wait_ge(ln_stat[s], k * 2 + 1)
                dve.bn_aggr(ln_mv[:, s, :], ln_st[:, s, :]).then_inc(ln_stat[s], 1)
            for s in range(LS):
                dve.wait_ge(ln_stat[s], k * 2 + 2)
            dve.tensor_scalar(ln_ve[:, :, :], ln_mv[:, :, 1:2], EPS, None, ALU.add).then_inc(ln_var, 1)

        def ln_normalize(dve, k, j, xn):
            dve.wait_ge(ln_rstd, k + 1)
            for s in range(LS):
                dve.wait_ge(ln_turned[s], k)
                dve.tensor_scalar(xn[:, s, :], x[:, j * LS + s, :], ln_mv[:, s, 0:1], ln_rs[:, s, :],
                                  ALU.subtract, ALU.mult).then_inc(ln_norm[s], 1)

        def ln_low(dve, k, j):
            for s in range(LS):
                dve.wait_ge(ln_hi[s], k + 1)
                dve.tensor_tensor(tile_cols(xt_lo, j, s), bank[s][:, :].rearrange("p (a b) -> p a b", a=DC),
                                  tile_cols(xt_hi, j, s), ALU.subtract).then_inc(ln_lo[s], 1)

        def ln_vector(dve, n, xn, meanwhile):
            ln_stats(dve, n * LN_IT, 0)
            for j in range(LN_IT):
                ln_normalize(dve, n * LN_IT + j, j, xn)
                if j == 0:
                    meanwhile()
                if j + 1 < LN_IT:
                    ln_stats(dve, n * LN_IT + j + 1, j + 1)
                ln_low(dve, n * LN_IT + j, j)

        def ln_gpsimd_group(pool, k):
            pool.wait_ge(ln_var, k + 1)
            pool.tensor_tensor(ln_rs[:, :, :], ln_ve[:, :, :], neg_half[:, :, :], ALU.pow).then_inc(ln_rstd, 1)

        def ln_gpsimd(pool, n):
            with pool.Fori(0, LN_IT) as j:
                ln_gpsimd_group(pool, j + n * LN_IT)

        def ln_turn(pe, k, j, xn):
            for s in range(LS):
                pe.wait_ge(ln_norm[s], k + 1)
                pe.wait_ge(ln_lo[s], ONE + k)
                for c in range(DC):
                    m = pe.transpose(bank[s][:, c * P:(c + 1) * P], xn[:, s, c * P:(c + 1) * P], id32[:, :])
                m.then_inc(ln_turned[s], 1)

        def ln_high(act, k, j):
            for s in range(LS):
                act.wait_ge(ln_turned[s], k + 1)
                act.activation(tile_cols(xt_hi, j, s), bank[s][:, :].rearrange("p (a b) -> p a b", a=DC),
                               ACT.Copy).then_inc(ln_hi[s], 1)

        def ln_scalar(act, n):
            for j in range(LN_IT):
                ln_high(act, n * LN_IT + j, j)

        def mm3(pe, o, a_hi, a_lo, b_hi, b_lo, start, stop):
            pe.matmul(o, a_hi, b_hi, start=start, stop=False)
            pe.matmul(o, a_hi, b_lo, start=False, stop=False)
            return pe.matmul(o, a_lo, b_hi, start=False, stop=stop)

        wr = Room(work_arena, WORK_W)
        att_a_hi = wr.take(H, 2 * P, dt=F16)
        att_a_lo = wr.take(H, 2 * P, dt=F16)
        att_vo_hi = wr.take(H, D, dt=F16)
        att_vo_lo = wr.take(H, D, dt=F16)
        SW = DC * 256 + DC * 128 + 256 + 2048
        sw_hi = wr.take(SW, dt=F16)
        sw_lo = wr.take(SW, dt=F16)
        qc0_at = wr.at
        qc0_hi = wr.take(T, dt=F16)
        qc0_lo = wr.take(T, dt=F16)
        qc1 = wr.take(T, dt=F16)
        kv_hi = wr.take(T, dt=F16)
        kv_lo = wr.take(T, dt=F16)
        kvt_at = wr.at
        kvt_hi = wr.take(B, KVC, dt=F16)
        kvt_lo = wr.take(B, KVC, dt=F16)
        kr_hi = wr.take(T, dt=F16)
        kr_lo = wr.take(T, dt=F16)
        seg_bias = wr.take(B, S, dt=BF16)
        seg_scale = wr.take(B)
        cos_q = wr.take(R)
        sin_q = wr.take(R)
        cos_k = wr.take(S)
        sin_k = wr.take(S)
        att_end = wr.at

        def swv(t, at, *dims):
            n = int(np.prod(dims))
            v = t[:, at:at + n]
            return v.rearrange("p (a b) -> p a b", a=dims[0]) if len(dims) == 2 else v
        o_kvc, o_kr, o_qr = DC * 256, DC * 384, DC * 384 + 256
        wdq = [swv(t, 0, DC, 256) for t in (sw_hi, sw_lo)]
        wkvc = [swv(t, o_kvc, DC, 128) for t in (sw_hi, sw_lo)]
        wkr = [swv(t, o_kr, 2, 128) for t in (sw_hi, sw_lo)]
        wqr = [swv(t, o_qr, 2, 1024) for t in (sw_hi, sw_lo)]

        HW = 256 + 128 + 128 + 512
        pr = Room(work_arena, WORK_W)
        pr.at = att_end
        hw32 = pr.take(2, HW)
        hw_hi = pr.take(2, HW, dt=F16)
        hw_lo = pr.take(2, HW, dt=F16)
        ln_xn_prep = pr.take(LS, D)
        sw32 = work_arena[:, kvt_at:kvt_at + SW]
        prep_load = [sem(f"prep_load{s}") for s in range(2)]
        prep_hi = [sem(f"prep_hi{s}") for s in range(2)]
        prep_lo = [sem(f"prep_lo{s}") for s in range(2)]
        prep_mm = [sem(f"prep_mm{s}") for s in range(2)]
        prep_ahi = [sem(f"prep_ahi{s}") for s in range(2)]
        prep_alo = [sem(f"prep_alo{s}") for s in range(2)]
        consts_in, small_in, small_hi = (sem(n) for n in ("consts_in", "small_in", "small_hi"))
        ident_in = sem("ident_in")
        x_in = [sem(f"x_in{s}") for s in range(LN_IT)]

        jr = Room(work_arena, WORK_W)
        jr.at = att_end
        ctx_hi = jr.take(2 * DC, BLK, dt=F16)
        ctx_lo = jr.take(2 * DC, BLK, dt=F16)
        kt1 = jr.take(BLK)
        kt2 = jr.take(BLK)
        krot = jr.take(BLK)
        jr.at = max(jr.at, pr.at)
        ctx32 = jr.take(DC, BLK)
        segi = jr.take(B, dt=I32)
        segf = jr.take(B)
        iota = jr.take(S)
        mask_room = Room(work_arena, WORK_W)
        mask_room.at = qc0_at
        dist = mask_room.take(B, S)
        ahead = mask_room.take(B, S)
        v1 = jr.take(B)
        v2 = jr.take(B)
        ctx_load, ctx_h, ctx_l = sem("ctx_load"), sem("ctx_h"), sem("ctx_l")
        qkv_mm, qkv_h, qkv_l = sem("qkv_mm"), sem("qkv_h"), sem("qkv_l")
        kr_mm, kr_mul, kr_sum, kr_h = (sem(n) for n in ("kr_mm", "kr_mul", "kr_sum", "kr_h"))
        kvt_mm, kvt_cp = sem("kvt_mm"), sem("kvt_cp")
        seg_step = sem("seg_step")

        ar = Room(work_arena, WORK_W)
        ar.at = att_end
        rt1 = ar.take(H, R)
        rt2 = ar.take(H, R)
        rot = rt1
        rhl = ar.take(H, 2, R, dt=F16)
        qrt = ar.take(2, H, P, dt=F16)
        prob = ar.take(2, 4, P)
        pt_hi = ar.take(2, 4 * P, dt=F16)
        pt_lo = ar.take(2, 4 * P, dt=F16)
        ot_hi = ar.take(2, 4 * P, dt=F16)
        ot_lo = ar.take(2, 4 * P, dt=F16)
        nmax = ar.take(2, 4)
        ebias = ar.take(2, 4)
        escale = ar.take(2, 1)
        esum = ar.take(2, 4)
        rinv = ar.take(2, 4)
        q_mm = [sem(f"q_mm{s}") for s in range(2)]
        q_h = [sem(f"q_h{s}") for s in range(2)]
        q_free = [sem(f"q_free{s}") for s in range(2)]
        rope_sum, rope_h, rope_l, rope_tr, rope_cp = (
            sem(n) for n in ("rope_sum", "rope_h", "rope_l", "rope_tr", "rope_cp"))
        score_mm, smax, pth, ptl, oth, otl, yadd = (
            sem(n) for n in ("score_mm", "smax", "pth", "ptl", "oth", "otl", "yadd"))
        exped = [sem(f"exped{s}") for s in range(2)]
        recip = [sem(f"recip{s}") for s in range(2)]
        normed = [sem(f"normed{s}") for s in range(2)]
        pt_mm = [sem(f"pt_mm{s}") for s in range(2)]
        o_mm = [sem(f"o_mm{s}") for s in range(2)]
        y_mm = [sem(f"y_mm{s}") for s in range(2)]
        NG = 4 * 4

        CHANGE = (("rope", 0), ("step", NG), ("heads", 0), ("step", NG + 1), ("rope_split", 0), ("heads", 4),
                  ("step", NG + 2), ("turn", 0), ("heads", 8), ("heads", 12))

        def change_block(now, after, todo):
            for what, i in CHANGE:
                if what in todo:
                    block_ = now if what == "step" else after
                    if block_ is not None:
                        todo[what](block_, i)

        def rope_index(u):
            return 0 if u == 0 else 8 + u

        mr = Room(work_arena, WORK_W)
        cwt = mr.take(T, dt=F16)
        ffn_at = mr.at

        ffn_sems = [[sem(f"ffn_{what}{s}") for s in range(2)] for what in (
            "landed", "whi", "wlo", "selc", "up", "silu", "m1d", "m2d", "hhi", "hlo", "ymm", "yadd")]

        class FFN:
            (landed, whi, wlo, selc, up, silu, m1d, m2d, hhi, hlo, ymm, yadd) = ffn_sems


        def make_ffn(groups, pieces, kind, at, before):
            f = FFN()
            f.groups, f.pieces, f.kind, f.land = groups, pieces, kind, 32 if kind == "moe" else 16
            f.step0 = before.step0 + before.groups * NB if before else 0
            f.piece0 = before.piece0 + before.groups // 2 * before.pieces if before else 0
            f.land0 = before.land0 + before.groups // 2 * before.land if before else 0
            r = Room(work_arena, WORK_W)
            r.at = at
            f.w32 = r.take(2, 3 * 1024)
            f.w_hi = r.take(2, 3 * 1024, dt=F16)
            f.w_lo = r.take(2, 3 * 1024, dt=F16)
            f.sg = r.take(2, BLK)
            if kind == "moe":
                f.sel32 = r.take(2, GW, dt=F16)
                f.sel = r.take(2, GW, dt=F16)
                f.m1 = r.take(2, BLK)
            f.m2 = r.take(2, BLK)
            f.h_hi = r.take(2, GC, BLK, dt=F16)
            f.h_lo = r.take(2, GC, BLK, dt=F16)
            f.end = r.at
            return f

        moe = make_ffn(E * MOE_D // GW, 3, "moe", ffn_at, None)
        gr = Room(work_arena, WORK_W)
        gr.at = moe.end
        gw32 = gr.take(DC, E)
        gw_hi = gr.take(DC, E, dt=F16)
        gw_lo = gr.take(DC, E, dt=F16)
        gmx = gr.take(NT)
        gsub = gr.take(NT, E)
        gexp = gr.take(NT, E)
        gsum = gr.take(NT)
        grc = gr.take(NT)
        gsc = gr.take(NT, E + 2)
        gtop = gr.take(NT, 8)
        grep_ = gr.take(NT, E + 2)
        gcw = gr.take(NT, E)
        ln_xn_moe = gr.take(LS, D)
        gate_done = sem("gate_done")
        later_in = sem("later_in")
        gate_s, gate_mm, gate_v, gate_t, gate_c = (
            sem(n) for n in ("gate_s", "gate_mm", "gate_v", "gate_t", "gate_c"))

        cm = Room(work_arena, WORK_W)
        cm.at = moe.end
        memT_hi = cm.take(DC, T, dt=F16)
        memT_lo = cm.take(DC, T, dt=F16)
        mem_hi = cm.take(B, D, dt=F16)
        mem_lo = cm.take(B, D, dt=F16)
        mem32 = cm.take(2, DC * P)
        cr = Room(work_arena, moe.end)
        mm8 = cr.take(T, dt=U8)
        mm_f = cr.take(B, S)
        mm_bias = cr.take(B, S, dt=BF16)
        mvalid = cr.take(B)
        mscale = cr.take(B)
        mprob = cr.take(LS, P)
        mpt_hi = cr.take(LS, P, dt=F16)
        mpt_lo = cr.take(LS, P, dt=F16)
        mmax = cr.take(LS)
        mexp_bias = cr.take(LS)
        msum = cr.take(LS)
        mrec = cr.take(LS)
        mfac = cr.take(LS)
        ln_xn_mem = cr.take(LS, D)
        mem_load = [sem(f"mem_load{s}") for s in range(2)]
        mem_h = [sem(f"mem_h{s}") for s in range(2)]
        mem_l = [sem(f"mem_l{s}") for s in range(2)]
        mask_s = sem("mask_s")
        mem_scored, mem_max, mem_exp, mem_sums, mem_turned, mem_pt_hi, mem_pt_lo = (
            sem(n) for n in ("mem_scored", "mem_max", "mem_exp", "mem_sums", "mem_turned", "mem_pt_hi", "mem_pt_lo"))
        mem_read = [sem(f"mem_read{s}") for s in range(2)]
        mem_added = [sem(f"mem_added{s}") for s in range(2)]
        LN_AT = {which: 2 * LN_IT + i for i, which in enumerate(
            ((2, 0), (2, 1), (2, 2), (3, 0), (2, 3), (3, 1), (3, 2), (3, 3)))}

        kr_ = Room(work_arena, WORK_W)
        gT = kr_.take(NEXP // P, T)
        pk_at = kr_.at
        mlp = make_ffn(INTER // GW, 3, "mlp", pk_at, moe)
        pkm = make_ffn(NEXP // GW, 2, "pkm", pk_at, mlp)
        rr = Room(work_arena, pk_at)
        rr.at = cr.at
        kw32 = rr.take(DC * P + 2 * P)
        kw_hi = rr.take(DC * P + 2 * P, dt=F16)
        kw_lo = rr.take(DC * P + 2 * P, dt=F16)
        qT_hi = rr.take(T, dt=F16)
        qT_lo = rr.take(T, dt=F16)
        rx = rr.take(16, NK)
        sx = rr.take(16, 8)
        sy = rr.take(16, 8)
        ixu = rr.take(16, 8, dt=U32)
        iyu = rr.take(16, 8, dt=U32)
        al = rr.take(16, 64)
        al_rep = rr.take(16, 64)
        top = rr.take(16, 8)
        wsum = rr.take(16, 8)
        wtmp = rr.take(16, 8)
        far = rr.take(16)
        ur = Room(work_arena, WORK_W)
        ur.at = mlp.end
        ry = ur.take(16, NK)
        ixf = ur.take(16, 8)
        iyf = ur.take(16, 8)
        cnt = ur.take(16, 8)
        den = ur.take(16)
        ex_ = ur.take(16, KX)
        iota64 = ur.take(NK)
        rank8 = ur.take(8)
        G = ur.take(KX, NK)
        cc = ur.take(1, KX)
        s64 = ur.take(1, NK)
        eq = ur.take(8, NK)
        eqx = ur.take(KX, 8)
        pk_in = sem("pk_in")
        pk_s, pk_qmm, pk_qh, pk_ql, pk_rmm, pk_r, pk_act = (
            sem(n) for n in ("pk_s", "pk_qmm", "pk_qh", "pk_ql", "pk_rmm", "pk_r", "pk_act"))
        pk_v, pk_g, pk_t, pk_c = (sem(n) for n in ("pk_v", "pk_g", "pk_t", "pk_c"))
        pk_g0, pk_u = sem("pk_chain"), sem("pk_unit")
        stored = sem("stored")

        ONE = 1
        from_one = [prep_lo, prep_alo, FFN.wlo, FFN.selc, FFN.yadd, ln_lo, q_free, exped, pt_mm, o_mm, y_mm,
                    mem_l,
                    [ctx_l, qkv_l, kr_mul, kvt_cp, ptl, otl, yadd, rope_cp, score_mm, rope_tr, rope_h, rope_l,
                     pk_c, pk_u, pk_t]]

        block = ctx.enter_context(nc.Block())

        @block.sync
        def _(sp):
            def x_load(q):
                sp.dma_start(x[:, q * LS:(q + 1) * LS, :], ins["x"][:, q * LS:(q + 1) * LS, :]).then_inc(x_in[q], 16)

            def head_load(h):
                sp.wait_ge(prep_lo[h % 2], ONE + h // 2)
                sp.dma_start(hw32[:, h % 2, :], ins["head_w"][h:h + 1, :, :].rearrange(
                    "a p n -> p (a n)")).then_inc(prep_load[h % 2], 16)

            sp.dma_start(id32[:, :], ins["ident"]).then_inc(ident_in, 16)
            x_load(0)
            for several in from_one:
                for semaphore in several:
                    sp.sem_inc(semaphore, ONE)
            head_load(0)
            head_load(1)
            sp.dma_start(sw32, ins["small_w"]).then_inc(small_in, 16)
            x_load(1)
            for dst, src in ((cos_q, "cos_q"), (sin_q, "sin_q"), (cos_k, "cos_k"), (sin_k, "sin_k")):
                sp.dma_start(dst, ins[src]).then_inc(consts_in, 16)
            sp.dma_start(segi, ins["seg"]).then_inc(consts_in, 16)
            sp.dma_start(iota, ins["iota"]).then_inc(consts_in, 16)
            for h in range(2, H):
                head_load(h)
                if h in (3, 5):
                    x_load((h + 1) // 2)
            sp.dma_start(ctx32, ins["ctxT"][:, :, 0:BLK]).then_inc(ctx_load, 16)
            end_phase(sp, "sp")
            for j in range(1, NB):
                sp.wait_ge(ctx_l, ONE + j)
                sp.dma_start(ctx32, ins["ctxT"][:, :, j * BLK:(j + 1) * BLK]).then_inc(ctx_load, 16)
            end_phase(sp, "sp")
            end_phase(sp, "sp")

            def ffn_loads(f, w, sel, also=None):
                for g in range(f.groups):
                    s = g % 2
                    sp.wait_ge(f.wlo[s], ONE + f.piece0 + g // 2 * f.pieces)
                    if sel is not None:
                        sp.wait_ge(f.selc[s], ONE + g // 2)
                    sp.dma_start(f.w32[:, s, 0:f.pieces * 1024], w[ds(g, 1), :, :].rearrange("a p n -> p (a n)")).then_inc(
                        f.landed[s], 16)
                    if sel is not None:
                        sp.dma_start(f.sel32[:, s, :], sel[ds(g, 1), :, :].rearrange(
                            "a p n -> p (a n)")).then_inc(f.landed[s], 16)
                    if also is not None and 2 <= g < 2 + B:
                        also(g - 2)

            def memory_load(b):
                if b == 0:
                    sp.wait_ge(gate_c, 2 * NB)
                for s in range(2):
                    sp.wait_ge(mem_l[s], ONE + b)
                    src = (ins["ctxT"][:, :, b * P:(b + 1) * P], ins["ctx"][:, b:b + 1, :])[s]
                    dst = mem32[:, s, :].rearrange("p (a b) -> p a b", a=(DC, 1)[s])
                    sp.dma_start(dst, src).then_inc(mem_load[s], 16)

            sp.dma_start(gw32, ins["moe_gate"]).then_inc(later_in, 16)
            ffn_loads(moe, ins["moe_w"], ins["moe_sel"], memory_load)
            end_phase(sp, "sp")
            sp.dma_start(mm8, ins["mem_mask"].partition_broadcast(P)).then_inc(later_in, 16)
            sp.dma_start(kw32, ins["pk_w"]).then_inc(pk_in, 16)
            for s in range(2):
                sp.wait_ge(mem_read[s], B // 2)
            sp.dma_start(iota64, ins["iota"][:, 0:NK]).then_inc(pk_in, 16)
            sp.dma_start(rank8, ins["rank8"]).then_inc(pk_in, 16)
            ffn_loads(mlp, ins["mlp_w"], None)
            ffn_loads(pkm, ins["pk_e"], None)
            for t in range(NB):
                k = pkm.step0 + (pkm.groups - 1) * NB + t
                for yb in range(2):
                    sp.wait_ge(pkm.yadd[yb], ONE + k * 2 + 2)
                sp.dma_start(out[:, t * 4:(t + 1) * 4, :], x[:, t * 4:(t + 1) * 4, :]).then_inc(stored, 16)
            end_phase(sp, "sp")
            sp.wait_ge(stored, 16 * NB)

        @block.tensor
        def _(pe):
            pe.wait_ge(ident_in, 16)
            for q in range(LN_IT):
                ln_turn(pe, q, q, ln_xn_prep)
                with pe.Fori(q * 2, q * 2 + 2) as j:
                    for s in range(2):
                        hh, hl = hw_hi[:, s, :], hw_lo[:, s, :]
                        pe.wait_ge(prep_lo[s], ONE + j + 1)
                        pe.wait_ge(prep_alo[s], ONE + j)
                        for c in range(2):
                            cs = slice(c * P, (c + 1) * P)
                            mm3(pe, bank[4 + 2 * s][:, cs], hh[:, cs], hl[:, cs], hh[:, 256:384],
                                hl[:, 256:384], start=True, stop=True)
                        mm3(pe, bank[5 + 2 * s][:, :], hh[:, 384:512], hl[:, 384:512], hh[:, 512:1024],
                            hl[:, 512:1024], start=True, stop=True).then_inc(prep_mm[s], 1)
            end_phase(pe, "pe")
            with pe.Fori(0, NB // 2) as jj:
                for half in range(2):
                    j = jj * 2 + half
                    blk = ds(j * BLK, BLK)
                    pe.wait_ge(ctx_l, ONE + j + 1)
                    pe.wait_ge(qkv_l, ONE + j * 3)
                    for c in range(DC):
                        cc_ = half * DC + c
                        m = mm3(pe, bank[2][:, :], wkvc[0][:, c, :], wkvc[1][:, c, :], ctx_hi[:, cc_, :],
                                ctx_lo[:, cc_, :], start=(c == 0), stop=(c == DC - 1))
                    m.then_inc(qkv_mm, 1)
                    for c in range(DC):
                        for i in range(2):
                            cs = slice(i * P, (i + 1) * P)
                            m = mm3(pe, bank[i][:, :], wdq[0][:, c, cs], wdq[1][:, c, cs], xt_hi[:, c, blk],
                                    xt_lo[:, c, blk], start=(c == 0), stop=(c == DC - 1))
                    m.then_inc(qkv_mm, 1)
                    pe.wait_ge(qkv_l, ONE + j * 3 + 1)
                    pe.wait_ge(kr_mul, ONE + j * 2)
                    for i in range(2):
                        m = mm3(pe, bank[3 + i][:, :], wkr[0][:, i, :], wkr[1][:, i, :], kv_hi[:, blk],
                                kv_lo[:, blk], start=True, stop=True)
                    m.then_inc(kr_mm, 1)
                    pe.wait_ge(kvt_cp, ONE + j * 2)
                    o = bank[5][:, :].bitcast(F16)
                    for i, t in enumerate((kv_hi, kv_lo)):
                        for u in range(TPB):
                            m = pe.transpose(o[:, (i * TPB + u) * P:(i * TPB + u + 1) * P],
                                             t[:, ds(j * BLK + u * P, P)], id16[:, :])
                    m.then_inc(kvt_mm, 1)
            end_phase(pe, "pe")
            TR = bank[7][:, :].bitcast(F16)

            def rope_pe(j, u):
                tok = ds(j * BLK + u * P, P)
                for a in range(2):
                    pe.wait_ge(q_free[a], ONE + j * 12 + rope_index(u))
                    cs = slice(a * 512, (a + 1) * 512)
                    o = bank[5 + a][:, :]
                    pe.matmul(o, qc0_hi[:, tok], wqr[0][:, 0, cs], start=True, stop=False)
                    pe.matmul(o, qc0_hi[:, tok], wqr[1][:, 0, cs], start=False, stop=False)
                    pe.matmul(o, qc0_lo[:, tok], wqr[0][:, 0, cs], start=False, stop=False)
                    pe.matmul(o, qc1[:, tok], wqr[0][:, 1, cs], start=False, stop=False)
                    pe.matmul(o, qc1[:, tok], wqr[1][:, 1, cs], start=False, stop=True).then_inc(q_mm[a], 1)

            def rope_turn(j, u, a):
                if a == 0:
                    pe.wait_ge(rope_l, ONE + j * 4 + u + 1)
                pe.wait_ge(rope_cp, ONE + j * 8 + u * 2 + a)
                for h in range(8):
                    m = pe.transpose(TR[:, h * P:(h + 1) * P],
                                     rhl[:, a * 8 + h, :, :].rearrange("p a b -> p (a b)"), id16[:, :])
                m.then_inc(rope_tr, 1)

            def queries_pe(j, h0):
                blk = ds(j * BLK, BLK)
                for h in range(h0, h0 + 4):
                    o = bank[5 + h % 2][:, :]
                    pe.wait_ge(q_free[h % 2], ONE + j * 12 + 1 + h // 2)
                    pe.matmul(o, att_a_hi[:, h, 0:P], qc0_hi[:, blk], start=True, stop=False)
                    pe.matmul(o, att_a_hi[:, h, 0:P], qc0_lo[:, blk], start=False, stop=False)
                    pe.matmul(o, att_a_lo[:, h, 0:P], qc0_hi[:, blk], start=False, stop=False)
                    pe.matmul(o, att_a_hi[:, h, P:2 * P], qc1[:, blk], start=False, stop=False)
                    pe.matmul(o, att_a_lo[:, h, P:2 * P], qc1[:, blk], start=False,
                              stop=True).then_inc(q_mm[h % 2], 1)

            def attend_pe(j, n):
                if n < NG:
                    u, g, k = n // 4, n % 4, n % 2
                    if g in (0, 2):
                        pe.wait_ge(rope_cp, ONE + j * 8 + u * 2 + 1 + g // 2)
                    pe.wait_ge(q_free[0], ONE + j * 12 + 2 * g + 3)
                    pe.wait_ge(q_free[1], ONE + j * 12 + 2 * g + 3)
                    pe.wait_ge(exped[k], ONE + j * 8 + n // 2)
                    sc = bank[k]
                    keys = ds(j * BLK + u * P, P)
                    pe.matmul(sc[:, :].rearrange("p (a b) -> p a b", a=4), idbf[:, :],
                              seg_bias[:, ds(j * 4 + u, 1), :].to_broadcast([P, 4, S]),
                              start=True, stop=False)
                    for i in range(4):
                        h = 4 * g + i
                        o = sc[:, i * P:(i + 1) * P]
                        qs = slice(u * P, (u + 1) * P)
                        pe.matmul(o, qp_hi[:, h, qs], kv_hi[:, keys], start=False, stop=False)
                        pe.matmul(o, qp_hi[:, h, qs], kv_lo[:, keys], start=False, stop=False)
                        pe.matmul(o, qp_lo[:, h, qs], kv_hi[:, keys], start=False, stop=False)
                        pe.matmul(o, qrt[:, u % 2, h, :], kr_hi[:, keys], start=False, stop=False)
                        m = pe.matmul(o, qrt[:, u % 2, h, :], kr_lo[:, keys], start=False,
                                      stop=(i == 3))
                    m.then_inc(score_mm, 1)
                    if g == 0:
                        rope_turn(j, u, 1)
                        if u < 3:
                            rope_pe(j, u + 1)
                if 1 <= n <= NG:
                    q, k = n - 1, (n - 1) % 2
                    pe.wait_ge(normed[k], j * 8 + q // 2 + 1)
                    pe.wait_ge(ptl, ONE + j * NG + q)
                    for i in range(4):
                        m = pe.transpose(bank[2][:, i * P:(i + 1) * P], prob[:, k, i, :], id32[:, :])
                    m.then_inc(pt_mm[k], 1)
                if 2 <= n <= NG + 1:
                    q, k = n - 2, (n - 2) % 2
                    u = q // 4
                    pe.wait_ge(ptl, ONE + j * NG + q + 1)
                    pe.wait_ge(otl, ONE + j * NG + q)
                    kh, kl = (t[:, ds(j * 4 + u, 1), :].rearrange("p a b -> p (a b)")
                              for t in (kvt_hi, kvt_lo))
                    mm3(pe, bank[3][:, :], kh, kl, pt_hi[:, k, :], pt_lo[:, k, :],
                        start=True, stop=True).then_inc(o_mm[k], 1)
                if n < NG - 4 and n % 4 == 3:
                    rope_turn(j, n // 4 + 1, 0)
                if n >= 3:
                    q, k = n - 3, (n - 3) % 2
                    u, g = q // 4, q % 4
                    pe.wait_ge(otl, ONE + j * NG + q + 1)
                    if g == 0:
                        pe.wait_ge(yadd, ONE + j * 4 + u)
                    for i in range(4):
                        h = 4 * g + i
                        m = mm3(pe, bank[4][:, :], ot_hi[:, k, i * P:(i + 1) * P],
                                ot_lo[:, k, i * P:(i + 1) * P], att_vo_hi[:, h, :], att_vo_lo[:, h, :],
                                start=(h == 0), stop=(h == H - 1))
                    m.then_inc(y_mm[k], 1)

            todo = {"rope": rope_pe, "heads": queries_pe, "step": attend_pe,
                    "turn": lambda j, a: rope_turn(j, 0, a)}
            change_block(None, 0, todo)
            with pe.Fori(0, NB - 1) as j:
                for n in range(NG):
                    attend_pe(j, n)
                change_block(j, j + 1, todo)
            for n in range(NG):
                attend_pe(NB - 1, n)
            change_block(NB - 1, None, todo)
            end_phase(pe, "pe")
            for q in range(LN_IT + 1):
                if q < LN_IT:
                    ln_turn(pe, LN_IT + q, q, ln_xn_moe)
                if q == 0:
                    pe.wait_ge(gate_s, 2)
                    continue
                for s in range(LS):
                    pe.wait_ge(ln_lo[s], ONE + LN_IT + q)
                for t in range((q - 1) * LS, q * LS):
                    for c in range(DC):
                        ts_ = slice(t * P, (t + 1) * P)
                        m = mm3(pe, bank[4][:, t * E:(t + 1) * E], xt_hi[:, c, ts_], xt_lo[:, c, ts_],
                                gw_hi[:, c, :], gw_lo[:, c, :], start=(c == 0), stop=(c == DC - 1))
            m.then_inc(gate_mm, 1)

            def turn_expert_gates():
                pe.wait_ge(gate_done, 1)
                for t in range(NB):
                    pe.wait_ge(gate_c, 2 * t)
                    for i in range(TPB):
                        m = pe.transpose(bank[5][0:E, i * P:(i + 1) * P], gcw[:, t * TPB + i, :], id32[:, :])
                    m.then_inc(gate_t, 1)
                pe.wait_ge(gate_c, 2 * NB)

            def turn_gates(u):
                pe.wait_ge(pk_g, u + 1)
                pe.wait_ge(pk_c, ONE + u)
                for i in range(NEXP // P):
                    m = pe.transpose(bank[4 + i // 4][:, i % 4 * P:(i % 4 + 1) * P],
                                     G[:, 2 * i:2 * i + 2, :].rearrange("p a b -> p (a b)"), id32[:, :])
                m.then_inc(pk_t, 1)

            def ffn_tensor(f, started=False, following=None):
                def A(f, j, s, before_gates=None):
                    gs, t = (s // NB) % 2, s % NB
                    if t == 0:
                        it = j + 1 if s == 2 * NB else j
                        pe.wait_ge(f.wlo[gs], ONE + f.piece0 + it * f.pieces + f.pieces - 1)
                    k = f.step0 + j * (2 * NB) + s
                    wh, wl = f.w_hi[:, gs, :], f.w_lo[:, gs, :]
                    toks = slice(t * BLK, (t + 1) * BLK)
                    for c in range(GC):
                        pe.wait_ge(f.m2d[c], k)
                        for i in range(f.pieces - 1):
                            for d in range(DC):
                                ws = slice(i * 1024 + d * GW + c * P, i * 1024 + d * GW + (c + 1) * P)
                                m = mm3(pe, bank[2 * i + c][:, :], wh[:, ws], wl[:, ws], xt_hi[:, d, toks],
                                        xt_lo[:, d, toks], start=(d == 0), stop=(d == DC - 1))
                        if f.kind == "moe":
                            if before_gates is None:
                                expert_rows(j, s, c)
                        else:
                            m.then_inc(f.up[c], 1)
                    if before_gates is not None:
                        before_gates()
                        for c in range(GC):
                            expert_rows(j, s, c)

                def expert_rows(j, s, c):
                    gs, t = (s // NB) % 2, s % NB
                    if t == 0 and c == 0:
                        pe.wait_ge(f.selc[gs], ONE + (j + 1 if s == 2 * NB else j) + 1)
                    pe.matmul(bank[4 + c][:, :], f.sel[:, gs, c * P:(c + 1) * P], cwt[:, t * BLK:(t + 1) * BLK],
                              start=True, stop=True).then_inc(f.up[c], 1)

                def Dn(j, s):
                    gs, t, hp = s // NB, s % NB, s % 2
                    k = f.step0 + j * (2 * NB) + s
                    if t == 0:
                        pe.wait_ge(f.wlo[gs], ONE + f.piece0 + j * f.pieces + f.pieces)
                    for c in range(GC):
                        pe.wait_ge(f.hlo[c], k + 1)
                    wh, wl = f.w_hi[:, gs, :], f.w_lo[:, gs, :]
                    o0 = (f.pieces - 1) * 1024
                    for q in range(TPB):
                        yb = q % 2
                        pe.wait_ge(f.yadd[yb], ONE + k * 2 + q // 2)
                        for c in range(GC):
                            ws = slice(o0 + c * D, o0 + (c + 1) * D)
                            qs = slice(q * P, (q + 1) * P)
                            m = mm3(pe, bank[6 + yb][:, :], f.h_hi[:, hp, c, qs], f.h_lo[:, hp, c, qs],
                                    wh[:, ws], wl[:, ws], start=(c == 0), stop=(c == GC - 1))
                        m.then_inc(f.ymm[yb], 1)

                def body(j, last):
                    for s in range(2 * NB):
                        if not (last and s == 2 * NB - 1):
                            A(f, j, s + 1)
                        elif following is not None:
                            A(following, 0, 0)
                        if f.kind == "mlp" and s % 2 == 1:
                            turn_gates(j * NB + s // 2)
                        Dn(j, s)

                if not started:
                    A(f, 0, 0, turn_expert_gates if f.kind == "moe" else None)
                n = f.groups // 2
                if n > 1:
                    with pe.Fori(0, n - 1) as j:
                        body(j, False)
                body(n - 1, True)

            ffn_tensor(moe)
            end_phase(pe, "pe")
            def memory_scores(g):
                for s in range(LS):
                    pe.wait_ge(ln_lo[s], ONE + LN_AT[2, g] + 1)
                pe.matmul(bank[4][:, :], idbf[:, :],
                          mm_bias[:, g * LS:(g + 1) * LS, :].rearrange("p a b -> p (a b)"), start=True, stop=False)
                for i in range(LS):
                    toks = slice((g * LS + i) * P, (g * LS + i + 1) * P)
                    for c in range(DC):
                        m = mm3(pe, bank[4][:, i * P:(i + 1) * P], xt_hi[:, c, toks], xt_lo[:, c, toks],
                                memT_hi[:, c, toks], memT_lo[:, c, toks], start=False,
                                stop=(i == LS - 1 and c == DC - 1))
                m.then_inc(mem_scored, 1)

            def memory_readout(g):
                pe.wait_ge(mem_exp, g + 1)
                for i in range(LS):
                    m = pe.transpose(bank[5][:, i * P:(i + 1) * P], mprob[:, i, :], id32[:, :])
                m.then_inc(mem_turned, 1)
                pe.wait_ge(mem_pt_lo, g + 1)
                for i in range(LS):
                    b, k = g * LS + i, i % 2
                    pe.wait_ge(mem_added[k], b // 2)
                    mm3(pe, bank[6 + k][:, :], mpt_hi[:, i, :], mpt_lo[:, i, :], mem_hi[:, b, :], mem_lo[:, b, :],
                        start=True, stop=True).then_inc(mem_read[k], 1)

            def key_queries(t):
                for s in range(LS):
                    pe.wait_ge(ln_lo[s], ONE + LN_AT[3, t] + 1)
                toks = slice(t * BLK, (t + 1) * BLK)
                for c in range(DC):
                    ws = slice(c * P, (c + 1) * P)
                    m = mm3(pe, bank[4 + t][:, :], kw_hi[:, ws], kw_lo[:, ws], xt_hi[:, c, toks],
                            xt_lo[:, c, toks], start=(c == 0), stop=(c == DC - 1))
                m.then_inc(pk_qmm, 1)

            ln_turn(pe, LN_AT[2, 0], 0, ln_xn_mem)
            pe.wait_ge(mask_s, 4)
            for g in range(LN_IT):
                memory_scores(g)
                if g + 1 < LN_IT:
                    ln_turn(pe, LN_AT[2, g + 1], g + 1, ln_xn_mem)
                memory_readout(g)
                if g > 0:
                    ln_turn(pe, LN_AT[3, g - 1], g - 1, ln_xn_mem)
            pe.wait_ge(pk_s, 2)
            key_queries(0)
            key_queries(1)
            ln_turn(pe, LN_AT[3, 3], 3, ln_xn_mem)
            for k in range(2):
                pe.wait_ge(mem_added[k], B // 2)
            key_queries(2)
            key_queries(3)
            for t in range(NT):
                ts_, half = slice(t * P, (t + 1) * P), t // 8
                if t % 8 == 0:
                    pe.wait_ge(pk_ql, (half + 1) * NB // 2)
                ks = slice(DC * P + half * P, DC * P + (half + 1) * P)
                m = mm3(pe, bank[t // 4][:, (t % 4) * P:(t % 4 + 1) * P], qT_hi[:, ts_], qT_lo[:, ts_],
                        kw_hi[:, ks], kw_lo[:, ks], start=True, stop=True)
                if t % 8 == 7:
                    m.then_inc(pk_rmm, 1)
            pe.wait_ge(pk_r, 4)
            ffn_tensor(mlp, following=pkm)
            ffn_tensor(pkm, started=True)
            end_phase(pe, "pe")

        @block.scalar
        def _(act):
            act.wait_ge(ident_in, 16)
            act.activation(id16[:, :], id32[:, :], ACT.Copy).then_inc(small_hi, 1)
            act.activation(idbf[:, :], id32[:, :], ACT.Copy).then_inc(small_hi, 1)

            def head_high(h):
                s = h % 2
                act.wait_ge(prep_load[s], h // 2 * 16 + 16)
                act.wait_ge(prep_mm[s], h // 2)
                act.activation(hw_hi[:, s, :], hw32[:, s, :], ACT.Copy, scale=WS).then_inc(prep_hi[s], 1)

            for h in range(H):
                if h == 0:
                    head_high(0)
                if h + 1 < H:
                    head_high(h + 1)
                if h % LS == 0:
                    ln_high(act, h // LS, h // LS)
                if h == 1:
                    act.wait_ge(small_in, 16)
                    act.activation(sw_hi, sw32, ACT.Copy, scale=WS).then_inc(small_hi, 1)
                act.wait_ge(prep_mm[h % 2], h // 2 + 1)
                act.activation(att_a_hi[:, h, :], bank[4 + 2 * (h % 2)][:, 0:256], ACT.Copy, scale=1 / WS)
                act.activation(att_vo_hi[:, h, :], bank[5 + 2 * (h % 2)][:, :], ACT.Copy,
                               scale=1 / WS).then_inc(prep_ahi[h % 2], 1)
            end_phase(act, "act")

            def context_high(j):
                act.wait_ge(ctx_load, j * 16 + 16)
                act.activation(ctx_hi[:, j % 2 * DC:(j % 2 + 1) * DC, :], ctx32, ACT.Copy).then_inc(ctx_h, 1)

            context_high(0)
            for j in range(NB):
                blk = slice(j * BLK, (j + 1) * BLK)
                act.wait_ge(qkv_mm, j * 2 + 1)
                act.activation(kv_hi[:, blk], bank[2][:, :], ACT.Copy, scale=1 / WS).then_inc(qkv_h, 1)
                if j + 1 < NB:
                    context_high(j + 1)
                act.wait_ge(qkv_mm, j * 2 + 2)
                act.activation(qc0_hi[:, blk], bank[0][:, :], ACT.Copy, scale=1 / WS).then_inc(qkv_h, 1)
                act.activation(qc1[:, blk], bank[1][:, :], ACT.Copy, scale=1 / WS).then_inc(qkv_h, 1)
                act.wait_ge(kr_sum, j + 1)
                act.activation(kr_hi[:, blk], krot, ACT.Copy).then_inc(kr_h, 1)
                act.wait_ge(kvt_mm, j + 1)
                o = bank[5][:, :].bitcast(F16)
                for i, t in enumerate((kvt_hi, kvt_lo)):
                    act.activation(t[:, j * TPB:(j + 1) * TPB, :],
                                   o[:, i * BLK:(i + 1) * BLK].rearrange("p (a b) -> p a b", a=TPB),
                                   ACT.Copy).then_inc(kvt_cp, 1)
            end_phase(act, "act")
            TR = bank[7][:, :].bitcast(F16)

            def rope_act(j, u):
                act.wait_ge(rope_sum, j * 4 + u + 1)
                act.wait_ge(rope_tr, ONE + j * 8 + u * 2)
                act.activation(rhl[:, :, 0, :], rot, ACT.Copy).then_inc(rope_h, 1)

            def rope_copy(j, u, a):
                act.wait_ge(rope_tr, ONE + j * 8 + u * 2 + a + 1)
                act.activation(qrt[:, u % 2, a * 8:(a + 1) * 8, :].rearrange("p a b -> p (a b)"),
                               TR[:, :], ACT.Copy).then_inc(rope_cp, 1)

            def queries_act(j, h0):
                act.wait_ge(score_mm, ONE + j * NG)
                for h in range(h0, h0 + 4):
                    act.wait_ge(q_mm[h % 2], j * 12 + 1 + h // 2 + 1)
                    act.activation(qp_hi[:, h, :], bank[5 + h % 2][:, :], ACT.Copy,
                                   scale=1 / WS).then_inc(q_h[h % 2], 1)

            def attend_act(j, n):
                if n < NG:
                    u, g, k = n // 4, n % 4, n % 2
                    act.wait_ge(pt_mm[k], ONE + j * 8 + n // 2)
                    act.wait_ge(smax, (j * NG + n) * 2 + 2)
                    for i in range(4):
                        m = act.activation(prob[:, k, i, :], bank[k][:, i * P:(i + 1) * P], ACT.Exp,
                                           bias=ebias[:, k, i:i + 1],
                                           scale=escale[:, u % 2, :],
                                           accum_out=esum[:, k, i:i + 1])
                    m.then_inc(exped[k], 1)
                    if g == 0:
                        rope_copy(j, u, 1)
                    if g == 2 and u < 3:
                        rope_act(j, u + 1)
                if 1 <= n <= NG:
                    q, k = n - 1, (n - 1) % 2
                    act.wait_ge(pt_mm[k], ONE + j * 8 + q // 2 + 1)
                    act.wait_ge(o_mm[k], ONE + j * 8 + q // 2)
                    act.activation(pt_hi[:, k, :], bank[2][:, :], ACT.Copy, scale=PS).then_inc(pth, 1)
                if 2 <= n <= NG + 1:
                    q, k = n - 2, (n - 2) % 2
                    act.wait_ge(o_mm[k], ONE + j * 8 + q // 2 + 1)
                    act.wait_ge(y_mm[k], ONE + j * 8 + q // 2)
                    act.activation(ot_hi[:, k, :], bank[3][:, :], ACT.Copy, scale=OS / PS).then_inc(oth, 1)
                if n < NG - 4 and n % 4 == 3:
                    rope_copy(j, n // 4 + 1, 0)

            todo = {"rope_split": rope_act, "heads": queries_act, "step": attend_act,
                    "turn": lambda j, a: rope_copy(j, 0, a)}
            change_block(None, 0, todo)
            with act.Fori(0, NB - 1) as j:
                for n in range(NG):
                    attend_act(j, n)
                change_block(j, j + 1, todo)
            for n in range(NG):
                attend_act(NB - 1, n)
            change_block(NB - 1, None, todo)
            end_phase(act, "act")
            act.wait_ge(later_in, 16)
            act.activation(gw_hi, gw32, ACT.Copy, scale=WS).then_inc(gate_s, 1)
            ln_scalar(act, 1)
            def ffn_scalar(f, part="rest", following=None):
                def units(k, s):
                    for c in range(GC):
                        act.wait_ge(f.up[c], k + 1)
                        act.activation(f.sg[:, c, :], bank[c][:, :], ACT.Silu,
                                       scale=1 / WS).then_inc(f.silu[c], 1)
                    for c in range(GC):
                        act.wait_ge(f.m2d[c], k + 1)
                        act.activation(f.h_hi[:, s % 2, c, :], f.m2[:, c, :], ACT.Copy).then_inc(f.hhi[c], 1)

                def split(f, gs, it, piece):
                    if piece == 0:
                        act.wait_ge(f.landed[gs], f.land0 + it * f.land + f.land)
                        if f.kind == "moe":
                            act.activation(f.sel[:, gs, :], f.sel32[:, gs, :], ACT.Copy).then_inc(f.selc[gs], 1)
                    cs = slice(piece * 1024, (piece + 1) * 1024)
                    act.activation(f.w_hi[:, gs, cs], f.w32[:, gs, cs], ACT.Copy,
                                   scale=WS).then_inc(f.whi[gs], 1)

                if part == "split":
                    for piece in range(f.pieces):
                        split(f, 0, 0, piece)
                    return

                def body(j, last):
                    for s in range(2 * NB):
                        units(f.step0 + j * (2 * NB) + s, s)
                        gs, t = s // NB, s % NB
                        if 1 <= t <= f.pieces and not (last and gs == 1):
                            split(f, 1 - gs, j + gs, t - 1)
                        elif following is not None and last and gs == 1 and 1 <= t <= following.pieces:
                            split(following, 0, 0, t - 1)

                n = f.groups // 2
                if n > 1:
                    with act.Fori(0, n - 1) as j:
                        body(j, False)
                body(n - 1, True)

            ffn_scalar(moe, part="split")
            act.wait_ge(gate_v, 2)
            act.activation(gexp, gsub, ACT.Exp, scale=1 / WS).then_inc(gate_v, 1)
            for t in range(NB):
                act.wait_ge(gate_t, t + 1)
                act.activation(cwt[0:E, t * BLK:(t + 1) * BLK], bank[5][0:E, :], ACT.Copy,
                               scale=GS).then_inc(gate_c, 1)
            ffn_scalar(moe)
            end_phase(act, "act")
            def memory_exps(g):
                act.wait_ge(mem_turned, g)
                act.wait_ge(mem_max, 2 * g + 2)
                for i in range(LS):
                    m = act.activation(mprob[:, i, :], bank[4][:, i * P:(i + 1) * P], ACT.Exp,
                                       bias=mexp_bias[:, i:i + 1], scale=mscale[:, g * LS + i:g * LS + i + 1],
                                       accum_out=msum[:, i:i + 1])
                m.then_inc(mem_exp, 1)
                act.wait_ge(mem_turned, g + 1)
                act.activation(mpt_hi.rearrange("p a b -> p (a b)"), bank[5][:, :], ACT.Copy).then_inc(mem_pt_hi, 1)

            def queries_high(t):
                act.wait_ge(pk_qmm, t + 1)
                act.activation(qT_hi[:, t * BLK:(t + 1) * BLK], bank[4 + t][:, :], ACT.Copy,
                               scale=1 / WS).then_inc(pk_qh, 1)

            ln_high(act, LN_AT[2, 0], 0)
            act.wait_ge(pk_in, 16)
            act.activation(kw_hi, kw32, ACT.Copy, scale=WS).then_inc(pk_s, 1)
            for g in range(LN_IT):
                if g + 1 < LN_IT:
                    ln_high(act, LN_AT[2, g + 1], g + 1)
                memory_exps(g)
                if g > 0:
                    ln_high(act, LN_AT[3, g - 1], g - 1)
            queries_high(0)
            queries_high(1)
            ln_high(act, LN_AT[3, 3], 3)
            queries_high(2)
            queries_high(3)
            ffn_scalar(mlp, part="split")
            for i, t in enumerate((rx, ry)):
                act.wait_ge(pk_rmm, i + 1)
                for a in range(2):
                    act.activation(t[:, a * 8:(a + 1) * 8, :].rearrange("p a b -> p (a b)"),
                                   bank[2 * i + a][:, :], ACT.Copy, scale=1 / WS).then_inc(pk_r, 1)
            for i, t in enumerate((rx, ry)):
                act.wait_ge(pk_v, 3 * i + 3)
                act.activation(t, t, ACT.Exp).then_inc(pk_act, 1)
            act.wait_ge(pk_v, 8)
            act.activation(al, al, ACT.Exp).then_inc(pk_act, 1)
            ffn_scalar(mlp, following=pkm)
            ffn_scalar(pkm)
            end_phase(act, "act")

        @block.vector
        def _(dve):
            def lo_of(o, src, scale, hi):
                return dve.scalar_tensor_tensor(out=o, in0=src, scalar=scale, in1=hi, op0=ALU.mult,
                                                op1=ALU.subtract)

            def head_low(h):
                s = h % 2
                dve.wait_ge(prep_hi[s], h // 2 + 1)
                lo_of(hw_lo[:, s, :], hw32[:, s, :], WS, hw_hi[:, s, :]).then_inc(prep_lo[s], 1)

            def segment_scales():
                dve.wait_ge(consts_in, 96)
                dve.tensor_copy(segf, segi).then_inc(seg_step, 1)
                dve.wait_ge(seg_step, 1)
                dve.tensor_scalar(v1, segf, 0.0, A_SCALE, ALU.is_ge, ALU.mult).then_inc(seg_step, 1)
                dve.tensor_scalar(v2, segf, float(S - 1 + LOOKBACK), None, ALU.is_le).then_inc(seg_step, 1)
                dve.wait_ge(seg_step, 3)
                dve.tensor_tensor(seg_scale, v1, v2, ALU.mult).then_inc(seg_step, 1)

            for h in range(H):
                s, q = h % 2, h // LS
                if h == 0:
                    dve.wait_ge(x_in[0], 16)
                    ln_stats(dve, 0, 0)
                if h % LS == 0:
                    ln_normalize(dve, q, q, ln_xn_prep)
                if h == 0:
                    head_low(0)
                if h + 1 < H:
                    head_low(h + 1)
                if h % LS == 0:
                    ln_low(dve, q, q)
                if h == 1:
                    dve.wait_ge(small_hi, 3)
                    lo_of(sw_lo, sw32, WS, sw_hi)
                if h == 2:
                    segment_scales()
                if h % LS == LS - 1 and q + 1 < LN_IT:
                    dve.wait_ge(x_in[q + 1], 16)
                    ln_stats(dve, q + 1, q + 1)
                dve.wait_ge(prep_ahi[s], h // 2 + 1)
                lo_of(att_a_lo[:, h, :], bank[4 + 2 * s][:, 0:256], 1 / WS, att_a_hi[:, h, :])
                lo_of(att_vo_lo[:, h, :], bank[5 + 2 * s][:, :], 1 / WS, att_vo_hi[:, h, :]).then_inc(prep_alo[s], 1)
            end_phase(dve, "dve")

            def context_low(j):
                dve.wait_ge(ctx_h, j + 1)
                half = slice(j % 2 * DC, (j % 2 + 1) * DC)
                dve.tensor_tensor(ctx_lo[:, half, :], ctx32, ctx_hi[:, half, :], ALU.subtract).then_inc(ctx_l, 1)

            context_low(0)
            for j in range(NB):
                blk = slice(j * BLK, (j + 1) * BLK)
                dve.wait_ge(qkv_h, j * 3 + 1)
                lo_of(kv_lo[:, blk], bank[2][:, :], 1 / WS, kv_hi[:, blk]).then_inc(qkv_l, 1)
                if j + 1 < NB:
                    context_low(j + 1)
                dve.wait_ge(qkv_h, j * 3 + 2)
                lo_of(qc0_lo[:, blk], bank[0][:, :], 1 / WS, qc0_hi[:, blk]).then_inc(qkv_l, 1)
                dve.wait_ge(qkv_h, j * 3 + 3)
                lo_of(qc1[64:128, blk], bank[1][64:128, :], 1 / WS, qc1[64:128, blk]).then_inc(qkv_l, 1)
                dve.wait_ge(kr_mm, j + 1)
                for i, (t, tab) in enumerate(((kt1, cos_k), (kt2, sin_k))):
                    dve.tensor_tensor(t.rearrange("p (a b) -> p a b", a=TPB),
                                      bank[3 + i][:, :].rearrange("p (a b) -> p a b", a=TPB),
                                      tab.unsqueeze(1).to_broadcast([P, TPB, S]),
                                      ALU.mult).then_inc(kr_mul, 1)
                dve.wait_ge(kr_mul, ONE + j * 2 + 2)
                dve.tensor_tensor(krot, kt1, kt2, ALU.add).then_inc(kr_sum, 1)
                dve.wait_ge(kr_h, j + 1)
                dve.tensor_tensor(kr_lo[:, blk], krot, kr_hi[:, blk], ALU.subtract)
            end_phase(dve, "dve")

            def rope_dve(j, u):
                dve.wait_ge(rope_h, ONE + j * 4 + u)
                dve.wait_ge(rope_l, ONE + j * 4 + u)
                for a in range(2):
                    dve.wait_ge(q_mm[a], j * 12 + rope_index(u) + 1)
                    src = bank[5 + a][:, :].rearrange("p (h r) -> p h r", r=R)
                    hs = slice(8 * a, 8 * a + 8)
                    dve.tensor_tensor(rt1[:, hs, :], src, cos_q.unsqueeze(1).to_broadcast([P, 8, R]), ALU.mult)
                    for c in range(2):
                        oc = slice(32 * c, 32 * c + 32)
                        ic = slice(32 - 32 * c, 64 - 32 * c)
                        m = dve.tensor_tensor(rt2[:, hs, oc], src[:, :, ic],
                                              sin_q[:, oc].unsqueeze(1).to_broadcast([P, 8, 32]), ALU.mult)
                    m.then_inc(q_free[a], 1)

            def queries_dve(j, h0):
                for h in range(h0, h0 + 4):
                    k = h % 2
                    dve.wait_ge(q_h[k], j * 8 + h // 2 + 1)
                    lo_of(qp_lo[:, h, :], bank[5 + k][:, :], 1 / WS, qp_hi[:, h, :]).then_inc(q_free[k], 1)

            def attend_dve(j, n):
                if n < NG:
                    u, g, k = n // 4, n % 4, n % 2
                    dve.wait_ge(score_mm, ONE + j * NG + n + 1)
                    if g == 0:
                        dve.tensor_copy(escale[:, u % 2, :], seg_scale[:, ds(j * 4 + u, 1)])
                    dve.tensor_reduce(nmax[:, k, :], bank[k][:, :].rearrange("p (a b) -> p a b", a=4),
                                      AX.X, ALU.max, negate=True).then_inc(smax, 1)
                    dve.wait_ge(smax, (j * NG + n) * 2 + 1)
                    dve.tensor_scalar(ebias[:, k, :], nmax[:, k, :], seg_scale[:, ds(j * 4 + u, 1)],
                                      None, ALU.mult).then_inc(smax, 1)
                    if g == 0 and u < 3:
                        rope_dve(j, u + 1)
                    dve.wait_ge(exped[k], ONE + j * 8 + n // 2 + 1)
                    dve.reciprocal(rinv[:, k, :], esum[:, k, :]).then_inc(recip[k], 1)
                if 1 <= n <= NG:
                    q, k = n - 1, (n - 1) % 2
                    dve.wait_ge(pth, j * NG + q + 1)
                    lo_of(pt_lo[:, k, :], bank[2][:, :], PS, pt_hi[:, k, :]).then_inc(ptl, 1)
                if 2 <= n <= NG + 1:
                    q, k = n - 2, (n - 2) % 2
                    dve.wait_ge(oth, j * NG + q + 1)
                    lo_of(ot_lo[:, k, :], bank[3][:, :], OS / PS, ot_hi[:, k, :]).then_inc(otl, 1)
                if n >= 3 and (n - 3) % 4 == 3:
                    q = n - 3
                    u = q // 4
                    xv = x[:, ds(j * 4 + u, 1), :].rearrange("p a b -> p (a b)")
                    dve.wait_ge(y_mm[1], ONE + j * 8 + q // 2 + 1)
                    dve.scalar_tensor_tensor(out=xv, in0=bank[4][:, :], scalar=1 / (OS * WS), in1=xv,
                                             op0=ALU.mult, op1=ALU.add).then_inc(yadd, 1)

            todo = {"rope": rope_dve, "heads": queries_dve, "step": attend_dve}
            change_block(None, 0, todo)
            with dve.Fori(0, NB - 1) as j:
                for n in range(NG):
                    attend_dve(j, n)
                change_block(j, j + 1, todo)
            for n in range(NG):
                attend_dve(NB - 1, n)
            change_block(NB - 1, None, todo)
            end_phase(dve, "dve")
            def split_gate_weights():
                dve.wait_ge(gate_s, 1)
                lo_of(gw_lo, gw32, WS, gw_hi).then_inc(gate_s, 1)

            ln_vector(dve, 1, ln_xn_moe, split_gate_weights)
            def build_gates(u, part):
                u1 = ds(u, 1)
                if part == 0:
                    dve.wait_ge(pk_u, ONE + u * 6)
                    dve.tensor_tensor(eq, iota64.unsqueeze(1).to_broadcast([P, 8, NK]),
                                      iyf[:, u1, :].rearrange("p a b -> p b a").to_broadcast([P, 8, NK]),
                                      ALU.is_equal)
                    dve.tensor_tensor(eqx, iota64[:, 0:KX].unsqueeze(2).to_broadcast([P, KX, 8]),
                                      ixf[:, u1, :].to_broadcast([P, KX, 8]), ALU.is_equal).then_inc(pk_u, 1)
                    dve.wait_ge(pk_u, ONE + u * 6 + 1)
                    dve.tensor_tensor(eq, eq, rank8.unsqueeze(2).to_broadcast([P, 8, NK]), ALU.mult)
                    dve.tensor_tensor(eqx, eqx, cnt[:, u1, :].to_broadcast([P, KX, 8]), ALU.mult).then_inc(pk_u, 1)
                    dve.wait_ge(pk_u, ONE + u * 6 + 2)
                    dve.tensor_reduce(s64[:, 0, :], eq.rearrange("p a b -> p b a"), AX.X, ALU.add)
                    dve.tensor_reduce(cc[:, 0, :], eqx, AX.X, ALU.add).then_inc(pk_u, 1)
                    dve.wait_ge(pk_u, ONE + u * 6 + 3)
                    dve.wait_ge(pk_t, ONE + u)
                    dve.tensor_tensor(G, s64[:, 0:1, :].to_broadcast([P, KX, NK]),
                                      cc[:, 0, :].unsqueeze(2).to_broadcast([P, KX, NK]), ALU.add).then_inc(pk_u, 1)
                    return
                dve.wait_ge(pk_u, ONE + u * 6 + 4)
                dve.scalar_tensor_tensor(out=G, in0=G, scalar=8.0, in1=ry[:, u1, :].to_broadcast([P, KX, NK]),
                                         op0=ALU.is_gt, op1=ALU.mult).then_inc(pk_u, 1)
                dve.wait_ge(pk_u, ONE + u * 6 + 5)
                dve.tensor_tensor(G, G, ex_[:, u1, :].rearrange("p a b -> p b a").to_broadcast([P, KX, NK]),
                                  ALU.mult).then_inc(pk_u, 1)
                dve.wait_ge(pk_u, ONE + u * 6 + 6)
                dve.tensor_tensor(G[:, KX - 1, NK - 1:NK], G[:, KX - 1, NK - 1:NK], den[:, u1],
                                  ALU.add).then_inc(pk_g, 1)

            def keep_gates(u, token0):
                dve.wait_ge(pk_t, ONE + u + 1)
                for a in range(2):
                    m = dve.tensor_scalar(gT[:, a * 4:a * 4 + 4, ds(token0, P, 2)],
                                          bank[4 + a][:, :].rearrange("p (a b) -> p a b", a=4), WS, None, ALU.mult)
                m.then_inc(pk_c, 1)

            def split_memory(b):
                for s in range(2):
                    dst_hi = (memT_hi[:, :, ds(b * P, P)], mem_hi[:, ds(b, 1), :])[s]
                    dst_lo = (memT_lo[:, :, ds(b * P, P)], mem_lo[:, ds(b, 1), :])[s]
                    src = mem32[:, s, :].rearrange("p (a b) -> p a b", a=(DC, 1)[s])
                    dve.wait_ge(mem_load[s], b * 16 + 16)
                    dve.tensor_scalar(dst_hi, src, 1.0, None, ALU.mult).then_inc(mem_h[s], 1)
                    dve.wait_ge(mem_h[s], b + 1)
                    dve.tensor_tensor(dst_lo, src, dst_hi, ALU.subtract).then_inc(mem_l[s], 1)

            def ffn_vector(f, part="rest", after_first_units=None, started=False, following=None):
                def split(f, gs, it, piece):
                    dve.wait_ge(f.whi[gs], f.piece0 + it * f.pieces + piece + 1)
                    cs = slice(piece * 1024, (piece + 1) * 1024)
                    lo_of(f.w_lo[:, gs, cs], f.w32[:, gs, cs], WS, f.w_hi[:, gs, cs]).then_inc(f.wlo[gs], 1)

                if part == "split":
                    for piece in range(f.pieces):
                        split(f, 0, 0, piece)
                    return

                def units(f, j, s, add_first=None):
                    k = f.step0 + j * (2 * NB) + s
                    for c in range(GC):
                        dve.wait_ge(f.silu[c], k + 1)
                        dve.wait_ge(f.hlo[c], k)
                        if f.kind == "moe":
                            dve.scalar_tensor_tensor(out=f.m1[:, c, :], in0=f.sg[:, c, :], scalar=1 / GS,
                                                     in1=bank[2 + c][:, :], op0=ALU.mult,
                                                     op1=ALU.mult).then_inc(f.m1d[c], 1)
                            if c == GC - 1 and add_first is not None:
                                add(j, add_first, 0)
                            dve.wait_ge(f.m1d[c], k + 1)
                            dve.tensor_tensor(f.m2[:, c, :], f.m1[:, c, :], bank[4 + c][:, :],
                                              ALU.mult).then_inc(f.m2d[c], 1)
                        elif f.kind == "mlp":
                            dve.tensor_tensor(f.m2[:, c, :], f.sg[:, c, :], bank[2 + c][:, :],
                                              ALU.mult).then_inc(f.m2d[c], 1)
                        else:
                            g = gT[:, ds((j * 2 + s // NB) * GC + c, 1), (s % NB) * BLK:(s % NB + 1) * BLK]
                            dve.tensor_tensor(f.m2[:, c, :], f.sg[:, c, :], g.rearrange("p a b -> p (a b)"),
                                              ALU.mult).then_inc(f.m2d[c], 1)

                def add(j, s, q):
                    k = f.step0 + j * (2 * NB) + s
                    yb = q % 2
                    xv = x[:, (s % NB) * TPB + q, :]
                    dve.wait_ge(f.ymm[yb], k * 2 + q // 2 + 1)
                    dve.scalar_tensor_tensor(out=xv, in0=bank[6 + yb][:, :], scalar=1 / (WS * WS), in1=xv,
                                             op0=ALU.mult, op1=ALU.add).then_inc(f.yadd[yb], 1)

                def body(j, last, with_memory=False):
                    for s in range(2 * NB):
                        if f.kind == "mlp":
                            build_gates(j * NB + s // 2, s % 2)
                        first = 0
                        if not (last and s == 2 * NB - 1):
                            units(f, j, s + 1, s if f.kind == "moe" else None)
                            first = 1 if f.kind == "moe" else 0
                        for q in range(first, TPB):
                            add(j, s, q)
                        if f.kind == "mlp" and s % 2 == 1:
                            h = s // 2
                            keep_gates(j * NB + h, j * (2 * 256) + h // 2 * 256 + h % 2)
                        gs, t = (s + 1) // NB % 2, (s + 1) % NB
                        it = j + 1 if s + 1 == 2 * NB else j
                        if 1 <= t <= f.pieces and not (last and gs == 1):
                            split(f, 1 - gs, it + gs, t - 1)
                        elif following is not None and last and gs == 1 and 1 <= t <= following.pieces:
                            split(following, 0, 0, t - 1)
                        if following is not None and last and s == 2 * NB - 1:
                            dve.wait_ge(pk_c, ONE + NT)
                            units(following, 0, 0)
                        if with_memory and s % NB == NB - 1:
                            split_memory(j * 2 + s // NB)

                if not started:
                    units(f, 0, 0)
                if after_first_units is not None:
                    after_first_units()
                n = f.groups // 2
                if f.kind == "moe":
                    with dve.Fori(0, B // 2) as j:
                        body(j, False, with_memory=True)
                with dve.Fori(B // 2 if f.kind == "moe" else 0, n - 1) as j:
                    body(j, False)
                body(n - 1, True)

            ffn_vector(moe, part="split")
            dve.memset(gsc, 2.0)
            dve.memset(cwt, 0.0)
            lg = bank[4][:, 0:NT * E].rearrange("p (a b) -> p a b", b=E)
            dve.wait_ge(gate_mm, 1)
            dve.tensor_reduce(gmx, lg, AX.X, ALU.max).then_inc(gate_v, 1)
            dve.wait_ge(gate_v, 1)
            dve.tensor_tensor(gsub, lg, gmx.unsqueeze(2).to_broadcast([P, NT, E]), ALU.subtract).then_inc(gate_v, 1)
            dve.wait_ge(gate_v, 3)
            dve.tensor_reduce(gsum, gexp, AX.X, ALU.add).then_inc(gate_v, 1)
            dve.wait_ge(gate_v, 4)
            dve.reciprocal(grc, gsum).then_inc(gate_v, 1)
            dve.wait_ge(gate_v, 5)
            dve.tensor_tensor(gsc[:, :, 0:E], gexp, grc.unsqueeze(2).to_broadcast([P, NT, E]),
                              ALU.mult).then_inc(gate_v, 1)
            dve.wait_ge(gate_v, 6)
            for t in range(NT):
                m = dve.max(gtop[:, t, :], gsc[:, t, :])
            m.then_inc(gate_v, 1)
            dve.wait_ge(gate_v, 7)
            for t in range(NT):
                m = dve.match_replace(grep_[:, t, :], gtop[:, t, :], gsc[:, t, :], 0.0)
            m.then_inc(gate_v, 1)
            dve.wait_ge(gate_v, 8)
            dve.tensor_tensor(gcw, gsc[:, :, 0:E], grep_[:, :, 0:E], ALU.subtract).then_inc(gate_done, 1)
            for t in range(NB):
                dve.wait_ge(gate_c, 2 * t + 1)
                lo_of(cwt[32:32 + E, t * BLK:(t + 1) * BLK], bank[5][0:E, :], GS,
                      cwt[0:E, t * BLK:(t + 1) * BLK]).then_inc(gate_c, 1)
            ffn_vector(moe)
            end_phase(dve, "dve")
            def memory_masks():
                dve.wait_ge(later_in, 32)
                dve.tensor_copy(mm_f.rearrange("p a b -> p (a b)"), mm8).then_inc(mask_s, 1)
                dve.wait_ge(mask_s, 1)
                dve.tensor_scalar(mm_bias, mm_f, -NEG, NEG, ALU.mult, ALU.add).then_inc(mask_s, 1)
                dve.tensor_reduce(mvalid, mm_f, AX.X, ALU.max).then_inc(mask_s, 1)
                dve.wait_ge(mask_s, 3)
                dve.tensor_scalar(mscale, mvalid, M_SCALE, None, ALU.mult).then_inc(mask_s, 1)
                dve.wait_ge(mask_s, 4)

            def memory_max(g):
                dve.wait_ge(mem_scored, g + 1)
                dve.tensor_reduce(mmax, bank[4][:, :].rearrange("p (a b) -> p a b", a=LS), AX.X, ALU.max,
                                  negate=True).then_inc(mem_max, 1)
                dve.wait_ge(mem_max, 2 * g + 1)
                dve.tensor_tensor(mexp_bias, mmax, mscale[:, g * LS:(g + 1) * LS], ALU.mult).then_inc(mem_max, 1)

            def memory_sums(g):
                dve.wait_ge(mem_exp, g + 1)
                dve.reciprocal(mrec, msum).then_inc(mem_sums, 1)
                dve.wait_ge(mem_sums, 2 * g + 1)
                dve.tensor_tensor(mfac, mrec, mvalid[:, g * LS:(g + 1) * LS], ALU.mult).then_inc(mem_sums, 1)

            def memory_low(g):
                dve.wait_ge(mem_pt_hi, g + 1)
                dve.tensor_tensor(mpt_lo.rearrange("p a b -> p (a b)"), bank[5][:, :],
                                  mpt_hi.rearrange("p a b -> p (a b)"), ALU.subtract).then_inc(mem_pt_lo, 1)
                dve.wait_ge(mem_sums, 2 * g + 2)

            def memory_add(g):
                for i in range(LS):
                    b, k = g * LS + i, i % 2
                    dve.wait_ge(mem_read[k], b // 2 + 1)
                    dve.scalar_tensor_tensor(out=x[:, b, :], in0=bank[6 + k][:, :], scalar=mfac[:, i:i + 1],
                                             in1=x[:, b, :], op0=ALU.mult, op1=ALU.add).then_inc(mem_added[k], 1)

            def queries_low(t):
                dve.wait_ge(pk_qh, t + 1)
                ts_ = slice(t * BLK, (t + 1) * BLK)
                lo_of(qT_lo[:, ts_], bank[4 + t][:, :], 1 / WS, qT_hi[:, ts_]).then_inc(pk_ql, 1)

            ln_stats(dve, LN_AT[2, 0], 0)
            ln_normalize(dve, LN_AT[2, 0], 0, ln_xn_mem)
            memory_masks()
            ln_stats(dve, LN_AT[2, 1], 1)
            ln_low(dve, LN_AT[2, 0], 0)
            for g in range(LN_IT):
                if g + 1 < LN_IT:
                    ln_normalize(dve, LN_AT[2, g + 1], g + 1, ln_xn_mem)
                memory_max(g)
                if g + 1 < LN_IT:
                    ln_low(dve, LN_AT[2, g + 1], g + 1)
                memory_sums(g)
                if g == 0:
                    dve.wait_ge(pk_s, 1)
                    lo_of(kw_lo, kw32, WS, kw_hi).then_inc(pk_s, 1)
                else:
                    ln_stats(dve, LN_AT[3, g - 1], g - 1)
                memory_low(g)
                if g > 0:
                    ln_normalize(dve, LN_AT[3, g - 1], g - 1, ln_xn_mem)
                memory_add(g)
                if g + 2 < LN_IT:
                    ln_stats(dve, LN_AT[2, g + 2], g + 2)
                if g > 0:
                    ln_low(dve, LN_AT[3, g - 1], g - 1)
                for k in range(2):
                    dve.wait_ge(mem_added[k], 2 * g + 2)
            ln_stats(dve, LN_AT[3, 3], 3)
            ln_normalize(dve, LN_AT[3, 3], 3, ln_xn_mem)
            queries_low(0)
            queries_low(1)
            ln_low(dve, LN_AT[3, 3], 3)
            queries_low(2)
            queries_low(3)
            ffn_vector(mlp, part="split")
            for i, (r, best, at) in enumerate(((rx, sx, ixu), (ry, sy, iyu))):
                dve.wait_ge(pk_r, 2 * i + 2)
                for u in range(NT):
                    m = dve.max(best[:, u, :], r[:, u, :])
                m.then_inc(pk_v, 1)
                dve.wait_ge(pk_v, 3 * i + 1)
                for u in range(NT):
                    m = dve.max_index(at[:, u, :], best[:, u, :], r[:, u, :])
                m.then_inc(pk_v, 1)
                dve.wait_ge(pk_v, 3 * i + 2)
                dve.tensor_tensor(r, r, best[:, :, 0:1].to_broadcast([P, NT, NK]), ALU.subtract).then_inc(pk_v, 1)
            for u in range(NT):
                m = dve.tensor_tensor(al[:, u, :].rearrange("p (a b) -> p a b", a=8),
                                      sx[:, u, :].unsqueeze(2).to_broadcast([P, 8, 8]),
                                      sy[:, u, :].unsqueeze(1).to_broadcast([P, 8, 8]), ALU.add)
            m.then_inc(pk_v, 1)
            step = [0]

            def after(m):
                step[0] += 1
                m.then_inc(pk_g0, 1)
                dve.wait_ge(pk_g0, step[0])

            dve.wait_ge(pk_v, 7)
            dve.wait_ge(pk_in, 48)
            dve.tensor_copy(ixf, ixu)
            for u in range(NT):
                m = dve.max(top[:, u, :], al[:, u, :])
            after(dve.tensor_copy(iyf, iyu))
            for u in range(NT):
                m = dve.match_replace(al_rep[:, u, :], top[:, u, :], al[:, u, :], -3e38)
            after(m)
            after(dve.tensor_tensor(al_rep, al_rep, al, ALU.not_equal))
            dve.tensor_tensor(al, al, top[:, :, 0:1].to_broadcast([P, NT, 64]), ALU.subtract).then_inc(pk_v, 1)
            dve.wait_ge(pk_act, 3)
            def finish_routing():
                after(dve.tensor_tensor(al, al, al_rep, ALU.mult))
                dve.tensor_reduce(den, al, AX.X, ALU.add)
                dve.tensor_reduce(wsum.rearrange("p a b -> p (a b)"), al.rearrange("p u (a b) -> p (u a) b", b=8),
                                  AX.X, ALU.add)
                after(dve.tensor_reduce(cnt.rearrange("p a b -> p (a b)"),
                                        al_rep.rearrange("p u (a b) -> p (u a) b", b=8), AX.X, ALU.add))
                dve.tensor_scalar(wtmp, ixf, float(KX), None, ALU.is_ge)
                after(dve.reciprocal(far, den))
                dve.tensor_tensor(ex_, rx[:, :, 0:KX], far.unsqueeze(2).to_broadcast([P, NT, KX]), ALU.mult)
                after(dve.tensor_tensor(wtmp, wtmp, wsum, ALU.mult))
                after(dve.tensor_reduce(den, wtmp, AX.X, ALU.add))
                after(dve.tensor_tensor(den, den, far, ALU.mult))

            ffn_vector(mlp, after_first_units=finish_routing, following=pkm)
            ffn_vector(pkm, started=True)
            end_phase(dve, "dve")

        @block.gpsimd
        def _(pool):
            pool.memset(neg_half[:, :, :], -0.5).then_inc(half_set, 1)
            pool.wait_ge(half_set, 1)
            ln_gpsimd_group(pool, 0)
            pool.wait_ge(seg_step, 4)
            pool.tensor_tensor(dist, iota.unsqueeze(1).to_broadcast([P, B, S]),
                               segf.unsqueeze(2).to_broadcast([P, B, S]), ALU.subtract).then_inc(seg_step, 1)
            ln_gpsimd_group(pool, 1)
            pool.wait_ge(seg_step, 5)
            pool.tensor_scalar(ahead, dist, 0.0, NEG, ALU.is_gt, ALU.mult).then_inc(seg_step, 1)
            pool.wait_ge(seg_step, 6)
            pool.tensor_scalar(dist, dist, float(-LOOKBACK), NEG, ALU.is_lt, ALU.mult).then_inc(seg_step, 1)
            ln_gpsimd_group(pool, 2)
            pool.wait_ge(seg_step, 7)
            pool.tensor_tensor(seg_bias, ahead, dist, ALU.add)
            ln_gpsimd_group(pool, 3)
            end_phase(pool, "pool")
            end_phase(pool, "pool")

            def rope_sum_pool(j, u):
                for a in range(2):
                    pool.wait_ge(q_free[a], ONE + j * 12 + rope_index(u) + 1)
                pool.tensor_tensor(rot, rt1, rt2, ALU.add).then_inc(rope_sum, 1)

            def rope_low_pool(j, u):
                pool.wait_ge(rope_sum, j * 4 + u + 1)
                pool.wait_ge(rope_h, ONE + j * 4 + u + 1)
                pool.tensor_tensor(rhl[:, :, 1, :], rot, rhl[:, :, 0, :], ALU.subtract).then_inc(rope_l, 1)

            def attend_pool(j):
                for n in range(NG):
                    u, g, k = n // 4, n % 4, n % 2
                    pool.wait_ge(recip[k], j * 8 + n // 2 + 1)
                    pool.tensor_tensor(prob[:, k, :, :], prob[:, k, :, :],
                                       rinv[:, k, :].unsqueeze(2).to_broadcast([P, 4, P]),
                                       ALU.mult).then_inc(normed[k], 1)
                    if g == 1 and u < 3:
                        rope_sum_pool(j, u + 1)
                    if g == 2 and u < 3:
                        rope_low_pool(j, u + 1)

            rope_sum_pool(0, 0)
            rope_low_pool(0, 0)
            with pool.Fori(0, NB - 1) as j:
                attend_pool(j)
                rope_sum_pool(j + 1, 0)
                rope_low_pool(j + 1, 0)
            attend_pool(NB - 1)
            end_phase(pool, "pool")
            ln_gpsimd(pool, 1)

            def ffn_gpsimd(f):
                def body(j, last):
                    for s in range(2 * NB):
                        k = f.step0 + j * (2 * NB) + s
                        for c in range(GC):
                            pool.wait_ge(f.hhi[c], k + 1)
                            pool.tensor_tensor(f.h_lo[:, s % 2, c, :], f.m2[:, c, :], f.h_hi[:, s % 2, c, :],
                                               ALU.subtract).then_inc(f.hlo[c], 1)

                n = f.groups // 2
                if n > 1:
                    with pool.Fori(0, n - 1) as j:
                        body(j, False)
                body(n - 1, True)

            ffn_gpsimd(moe)
            end_phase(pool, "pool")
            ln_gpsimd(pool, 2)
            ln_gpsimd(pool, 3)
            ffn_gpsimd(mlp)
            ffn_gpsimd(pkm)
            end_phase(pool, "pool")


def shape_constants():
    half = R // 2
    inv = (1.0 / 10000.0 ** (np.arange(half, dtype=np.float32) / np.float32(half))).astype(np.float32)
    ang = np.arange(S, dtype=np.float32)[:, None] * inv
    cos, sin = np.cos(ang).astype(np.float32), np.sin(ang).astype(np.float32)
    cos2, sin2 = np.concatenate([cos, cos], 1) / WS, np.concatenate([-sin, sin], 1) / WS
    sel = np.zeros((P, E * MOE_D), np.float16)
    for e in range(E):
        sel[e, e * MOE_D:(e + 1) * MOE_D] = 1.0
        sel[32 + e, e * MOE_D:(e + 1) * MOE_D] = 1.0
    return {
        "ident": np.eye(P, dtype=np.float32),
        "iota": np.tile(np.arange(S, dtype=np.float32), (P, 1)),
        "rank8": np.tile(8.0 - np.arange(8, dtype=np.float32), (P, 1)),
        "cos_q": cos2.astype(np.float32), "sin_q": sin2.astype(np.float32),
        "cos_k": np.tile(cos2.T, (2, 1)).astype(np.float32), "sin_k": np.tile(sin2.T, (2, 1)).astype(np.float32),
        "moe_sel": np.ascontiguousarray(sel.reshape(P, -1, GW).transpose(1, 0, 2)),
    }


def by_group(gate_t, up_t, down):
    def wide(w):
        return w.reshape(DC, P, -1, GW).transpose(2, 1, 0, 3).reshape(-1, P, DC * GW)
    parts = [wide(gate_t)] + ([wide(up_t)] if up_t is not None else [])
    parts.append(down.reshape(-1, GC, P, D).transpose(0, 2, 1, 3).reshape(-1, P, GC * D))
    return np.concatenate(parts, axis=2)


def lay_out(i):
    i = {k: np.asarray(v) for k, v in i.items()}
    a = dict(shape_constants())
    a["x"] = i["x"].transpose(1, 0, 2)
    a["ctx"] = i["ctx_2048"].transpose(1, 0, 2)
    a["ctxT"] = i["ctx_2048"].reshape(T, DC, P).transpose(2, 1, 0)
    a["seg"] = i["itok_BxS_0_1023"].T
    a["mem_mask"] = i["mask_BxS2_bk0"].reshape(T)
    dq = i["L0_xattn_W_dq"].reshape(DC, P, QC).transpose(1, 0, 2)
    dq = np.concatenate([dq, dq[:, :, P:]], axis=2).reshape(P, -1)
    kvc = i["L0_xattn_W_kvc"].reshape(DC, P, KVC).transpose(1, 0, 2).reshape(P, -1)
    kr = i["L0_xattn_W_kr"]
    sw = np.concatenate([kr[:, R // 2:], kr[:, :R // 2]], axis=1)
    qr = i["L0_xattn_W_qr"]
    a["small_w"] = np.concatenate([dq, kvc, kr, kr, sw, sw, qr[:P], np.concatenate([qr[P:], qr[P:]], axis=0)],
                                  axis=1)
    uq = i["L0_xattn_W_uq"].reshape(QC, H, HD).transpose(1, 2, 0)
    uk = i["L0_xattn_W_uk"].reshape(KVC, H, HD).transpose(1, 2, 0)
    uv = i["L0_xattn_W_uv"].reshape(KVC, H, HD).transpose(1, 2, 0)
    wo = i["L0_xattn_W_o"].reshape(H, HD, D)
    a["head_w"] = np.concatenate([uq, uq[:, :, P:], uk, uv, wo], axis=2)
    a["moe_gate"] = i["L0_ffn_gate_w"].reshape(E, DC, P).transpose(2, 1, 0).reshape(P, DC * E)
    a["moe_w"] = by_group(i["L0_ffn_w_gate"].reshape(-1, D).T, i["L0_ffn_w_up"].reshape(-1, D).T,
                          i["L0_ffn_w_down"].transpose(0, 2, 1).reshape(-1, D))
    a["mlp_w"] = by_group(i["L1_ffn_gate_w"], i["L1_ffn_up_w"], i["L1_ffn_down_w"])
    a["pk_e"] = by_group(i["L1_ffn_down_embed"].T, None, i["L1_ffn_up_embed"])
    wq = i["L1_ffn_W_q"].reshape(DC, P, P).transpose(1, 0, 2).reshape(P, -1)
    keys = np.zeros((P, 2, 2, NK), np.float32)
    for t in range(2):
        for h in range(2):
            keys[h * NK:(h + 1) * NK, t, h] = i["L1_ffn_keys"][t]
    a["pk_w"] = np.concatenate([wq, keys.reshape(P, -1)], axis=1)
    return {k: np.ascontiguousarray(v) for k, v in a.items()}


def kernel(**inputs):
    import concourse.bacc as bacc
    from concourse.bass_utils import run_bass_kernel_spmd

    nc = bacc.Bacc("TRN2", target_bir_lowering=False, num_devices=1)
    arrays, aps = {}, {}
    for name, a in lay_out(inputs).items():
        arrays[f"in_{name}"] = a
        aps[name] = nc.dram_tensor(f"in_{name}", a.shape, mybir.dt.from_np(a.dtype), kind="ExternalInput").ap()
    out = nc.dram_tensor("out", (P, NT, D), F32, kind="ExternalOutput").ap()
    build(nc, aps, out)
    r = run_bass_kernel_spmd(nc, [arrays], core_ids=[0])
    return r.results[0]["out"].transpose(1, 0, 2).reshape(B, S, D)
```
